# Optimizing a Trainium2 kernel written in Bass

```python
import numpy as np
import jax
import jax.numpy as jnp

def _softmax(x, axis=-1):
    return jax.nn.softmax(x, axis=axis)

def _gelu(x):
    return jax.nn.gelu(x, approximate=True)

def _silu(x):
    return jax.nn.silu(x)

def _sigmoid(x):
    return jax.nn.sigmoid(x)

def _layernorm(x, axis=-1, eps=1e-05):
    m = jnp.mean(x, axis=axis, keepdims=True)
    v = jnp.var(x, axis=axis, keepdims=True)
    return (x - m) / jnp.sqrt(v + eps)

def _scatter_add(tgt, idx, src, axis=0):
    return tgt.at[idx].add(src)

def _segment_sum(src, seg, n):
    return jax.ops.segment_sum(src, seg, n)
kernel_name = 'mk_audio_tower_d2_tok_audfeat512_r4_1dc763'

def setup_inputs(seed: int=0):
    np.random.seed(seed)
    _w = jnp.asarray

    def _rec_inputs():
        import jax
        import jax.numpy as jnp
        _rk = jax.random.key(seed)
        x = -0.0003702 + 0.999946 * jax.random.normal(jax.random.fold_in(_rk, 1), (64, 256, 64), jnp.float32)
        return x
    x = _rec_inputs()

    def _L0_tok_setup():
        import jax, jax.numpy as jnp
        import numpy as np
        CONTEXT_LEN = 3
        SUBSAMPLING = 3
        key = jax.random.key(seed)
        k1, k2, k3 = jax.random.split(key, 3)
        B, T, D = (32, 500, 64)
        OUT = 128
        x = jax.random.normal(k1, (B, T, D), dtype=jnp.float32)
        weight = jax.random.normal(k2, (OUT, D * CONTEXT_LEN), dtype=jnp.float32)
        weight = weight * (1.0 / np.sqrt(D * CONTEXT_LEN * OUT).astype(np.float32))
        bias = jax.random.normal(k3, (1, OUT), dtype=jnp.float32)
        return {'x': x, 'weight': weight, 'bias': bias}
    _L0_tok_all = _L0_tok_setup()
    _L0_tok_in = {k: v for k, v in _L0_tok_all.items() if k in ('weight', 'bias')}
    del _L0_tok_all

    def _L0_attn_setup():
        import jax, jax.numpy as jnp
        import numpy as np
        import math
        D_MODEL = 128
        key = jax.random.key(seed)
        k1, k2, k3 = jax.random.split(key, 3)
        X = jax.random.normal(k1, (4, 2048, D_MODEL), dtype=jnp.float32)
        s = 1.0 / math.sqrt(D_MODEL)
        W_v = jax.random.uniform(k2, (D_MODEL, D_MODEL), dtype=jnp.float32, minval=-s, maxval=s)
        W_theta = jax.random.uniform(k3, (D_MODEL, D_MODEL), dtype=jnp.float32, minval=-s, maxval=s)
        return {'X': X, 'W_v': W_v, 'W_theta': W_theta}
    _L0_attn_all = _L0_attn_setup()
    _L0_attn_in = {k: v for k, v in _L0_attn_all.items() if k in ('W_v', 'W_theta')}
    del _L0_attn_all

    def _L0_ffn_setup():
        import jax, jax.numpy as jnp
        import numpy as np
        import math
        D_MODEL = 128
        N_EXPERTS = 128
        TOP_K = 8
        N_HEADS = 8
        D_KEYS = 128
        HALF = D_KEYS // 2
        N_BATCH, T_SEQ = (2, 512)
        key = jax.random.key(seed)
        k1, k2, k3, k4, k5, k6 = jax.random.split(key, 6)
        queries = jax.random.normal(k1, (N_BATCH, T_SEQ, D_MODEL), dtype=jnp.float32)
        bound_q = 1.0 / math.sqrt(D_MODEL)
        Wq = jax.random.uniform(k2, (N_HEADS * D_KEYS, D_MODEL), minval=-bound_q, maxval=bound_q, dtype=jnp.float32)
        bq = jax.random.uniform(k3, (N_HEADS * D_KEYS,), minval=-bound_q, maxval=bound_q, dtype=jnp.float32)
        bound_k = 1.0 / math.sqrt(HALF)
        keys = jax.random.uniform(k4, (N_HEADS, 2, N_EXPERTS, HALF), minval=-bound_k, maxval=bound_k, dtype=jnp.float32)
        std = D_MODEL ** (-0.5)
        w_down_embed = std * jax.random.normal(k5, (N_EXPERTS * N_EXPERTS, D_MODEL), dtype=jnp.float32)
        w_up_embed = std * jax.random.normal(k6, (N_EXPERTS * N_EXPERTS, D_MODEL), dtype=jnp.float32)
        return {'queries': queries, 'Wq': Wq, 'bq': bq, 'keys': keys, 'w_down_embed': w_down_embed, 'w_up_embed': w_up_embed}
    _L0_ffn_all = _L0_ffn_setup()
    _L0_ffn_in = {k: v for k, v in _L0_ffn_all.items() if k in ('Wq', 'bq', 'keys', 'w_down_embed', 'w_up_embed')}
    del _L0_ffn_all

    def _L1_attn_setup():
        import jax, jax.numpy as jnp
        import numpy as np
        EPS = 0.001
        HEADS = 8
        DIM_HEAD = 64

        def _causal_linear_attn_bucket1(q, k, v):
            d = q.shape[-1]
            q = jax.nn.softmax(q, axis=-1) * d ** (-0.5)
            k = jnp.exp(k)
            k_cumsum = jnp.cumsum(k, axis=2)
            context = jnp.cumsum(k[..., :, None] * v[..., None, :], axis=2)
            D_inv = 1.0 / jnp.clip(jnp.einsum('bhnd,bhnd->bhn', k_cumsum, q), EPS, None)
            attn = jnp.einsum('bhnd,bhnde,bhn->bhne', q, context, D_inv)
            return attn
        key = jax.random.key(seed)
        ks = jax.random.split(key, 6)
        b, t, qd = (2, 512, 128)
        inner = HEADS * DIM_HEAD
        x = jax.random.normal(ks[0], (b, t, qd), dtype=jnp.float32)
        scale = 0.02
        Wq = scale * jax.random.normal(ks[1], (qd, inner), dtype=jnp.float32)
        Wk = scale * jax.random.normal(ks[2], (qd, inner), dtype=jnp.float32)
        Wv = scale * jax.random.normal(ks[3], (qd, inner), dtype=jnp.float32)
        Wo = scale * jax.random.normal(ks[4], (inner, qd), dtype=jnp.float32)
        bo = jnp.zeros((qd,), dtype=jnp.float32)
        return {'x': x, 'Wq': Wq, 'Wk': Wk, 'Wv': Wv, 'Wo': Wo, 'bo': bo}
    _L1_attn_all = _L1_attn_setup()
    _L1_attn_in = {k: v for k, v in _L1_attn_all.items() if k in ('Wq', 'Wk', 'Wv', 'Wo', 'bo')}
    del _L1_attn_all

    def _L1_ffn_setup():
        import jax, jax.numpy as jnp
        import numpy as np
        B, S, D = (32, 128, 128)
        E, H, O, K = (8, 512, 128, 2)
        key = jax.random.key(seed)
        ks = jax.random.split(key, 5)
        sc = lambda k, shape, scale: jax.random.normal(k, shape, jnp.float32) * scale
        return {'x': sc(ks[0], (B, S, D), 1.0), 'attn_w': sc(ks[1], (D, 1), 0.05), 'attn_b': jnp.zeros((1,), jnp.float32), 'gate_w': sc(ks[2], (D, E), 0.05), 'gate_b': jnp.zeros((E,), jnp.float32), 'w1': sc(ks[3], (E, D, H), 0.02), 'b1': jnp.zeros((E, H), jnp.float32), 'w2': sc(ks[4], (E, H, O), 0.02), 'b2': jnp.zeros((E, O), jnp.float32)}
    _L1_ffn_all = _L1_ffn_setup()
    _L1_ffn_in = {k: v for k, v in _L1_ffn_all.items() if k in ('attn_w', 'attn_b', 'gate_w', 'gate_b', 'w1', 'b1', 'w2', 'b2')}
    del _L1_ffn_all
    return {'x': x, 'L0_tok_weight': _L0_tok_in['weight'], 'L0_tok_bias': _L0_tok_in['bias'], 'L0_attn_W_v': _L0_attn_in['W_v'], 'L0_attn_W_theta': _L0_attn_in['W_theta'], 'L0_ffn_Wq': _L0_ffn_in['Wq'], 'L0_ffn_bq': _L0_ffn_in['bq'], 'L0_ffn_keys': _L0_ffn_in['keys'], 'L0_ffn_w_down_embed': _L0_ffn_in['w_down_embed'], 'L0_ffn_w_up_embed': _L0_ffn_in['w_up_embed'], 'L1_attn_Wq': _L1_attn_in['Wq'], 'L1_attn_Wk': _L1_attn_in['Wk'], 'L1_attn_Wv': _L1_attn_in['Wv'], 'L1_attn_Wo': _L1_attn_in['Wo'], 'L1_attn_bo': _L1_attn_in['bo'], 'L1_ffn_attn_w': _L1_ffn_in['attn_w'], 'L1_ffn_attn_b': _L1_ffn_in['attn_b'], 'L1_ffn_gate_w': _L1_ffn_in['gate_w'], 'L1_ffn_gate_b': _L1_ffn_in['gate_b'], 'L1_ffn_w1': _L1_ffn_in['w1'], 'L1_ffn_b1': _L1_ffn_in['b1'], 'L1_ffn_w2': _L1_ffn_in['w2'], 'L1_ffn_b2': _L1_ffn_in['b2']}

def reference(x, L0_tok_weight, L0_tok_bias, L0_attn_W_v, L0_attn_W_theta, L0_ffn_Wq, L0_ffn_bq, L0_ffn_keys, L0_ffn_w_down_embed, L0_ffn_w_up_embed, L1_attn_Wq, L1_attn_Wk, L1_attn_Wv, L1_attn_Wo, L1_attn_bo, L1_ffn_attn_w, L1_ffn_attn_b, L1_ffn_gate_w, L1_ffn_gate_b, L1_ffn_w1, L1_ffn_b1, L1_ffn_w2, L1_ffn_b2):
    import jax
    import jax.numpy as jnp

    def _L0_tok_ref(x, weight, bias):
        import jax, jax.numpy as jnp
        import numpy as np
        CONTEXT_LEN = 3
        SUBSAMPLING = 3
        B, T, D = x.shape
        l = CONTEXT_LEN
        N = T - l + 1
        spliced = jnp.concatenate([x[:, i:i + N, :] for i in range(l)], axis=-1)
        spliced = spliced[:, ::SUBSAMPLING, :]
        return jnp.einsum('bnk,ok->bno', spliced, weight) + bias[0]

    def _L0_attn_ref(X, W_v, W_theta):
        import jax, jax.numpy as jnp
        import numpy as np
        import math
        D_MODEL = 128
        n = X.shape[1]
        d = X.shape[2]
        XW_v = X @ W_v.T
        theta_X = X @ W_theta.T
        first_term = jnp.mean(XW_v, axis=1, keepdims=True)
        kv = jnp.einsum('bnd,bne->bde', theta_X, XW_v)
        second_term = X @ kv / (n * math.sqrt(d))
        return first_term + second_term

    def _L0_ffn_ref(queries, Wq, bq, keys, w_down_embed, w_up_embed):
        import jax, jax.numpy as jnp
        import numpy as np
        import math
        D_MODEL = 128
        N_EXPERTS = 128
        TOP_K = 8
        N_HEADS = 8
        D_KEYS = 128
        HALF = D_KEYS // 2
        N_BATCH, T_SEQ = (2, 512)
        N, T, D = queries.shape
        H, E, K = (N_HEADS, N_EXPERTS, TOP_K)
        q_tok = queries.reshape(-1, D)
        qh = q_tok @ Wq.T + bq
        qh = qh.reshape(-1, H, 2, HALF)
        sub_scores = jnp.einsum('nhcf,hcef->nhce', qh, keys)
        s, idx = jax.lax.top_k(sub_scores, K)
        all_scores = (s[:, :, 0, :, None] + s[:, :, 1, None, :]).reshape(-1, H, K * K)
        all_idx = (idx[:, :, 0, :, None] * E + idx[:, :, 1, None, :]).reshape(-1, H, K * K)
        best_s, best_pos = jax.lax.top_k(all_scores, K)
        indices = jnp.take_along_axis(all_idx, best_pos, axis=-1)
        w_down = w_down_embed[indices]
        w_up = w_up_embed[indices]
        x = jnp.einsum('nd,nhkd->nhk', q_tok, w_down)
        x = jax.nn.gelu(x)
        vals = x * jax.nn.softmax(best_s, axis=-1)
        out = jnp.einsum('nhk,nhkd->nd', vals, w_up)
        return out.reshape(N, T, D)

    def _L1_attn_ref(x, Wq, Wk, Wv, Wo, bo):
        import jax, jax.numpy as jnp
        import numpy as np
        EPS = 0.001
        HEADS = 8
        DIM_HEAD = 64

        def _causal_linear_attn_bucket1(q, k, v):
            d = q.shape[-1]
            q = jax.nn.softmax(q, axis=-1) * d ** (-0.5)
            k = jnp.exp(k)
            k_cumsum = jnp.cumsum(k, axis=2)
            context = jnp.cumsum(k[..., :, None] * v[..., None, :], axis=2)
            D_inv = 1.0 / jnp.clip(jnp.einsum('bhnd,bhnd->bhn', k_cumsum, q), EPS, None)
            attn = jnp.einsum('bhnd,bhnde,bhn->bhne', q, context, D_inv)
            return attn
        b, t, _ = x.shape
        q = x @ Wq
        k = x @ Wk
        v = x @ Wv
        split = lambda z: z.reshape(b, t, HEADS, DIM_HEAD).transpose(0, 2, 1, 3)
        q, k, v = (split(q), split(k), split(v))
        attn = _causal_linear_attn_bucket1(q, k, v)
        attn = attn.transpose(0, 2, 1, 3).reshape(b, t, HEADS * DIM_HEAD)
        return attn @ Wo + bo

    def _L1_ffn_ref(x, attn_w, attn_b, gate_w, gate_b, w1, b1, w2, b2):
        import jax, jax.numpy as jnp
        import numpy as np
        B, S, D = (32, 128, 128)
        E, H, O, K = (8, 512, 128, 2)
        scores = x @ attn_w + attn_b
        aw = jax.nn.softmax(scores, axis=1)
        pooled = jnp.sum(x * aw, axis=1)
        gates = jax.nn.softmax(pooled @ gate_w + gate_b, axis=-1)
        _, idx = jax.lax.top_k(gates, K)
        mask = jnp.sum(jax.nn.one_hot(idx, E, dtype=gates.dtype), axis=-2)
        g = gates * mask
        g = g / (jnp.sum(g, axis=-1, keepdims=True) + 1e-09)
        h = jax.nn.gelu(jnp.einsum('bsd,edh->ebsh', x, w1) + b1[:, None, None, :], approximate=False)
        eo = jax.nn.gelu(jnp.einsum('ebsh,eho->ebso', h, w2) + b2[:, None, None, :], approximate=False)
        return jnp.einsum('ebso,be->bso', eo, g)
    h = _L0_tok_ref(x, L0_tok_weight, L0_tok_bias)
    h = h + _L0_attn_ref(_layernorm(h, axis=-1), L0_attn_W_v, L0_attn_W_theta)
    h = h + _L0_ffn_ref(_layernorm(h, axis=-1), L0_ffn_Wq, L0_ffn_bq, L0_ffn_keys, L0_ffn_w_down_embed, L0_ffn_w_up_embed)
    h = h + _L1_attn_ref(_layernorm(h, axis=-1), L1_attn_Wq, L1_attn_Wk, L1_attn_Wv, L1_attn_Wo, L1_attn_bo)
    h = h + _L1_ffn_ref(_layernorm(h, axis=-1), L1_ffn_attn_w, L1_ffn_attn_b, L1_ffn_gate_w, L1_ffn_gate_b, L1_ffn_w1, L1_ffn_b1, L1_ffn_w2, L1_ffn_b2)
    return h

_drawn_inputs = setup_inputs


def setup_inputs(seed=0):
    import zlib

    import numpy as np

    out = dict(_drawn_inputs(seed))
    spreads = {'L1_attn_bo': (0.0, 0.1),
     'L1_ffn_gate_b': (0.0, 0.8),
     'L1_ffn_b1': (0.0, 0.8),
     'L1_ffn_b2': (0.0, 0.278)}
    factors = {'L0_ffn_bq': 3.468,
     'L1_attn_Wq': 8.0,
     'L1_attn_Wk': 8.0,
     'L1_ffn_attn_w': 8.0,
     'L1_ffn_gate_w': 3.295,
     'L1_ffn_w1': 3.634,
     'L1_ffn_w2': 3.327}
    for name, (base, spread) in spreads.items():
        noise = np.random.default_rng([zlib.crc32(name.encode()), seed]).standard_normal(out[name].shape)
        drawn = base * np.exp(spread * noise) if base else spread * noise
        out[name] = jnp.asarray(drawn.astype(out[name].dtype))
    for name, factor in factors.items():
        out[name] = (out[name] * factor).astype(out[name].dtype)
    return out
```

```python
from contextlib import ExitStack

import concourse.bass as bass
from concourse import mybir

F32 = mybir.dt.float32
BF16 = mybir.dt.bfloat16
I32 = mybir.dt.int32
U32 = mybir.dt.uint32
ALU = mybir.AluOpType
ACT = mybir.ActivationFunctionType
AX = mybir.AxisListType

B, FRAMES, FEAT = 64, 256, 64
CTX = 3
N = 85
D = 128
KIN = CTX * FEAT // 2
HEADS, EXP, TOPK = 8, 128, 8
ROW = 2 * D
LH, LD = 8, 64
E, HID = 8, 512
HB = HID // D
LN_EPS = 1e-5
CLIP = 1e-3
DEN_EPS = 1e-9

NB = 3
GROUPS = B // NB
LAST = B - GROUPS * NB
GT = NB * N
UNITS = 4
UR = HEADS * TOPK // UNITS
MAGIC = 0x5F3759DF
NEWTON = 3
ONES_ROWS = 16


def tower(nc, xg, xl, tok_w, tok_b, wv_t, wth_t, pq_w, pq_b, pkeys, table, aq, ak, av, ao, abo,
          pool_w, pool_b, gate_w, gate_b, w1, b1, w2, b2, out, out_last):
    ctx = ExitStack()
    with ctx:
        def sb(name, shape, dt=F32):
            return ctx.enter_context(nc.sbuf_tensor(name, shape, dt))

        def bank(name):
            return ctx.enter_context(nc.psum_tensor(name, [128, 512], F32))

        def sem(name):
            return ctx.enter_context(nc.semaphore(name))

        tok_ws = sb("tok_ws", [KIN, 2, D])
        tok_bs = sb("tok_bs", [1, D])
        wv_s = sb("wv_s", [D, D])
        wth_s = sb("wth_s", [D, D])
        ck = sb("ck", [D, 2 * HEADS * EXP])
        cb3 = sb("cb3", [D, 2 * HEADS * EXP], BF16)
        aq_s = sb("aq_s", [D, LH * LD])
        ak_s = sb("ak_s", [D, LH * LD])
        av_s = sb("av_s", [D, LH * LD])
        ao_s = sb("ao_s", [D, HB, D])
        abo_s = sb("abo_s", [1, D])
        pool_ws = sb("pool_ws", [D, 1])
        pool_bs = sb("pool_bs", [1, 1])
        gate_ws = sb("gate_ws", [D, E])
        gate_bs = sb("gate_bs", [1, E])
        w1_s = sb("w1_s", [D, E, HID])
        w2_s = sb("w2_s", [D, E, HB, D])
        b1_s = sb("b1_s", [D, E, HB])
        b2_s = sb("b2_s", [D, E])
        ident = sb("ident", [128, 128])
        ones = sb("ones", [128, 128])
        ones3 = sb("ones3", [128, 128], BF16)
        mean_col = sb("mean_col", [N, 1])
        causal = sb("causal", [N, N])
        iota8 = sb("iota8", [128, 8])
        own_batch = sb("own_batch", [NB, NB, E])
        x_s = sb("x_s", [KIN, 2, GT])
        h0 = sb("h0", [N, NB, D])
        z0 = sb("z0", [N, NB, D])
        z0t = sb("z0t", [D, NB, N])
        gram = sb("gram", [D, NB, D])
        zmean = sb("zmean", [D, NB])
        gv = sb("gv", [D, NB, D])
        rmean = sb("rmean", [1, NB, D])
        kv = sb("kv", [D, NB, D])
        h1 = sb("h1", [N, NB, D])
        st0 = sb("st0", [N, NB, 6])
        mv0 = sb("mv0", [N, NB, 2])
        nw0 = sb("nw0", [N, 4, NB])
        h1p = sb("h1p", [128, 2, D])
        hres = sb("hres", [128, 2, D])
        q_s = sb("q_s", [128, D])
        qt_s = sb("qt_s", [D, 128])
        st1 = sb("st1", [128, 6])
        mv1 = sb("mv1", [128, 2])
        nw1 = sb("nw1", [128, 4, 1])
        sc = sb("sc", [128, 2 * HEADS, EXP])
        s8 = sb("s8", [128, 2 * HEADS, TOPK])
        i8 = sb("i8", [128, 2 * HEADS, TOPK], U32)
        i8f = sb("i8f", [128, 2 * HEADS, TOPK])
        pair = sb("pair", [128, HEADS, TOPK, TOPK])
        best = sb("best", [128, HEADS, TOPK])
        pos = sb("pos", [128, HEADS, TOPK], U32)
        ab = sb("ab", [128, 2, HEADS * TOPK], U32)
        hit = sb("hit", [128, 2 * HEADS, TOPK, TOPK])
        iab = sb("iab", [128, 2, HEADS * TOPK])
        idx = sb("idx", [128, 2, HEADS * TOPK], U32)
        es = sb("es", [128, HEADS, TOPK])
        den = sb("den", [128, 2, HEADS])
        smh = sb("smh", [128, 2, HEADS * TOPK])
        ring = sb("ring", [128, UNITS, UR, ROW])
        spare = ring[0:1, 2:4, :, :].rearrange("p u k d -> p (u k d)")
        cb = spare[:, 0:2048]
        cbr = spare[:, 2048:4096]
        cbp = spare[:, 4096:6144].bitcast(BF16).rearrange("p (a n) -> p a n", a=2)
        xu = sb("xu", [128, 4, UR])
        th = sb("th", [128, UR])
        vu = sb("vu", [128, UNITS, UR])
        usum = sb("usum", [128, D])
        h2p = sb("h2p", [128, 2, D])
        h2 = sb("h2", [N, NB, D])
        st2 = sb("st2", [N, NB, 6])
        mv2 = sb("mv2", [N, NB, 2])
        nw2 = sb("nw2", [N, 4, NB])
        z2 = sb("z2", [N, NB, D])
        z2t = sb("z2t", [D, GT])
        kt = sb("kt", [D, HB, GT])
        mx = sb("mx", [N, NB, LH])
        qe = sb("qe", [N, NB, LH, LD])
        qsum = sb("qsum", [N, NB, LH])
        vx = sb("vx", [N, NB, LH, LD + 1])
        qt = sb("qt", [D, NB, HB, N])
        sm = sb("sm", [N, 2, LH, N])
        dn = sb("dn", [N, NB, 2, LH])
        at_s = qe
        att = qt
        h3 = sb("h3", [N, NB, D])
        z3 = sb("z3", [N, NB, D])
        z3t = sb("z3t", [D, NB, N])
        pw = sb("pw", [1, NB, N])
        pmx = sb("pmx", [1, 2, NB])
        pz = sb("pz", [D, NB, N])
        pooled = sb("pooled", [D, NB])
        gl = sb("gl", [NB, 6, E])
        g1 = sb("g1", [NB, 4])
        gi = sb("gi", [NB, E], U32)
        gd = sb("gd", [NB, NB, E])
        gb = sb("gb", [D, NB, E])
        ht = sb("ht", [D, 2, HB, GT])
        eo = sb("eo", [D, 2, NB, N])
        acc = sb("acc", [D, NB, N])

        S = [bank("bank_s0"), bank("bank_s1")]
        U = bank("bank_u")
        Q = bank("bank_q")
        G = [bank(f"bank_g{i}") for i in range(4)]
        qrep = Q[:, 0:2 * D].rearrange("p (j d) -> p j d", j=2)
        qtp = S[0][:, 0:128]

        loaded = sem("loaded")
        late_loaded = sem("late_loaded")
        split_moved = sem("split_moved")
        consts = sem("consts")
        pool_order = sem("pool_order")
        setup_ps = sem("setup_ps")
        setup_ck = sem("setup_ck")
        setup_cb = sem("setup_cb")
        setup_dve = sem("setup_dve")
        x_in = sem("x_in")
        a_tok = sem("a_tok")
        a_h0 = sem("a_h0")
        a_dve = sem("a_dve")
        a_z0 = sem("a_z0")
        a_gram_ps = sem("a_gram_ps")
        a_gram = sem("a_gram")
        a_gv_ps = sem("a_gv_ps")
        a_gv = sem("a_gv")
        a_kv_ps = sem("a_kv_ps")
        a_kv = sem("a_kv")
        a_out_ps = sem("a_out_ps")
        a_h1 = sem("a_h1")
        packed = sem("packed")
        t_dve = sem("t_dve")
        t_q = sem("t_q")
        t_qt_ps = sem("t_qt_ps")
        t_qt = sem("t_qt")
        t_qrep = sem("t_qrep")
        t_sc_ps = sem("t_sc_ps")
        t_sc = sem("t_sc")
        t_idx = sem("t_idx")
        t_es = sem("t_es")
        t_ee = sem("t_ee")
        gathered = [sem(f"gathered{u}") for u in range(UNITS)]
        u_dve = sem("u_dve")
        u_arg = sem("u_arg")
        u_th = sem("u_th")
        u_v = sem("u_v")
        u_up = sem("u_up")
        u_sum = sem("u_sum")
        t_red = sem("t_red")
        t_h2 = sem("t_h2")
        unpacked = sem("unpacked")
        l_dve = sem("l_dve")
        l_z2 = sem("l_z2")
        l_z2t_ps = sem("l_z2t_ps")
        l_z2t = sem("l_z2t")
        l_q_ps = sem("l_q_ps")
        l_qs = sem("l_qs")
        l_qe = sem("l_qe")
        l_k_ps = sem("l_k_ps")
        l_k = sem("l_k")
        l_v_ps = sem("l_v_ps")
        l_v = sem("l_v")
        l_qt_ps = sem("l_qt_ps")
        l_qt = sem("l_qt")
        l_s_ps = sem("l_s_ps")
        l_s = sem("l_s")
        l_a_ps = sem("l_a_ps")
        l_a = sem("l_a")
        l_at_ps = sem("l_at_ps")
        l_at = sem("l_at")
        l_o_ps = sem("l_o_ps")
        l_h3 = sem("l_h3")
        l_z3 = sem("l_z3")
        l_z3t_ps = sem("l_z3t_ps")
        l_z3t = sem("l_z3t")
        l_acc0 = sem("l_acc0")
        r_sc_ps = sem("r_sc_ps")
        r_sub = sem("r_sub")
        r_exp = sem("r_exp")
        r_aw = sem("r_aw")
        r_aw_ps = sem("r_aw_ps")
        r_pool = sem("r_pool")
        r_gate_ps = sem("r_gate_ps")
        r_gsub = sem("r_gsub")
        r_gexp = sem("r_gexp")
        r_gd = sem("r_gd")
        r_gb_ps = sem("r_gb_ps")
        r_gb = sem("r_gb")
        m_h_ps = sem("m_h_ps")
        m_h = sem("m_h")
        m_e_ps = sem("m_e_ps")
        m_e = sem("m_e")
        m_acc = sem("m_acc")
        stored = sem("stored")

        carried = sem("carried")
        EARLY = 8 * 16
        LATE = 13 * 16
        NCONST = 9

        def tiles_of(nb):
            return 2 if nb == NB else 1

        class Chain:

            def __init__(self, eng, s, turn, per):
                self.eng, self.s, self.base, self.n, self.per = eng, s, turn * per, 0, per

            def did(self, ins):
                ins.then_inc(self.s, 1)
                self.n += 1

            def wait(self, back=0):
                self.eng.wait_ge(self.s, self.base + (self.n - back))

            def end(self, whole=True):
                assert self.n == self.per or not whole, (self.s, self.n, self.per)

        block = ctx.enter_context(nc.Block())

        @block.sync
        def _(sp):
            def load_x(g, nb):
                if nb == NB:
                    sp.dma_start(x_s[:].rearrange("p c n -> p (c n)"), xg[bass.ds(g * KIN, KIN), :]).then_inc(x_in, 16)
                else:
                    sp.dma_start(x_s[:, :, 0:nb * N], xl.rearrange("p (c n) -> p c n", c=2)).then_inc(x_in, 16)

            def pack(g, nb):
                sp.wait_ge(a_h1, g + 1)
                sp.sem_inc(carried)
                sp.wait_ge(t_qrep, g * 2)
                sp.sem_inc(carried)
                pieces = [(0, 0, N, 0, 0)]
                if nb == NB:
                    a = 128 - N
                    pieces += [(1, 0, a, 0, N), (1, a, N - a, 1, 0), (2, 0, N, 1, N - a)]
                for b, r, n, j, p in pieces:
                    sp.dma_start(h1p[p:p + n, j, :], h1[r:r + n, b, :]).then_inc(packed, 16)

            def unpack(g, j, nb):
                sp.wait_ge(t_h2, 2 * g + (j + 1))
                a = 128 - N
                if j == 0:
                    pieces = [(0, 0, N, 0)] + ([(1, 0, a, N)] if nb == NB else [])
                else:
                    pieces = [(1, a, N - a, 0), (2, 0, N, N - a)]
                for b, r, n, p in pieces:
                    sp.dma_start(h2[r:r + n, b, :], h2p[p:p + n, j, :]).then_inc(unpacked, 16)

            def store(g, nb):
                sp.wait_ge(m_acc, g * E + E)
                if nb == NB:
                    sp.dma_start(out[bass.ds(g * D, D), :], acc[:].rearrange("p b n -> p (b n)")).then_inc(stored, 16)
                else:
                    sp.dma_start(out_last, acc[:, 0, :]).then_inc(stored, 16)

            for dst, src in ((tok_ws[:], tok_w), (tok_bs[:], tok_b), (wv_s[:], wv_t), (wth_s[:], wth_t)):
                sp.dma_start(dst, src).then_inc(loaded, 16)
            load_x(0, NB)
            for dst, src in ((ring[:, 0, 0:4, :], pq_w), (ring[:, 0, 4:8, :], pkeys)):
                sp.dma_start(dst.rearrange("p a b -> p (a b)"), src).then_inc(loaded, 16)
            sp.dma_start(ring[:, 1, 0, 0:HEADS], pq_b).then_inc(loaded, 16)
            sp.dma_start(aq_s[:], aq).then_inc(loaded, 16)
            sp.wait_ge(setup_cb, 2)
            sp.dma_start(cb3[1:2, :], cbp[:, 0, :]).then_inc(split_moved, 16)
            sp.dma_start(cb3[2:3, :], cbp[:, 1, :]).then_inc(split_moved, 16)
            pack(0, NB)
            for dst, src in ((ak_s[:], ak), (av_s[:], av), (ao_s[:].rearrange("p a b -> p (a b)"), ao),
                             (abo_s[:], abo), (pool_ws[:], pool_w), (pool_bs[:], pool_b), (gate_ws[:], gate_w),
                             (gate_bs[:], gate_b), (w1_s[:].rearrange("p e h -> p (e h)"), w1),
                             (w2_s[:].rearrange("p e m d -> p (e m d)"), w2),
                             (b1_s[:].rearrange("p e m -> p (e m)"), b1), (b2_s[:], b2)):
                sp.dma_start(dst, src).then_inc(late_loaded, 16)

            def step(s, nxt, cur, prev):
                if nxt:
                    sp.wait_ge(a_tok, s + 1)
                    load_x(s + 1, nxt)
                    pack(s + 1, nxt)
                if cur:
                    if prev:
                        sp.wait_ge(l_h3, s)
                    unpack(s, 0, cur)
                if prev:
                    store(s - 1, prev)
                if cur == NB:
                    unpack(s, 1, cur)

            step(0, NB, NB, 0)
            step(1, NB, NB, NB)
            with sp.Fori(2, GROUPS - 1) as s:
                step(s, NB, NB, NB)
            step(GROUPS - 1, LAST, NB, NB)
            step(GROUPS, 0, LAST, NB)
            step(GROUPS + 1, 0, 0, LAST)
            sp.wait_ge(stored, (GROUPS + 1) * 16)

        @block.gpsimd
        def _(pool):
            pool.memset(ident[:], 0.0).then_inc(pool_order, 1)
            pool.memset(ones[:], 1.0).then_inc(consts, 1)
            pool.memset(mean_col[:], 1.0 / N).then_inc(consts, 1)
            pool.memset(causal[:], 1.0).then_inc(pool_order, 1)
            pool.memset(own_batch[:], 1.0).then_inc(pool_order, 1)
            pool.memset(ones3[:], 0.0).then_inc(pool_order, 1)
            pool.wait_ge(pool_order, 4)
            pool.affine_select(out=ident[:], in_=ident[:], compare_op=ALU.not_equal, fill=1.0, base=0,
                               pattern=[[-1, 128]], channel_multiplier=1).then_inc(consts, 1)
            pool.affine_select(out=causal[:], in_=causal[:], compare_op=ALU.is_ge, fill=0.0, base=0,
                               pattern=[[1, N]], channel_multiplier=-1).then_inc(consts, 1)
            pool.affine_select(out=own_batch[:], in_=own_batch[:], compare_op=ALU.is_equal, fill=0.0, base=0,
                               pattern=[[1, NB], [0, E]], channel_multiplier=-1).then_inc(consts, 1)
            pool.affine_select(out=ones3[:], in_=ones3[:], compare_op=ALU.is_ge, fill=1.0, base=-3,
                               pattern=[[0, 128]], channel_multiplier=1).then_inc(consts, 1)
            pool.iota(iota8[:], pattern=[[1, 8]], base=0, channel_multiplier=0,
                      allow_small_or_imprecise_dtypes=True).then_inc(consts, 1)
            pool.memset(vx[:, :, :, LD:LD + 1], 1.0).then_inc(consts, 1)
            pool.memset(h1p[:], 0.0).then_inc(consts, 1)

            def gather(t, j, rows, first):
                pool.wait_ge(t_idx, t + 1)
                for u in range(UNITS):
                    if not first:
                        pool.wait_ge(u_sum, (t - 1) * UNITS + (u + 1))
                    pool.sem_inc(carried)
                    for k in range(UR):
                        c = u * UR + k
                        pool.indirect_dma_start(
                            ring[0:rows, u, k, :], None, table,
                            bass.IndirectOffsetOnAxis(ap=idx[0:rows, j, c:c + 1], axis=0)).then_inc(gathered[u], 16)

            gather(0, 0, 128, True)
            gather(1, 1, 128, False)
            with pool.Fori(1, GROUPS) as g:
                gather(g * 2, 0, 128, False)
                gather(g * 2 + 1, 1, 128, False)
            gather(2 * GROUPS, 0, N, False)

        @block.tensor
        def _(pe):
            mm = pe.matmul

            def a_stage(g, nb, first):
                pe.wait_ge(x_in, g * 16 + 16)
                if not first and (not isinstance(g, int) or g >= 3):
                    pe.wait_ge(m_acc, (g - 2) * E)
                for b in range(nb):
                    o = G[0][0:N, b * D:b * D + D]
                    mm(o, x_s[:, 0, b * N:b * N + N], tok_ws[:, 0, :], start=True, stop=False)
                    mm(o, x_s[:, 1, b * N:b * N + N], tok_ws[:, 1, :], start=False, stop=False)
                    ins = mm(o, ones[0:1, 0:N], tok_bs[:], start=False, stop=True)
                ins.then_inc(a_tok, 1)
                pe.wait_ge(a_z0, g + 1)
                for b in range(nb):
                    pe.transpose(G[1][:, b * N:b * N + N], z0[:, b, :], ident[0:N, 0:N])
                for b in range(nb):
                    mm(G[2][:, b * D:b * D + D], z0[:, b, :], z0[:, b, :], start=True, stop=True)
                for b in range(nb):
                    ins = mm(G[3][:, b:b + 1], z0[:, b, :], mean_col[:], start=True, stop=True)
                ins.then_inc(a_gram_ps, 1)
                pe.wait_ge(a_gram, g + 1)
                for b in range(nb):
                    mm(G[2][:, b * D:b * D + D], gram[:, b, :], wv_s[:], start=True, stop=True)
                for b in range(nb):
                    ins = mm(G[3][0:1, b * D:b * D + D], zmean[:, b:b + 1], wv_s[:], start=True, stop=True)
                ins.then_inc(a_gv_ps, 1)
                pe.wait_ge(a_gv, g + 1)
                mm(G[1][:, 0:nb * D], wth_s[:], gv[:, 0:nb, :].rearrange("p b d -> p (b d)"), start=True, stop=True).then_inc(a_kv_ps, 1)
                pe.wait_ge(a_kv, g + 1)
                for b in range(nb):
                    o = G[0][0:N, b * D:b * D + D]
                    mm(o, z0t[:, b, :], kv[:, b, :], start=True, stop=False)
                    ins = mm(o, ones[0:1, 0:N], rmean[:, b, :], start=False, stop=True)
                ins.then_inc(a_out_ps, 1)

            def t_stage(t, j, rows):
                pe.wait_ge(t_q, t + 1)
                pe.transpose(qtp[:, 0:rows], q_s[0:rows, :], ident[0:rows, 0:rows]).then_inc(t_qt_ps, 1)
                pe.wait_ge(t_qt, t + 1)
                for c in range(4):
                    if c >= 2:
                        pe.wait_ge(t_sc, t * 4 + (c - 1))
                    cols = slice(c * 512, c * 512 + 512)
                    mm(S[c % 2][0:rows, :], qt_s[:, 0:rows], ck[:, cols], start=True, stop=False)
                    mm(S[c % 2][0:rows, :], ones3[:, 0:rows], cb3[:, cols], start=False, stop=True).then_inc(t_sc_ps, 1)

            def unit(t, u, rows, first):
                pe.wait_ge(u_up, t * UNITS + (u + 1))
                if u == 0 and not first:
                    pe.wait_ge(t_red, t)
                for c in range(UR // 4):
                    ins = mm(U[0:rows, :], ident[0:rows, 0:rows], ring[0:rows, u, 4 * c:4 * c + 4, D:ROW],
                             start=(u == 0 and c == 0), stop=(u == UNITS - 1 and c == UR // 4 - 1))
                ins.then_inc(u_sum, 1)

            def l_proj(g, nb):
                n = nb * N
                pe.wait_ge(l_z2, g + 1)
                for b in range(nb):
                    ins = pe.transpose(G[3][:, b * N:b * N + N], z2[:, b, :], ident[0:N, 0:N])
                ins.then_inc(l_z2t_ps, 1)
                pe.wait_ge(l_z2t, g + 1)
                for b in range(nb):
                    mm(G[b][0:N, :], z2t[:, b * N:b * N + N], aq_s[:], start=True, stop=True).then_inc(l_q_ps, 1)
                for half in range(2):
                    if half:
                        pe.wait_ge(l_k, g * 2 + 1)
                    for m in range(2):
                        w = ak_s[:, (2 * half + m) * D:(2 * half + m + 1) * D]
                        ins = mm(G[3][:, m * n:m * n + n], w, z2t[:, 0:n], start=True, stop=True)
                    ins.then_inc(l_k_ps, 1)
                for b in range(nb):
                    pe.wait_ge(l_qs, g * NB + (b + 1))
                    mm(G[b][0:N, :], z2t[:, b * N:b * N + N], av_s[:], start=True, stop=True).then_inc(l_v_ps, 1)

            def l_attn(g, nb):
                for b in range(nb):
                    bk = G[3] if b == 0 else G[b - 1]
                    if b == 0:
                        pe.wait_ge(l_k, g * 2 + 2)
                    else:
                        pe.wait_ge(l_v, g * NB + b)
                    pe.wait_ge(l_qe, g * NB + (b + 1))
                    for m in range(HB):
                        ins = pe.transpose(bk[:, m * N:m * N + N], qe[:, b, 2 * m:2 * m + 2, :].rearrange("p a d -> p (a d)"),
                                           ident[0:N, 0:N])
                    ins.then_inc(l_qt_ps, 1)

                def keys_queries(b, pair_of):
                    pe.wait_ge(l_qt, g * NB + (b + 1))
                    for hh in range(LH):
                        m, odd = hh // 2, hh % 2
                        r = slice(odd * LD, odd * LD + LD)
                        ins = mm(G[pair_of + odd][0:N, m * N:m * N + N], kt[r, m, b * N:b * N + N], qt[r, b, m, :],
                                 start=True, stop=True)
                    ins.then_inc(l_s_ps, 1)

                def values(b, pair_of):
                    pe.wait_ge(l_s, g * NB + (b + 1))
                    for hh in range(LH):
                        ins = mm(G[pair_of + hh // 4][0:N, (hh % 4) * (LD + 1):(hh % 4 + 1) * (LD + 1)],
                                 sm[:, b % 2, hh, :], vx[:, b, hh, :], start=True, stop=True)
                    ins.then_inc(l_a_ps, 1)

                def turn(b, bk):
                    pe.wait_ge(l_a, g * NB + (b + 1))
                    for m in range(HB):
                        ins = pe.transpose(bk[:, m * N:m * N + N], at_s[:, b, 2 * m:2 * m + 2, :].rearrange("p a d -> p (a d)"),
                                           ident[0:N, 0:N])
                    ins.then_inc(l_at_ps, 1)

                if nb == NB:
                    pe.wait_ge(l_qt, g * NB + 3)
                    keys_queries(0, 0)
                    pe.wait_ge(l_v, g * NB + 3)
                    keys_queries(1, 2)
                    values(0, 0)
                    pe.wait_ge(l_s, g * NB + 2)
                    keys_queries(2, 2)
                    pe.wait_ge(l_a, g * NB + 1)
                    values(1, 0)
                    values(2, 2)
                    pe.wait_ge(l_a, g * NB + 2)
                    turn(0, G[0])
                    turn(1, G[1])
                    turn(2, G[2])
                else:
                    keys_queries(0, 0)
                    values(0, 2)
                    turn(0, G[0])
                for b in range(nb):
                    pe.wait_ge(l_at, g * NB + (b + 1))
                    o = G[3][0:N, b * D:b * D + D]
                    for m in range(HB):
                        mm(o, att[:, b, m, :], ao_s[:, m, :], start=(m == 0), stop=False)
                    ins = mm(o, ones[0:1, 0:N], abo_s[:], start=False, stop=True)
                ins.then_inc(l_o_ps, 1)
                pe.wait_ge(l_z3, g + 1)
                for b in range(nb):
                    pe.transpose(G[0][:, b * N:b * N + N], z3[:, b, :], ident[0:N, 0:N])
                for b in range(nb):
                    ins = pe.transpose(G[1][:, b * N:b * N + N], h3[:, b, :], ident[0:N, 0:N])
                ins.then_inc(l_z3t_ps, 1)

            def route(g, nb):
                n = nb * N
                pe.wait_ge(l_z3t, g + 1)
                mm(G[2][0:1, 0:n], pool_ws[:], z3t[:, 0:nb, :].rearrange("p b n -> p (b n)"), start=True, stop=True).then_inc(r_sc_ps, 1)
                pe.wait_ge(r_aw, g + 1)
                mm(G[3][:, 0:n], ones[0:1, :], pw[:, 0:nb, :].rearrange("p b n -> p (b n)"), start=True, stop=True).then_inc(r_aw_ps, 1)
                pe.wait_ge(r_pool, g + 1)
                mm(G[2][0:nb, 256:256 + E], pooled[:, 0:nb], gate_ws[:], start=True, stop=False)
                mm(G[2][0:nb, 256:256 + E], ones[0:1, 0:nb], gate_bs[:], start=False, stop=True).then_inc(r_gate_ps, 1)
                pe.wait_ge(r_gd, g + 1)
                mm(G[2][:, 320:320 + nb * E], ones[0:nb, :], gd[0:nb, 0:nb, :].rearrange("p b e -> p (b e)"), start=True, stop=True).then_inc(r_gb_ps, 1)

            def experts(g, nb, lo, hi):
                n = nb * N
                x = z3t[:, 0:nb, :].rearrange("p b n -> p (b n)")
                for e in range(lo, hi):
                    if e == 0:
                        pe.wait_ge(r_gb, g + 1)
                        pe.wait_ge(l_acc0, g + 1)
                    for m in range(HB):
                        i = e * HB + m
                        if i >= 3:
                            pe.wait_ge(m_h, g * (E * HB) + (i - 2))
                        mm(G[i % 3][:, 0:n], w1_s[:, e, m * D:(m + 1) * D], x,
                           start=True, stop=True).then_inc(m_h_ps, 1)
                    if e > 0:
                        down(g, nb, e - 1)
                if hi == E:
                    down(g, nb, E - 1)

            def down(g, nb, e):
                n = nb * N
                if e >= 1:
                    pe.wait_ge(m_e, g * E + e)
                pe.wait_ge(m_h, g * (E * HB) + (e + 1) * HB)
                for m in range(HB):
                    ins = mm(G[3][:, 0:n], w2_s[:, e, m, :], ht[:, e % 2, m, 0:n], start=(m == 0), stop=(m == HB - 1))
                ins.then_inc(m_e_ps, 1)

            pe.wait_ge(loaded, EARLY)
            pe.wait_ge(consts, NCONST)
            wq_r = ring[:, 0, 0:4, :].rearrange("p a b -> p (a b)").rearrange("p (h d) -> p h d", h=HEADS)
            ky_r = ring[:, 0, 4:8, :].rearrange("p a b -> p (a b)").rearrange("p (h d) -> p h d", h=HEADS)
            bq_r = ring[:, 1, 0, 0:HEADS]
            for c in range(4):
                if c >= 2:
                    pe.wait_ge(setup_ck, c - 1)
                for i in range(4):
                    half, h = c // 2, (c % 2) * 4 + i
                    r = slice(half * 64, half * 64 + 64)
                    ins = mm(S[c % 2][:, i * EXP:i * EXP + EXP], wq_r[r, h, :], ky_r[r, h, :], start=True, stop=True)
                ins.then_inc(setup_ps, 1)
            for c in range(4):
                for i in range(4):
                    half, h = c // 2, (c % 2) * 4 + i
                    r = slice(half * 64, half * 64 + 64)
                    ins = mm(G[c][0:1, i * EXP:i * EXP + EXP], bq_r[r, h:h + 1], ky_r[r, h, :], start=True, stop=True)
                ins.then_inc(setup_ps, 1)
            pe.wait_ge(setup_dve, 4)
            a_stage(0, NB, True)
            pe.wait_ge(split_moved, 32)
            pe.wait_ge(setup_cb, 3)
            pe.wait_ge(setup_ck, 4)
            t_stage(0, 0, 128)

            def step(s, nxt, cur, prev, first=False):
                t0 = s * 2
                rows = 128 if cur == NB else N
                if cur:
                    unit(t0, 0, rows, first)
                if cur == NB:
                    t_stage(t0 + 1, 1, 128)
                if cur:
                    unit(t0, 1, rows, first)
                if nxt:
                    a_stage(s + 1, nxt, first)
                if first:
                    pe.wait_ge(late_loaded, LATE - 16)
                if prev:
                    if nxt:
                        pe.wait_ge(a_h1, s + 2)
                    l_proj(s - 1, prev)
                if cur:
                    unit(t0, 2, rows, first)
                if prev:
                    l_attn(s - 1, prev)
                if cur:
                    unit(t0, 3, rows, first)
                if nxt:
                    t_stage(t0 + 2, 0, 128 if nxt == NB else N)
                if cur == NB:
                    unit(t0 + 1, 0, rows, False)
                if prev:
                    route(s - 1, prev)
                if cur == NB:
                    unit(t0 + 1, 1, rows, False)
                if prev:
                    experts(s - 1, prev, 0, 4)
                if cur == NB:
                    unit(t0 + 1, 2, rows, False)
                if prev:
                    experts(s - 1, prev, 4, E)
                if cur == NB:
                    unit(t0 + 1, 3, rows, False)

            step(0, NB, NB, 0, first=True)
            step(1, NB, NB, NB)
            with pe.Fori(2, GROUPS - 1) as s:
                step(s, NB, NB, NB)
            step(GROUPS - 1, LAST, NB, NB)
            step(GROUPS, 0, LAST, NB)
            step(GROUPS + 1, 0, 0, LAST)

        @block.scalar
        def _(act):
            def copy(o, i, scale=1.0):
                return act.activation(o, i, ACT.Copy, scale=scale)

            def a_stage(g, nb):
                act.wait_ge(a_tok, g + 1)
                copy(h0[:, 0:nb, :].rearrange("p b d -> p (b d)"), G[0][0:N, 0:nb * D]).then_inc(a_h0, 1)
                act.wait_ge(a_gram_ps, g + 1)
                copy(gram[:, 0:nb, :].rearrange("p b d -> p (b d)"), G[2][:, 0:nb * D])
                copy(zmean[:, 0:nb], G[3][:, 0:nb]).then_inc(a_gram, 1)
                copy(z0t[:, 0:nb, :].rearrange("p b n -> p (b n)"), G[1][:, 0:nb * N])
                act.wait_ge(a_gv_ps, g + 1)
                copy(rmean[:, 0:nb, :].rearrange("p b d -> p (b d)"), G[3][0:1, 0:nb * D])
                copy(gv[:, 0:nb, :].rearrange("p b d -> p (b d)"), G[2][:, 0:nb * D]).then_inc(a_gv, 1)
                act.wait_ge(a_kv_ps, g + 1)
                copy(kv[:, 0:nb, :].rearrange("p b d -> p (b d)"), G[1][:, 0:nb * D],
                     scale=1.0 / (N * float(D) ** 0.5)).then_inc(a_kv, 1)

            def t_stage(t, j, rows, first):
                act.wait_ge(t_q, t + 1)
                act.wait_ge(t_qt_ps, t + 1)
                copy(qt_s[:, 0:rows], qtp[:, 0:rows]).then_inc(t_qt, 1)
                if not isinstance(t, int) or t >= 2:
                    act.wait_ge(t_h2, t - 1)
                copy(hres[0:rows, j, :], h1p[0:rows, j, :])
                copy(qrep[0:rows, j, :], q_s[0:rows, :]).then_inc(t_qrep, 1)
                if not first:
                    act.wait_ge(t_idx, t)
                for c in range(4):
                    act.wait_ge(t_sc_ps, t * 4 + (c + 1))
                    copy(sc[0:rows, 4 * c:4 * c + 4, :].rearrange("p a b -> p (a b)"), S[c % 2][0:rows, :]).then_inc(t_sc, 1)

            def t_soft(t, rows):
                act.wait_ge(t_es, t + 1)
                act.activation(es[0:rows, :, :], es[0:rows, :, :], ACT.Exp).then_inc(t_ee, 1)

            def unit(t, u, rows):
                n = t * UNITS + (u + 1)
                act.wait_ge(u_arg, n)
                act.activation(th[0:rows, :], xu[0:rows, 2, :], ACT.Tanh, scale=0.7978845608028654).then_inc(u_th, 1)
                act.wait_ge(u_v, n)
                for k in range(UR):
                    up = ring[0:rows, u, k, D:ROW]
                    ins = act.activation(up, up, ACT.Copy, scale=vu[0:rows, u, k:k + 1])
                ins.then_inc(u_up, 1)

            def l_proj(g, nb):
                n = nb * N
                act.wait_ge(l_z2t_ps, g + 1)
                copy(z2t[:, 0:n], G[3][:, 0:n]).then_inc(l_z2t, 1)
                for half in range(2):
                    act.wait_ge(l_k_ps, g * 2 + (half + 1))
                    act.activation(kt[:, 2 * half:2 * half + 2, 0:n],
                                   G[3][:, 0:2 * n].rearrange("p (m n) -> p m n", m=2), ACT.Exp).then_inc(l_k, 1)
                for b in range(nb):
                    act.wait_ge(l_qs, g * NB + (b + 1))
                    act.activation(qe[:, b, :, :], qe[:, b, :, :], ACT.Exp).then_inc(l_qe, 1)

            def l_attn(g, nb):
                for b in range(nb):
                    act.wait_ge(l_v_ps, g * NB + (b + 1))
                    copy(vx[:, b, :, 0:LD], G[b][0:N, :].rearrange("p (h d) -> p h d", h=LH)).then_inc(l_v, 1)
                for b in range(nb):
                    act.wait_ge(l_qt_ps, g * NB + (b + 1))
                    bk = G[3] if b == 0 else G[b - 1]
                    copy(qt[:, b, :, :].rearrange("p m n -> p (m n)"), bk[:, 0:HB * N]).then_inc(l_qt, 1)
                for b in range(nb):
                    act.wait_ge(l_at_ps, g * NB + (b + 1))
                    copy(att[:, b, :, :].rearrange("p m n -> p (m n)"), G[b][:, 0:HB * N]).then_inc(l_at, 1)
                act.wait_ge(l_z3t_ps, g + 1)
                copy(z3t[:, 0:nb, :].rearrange("p b n -> p (b n)"), G[0][:, 0:nb * N]).then_inc(l_z3t, 1)

            def start_acc(g, nb):
                if not isinstance(g, int) or g > 0:
                    act.wait_ge(stored, g * 16)
                copy(acc[:, 0:nb, :].rearrange("p b n -> p (b n)"), G[1][:, 0:nb * N]).then_inc(l_acc0, 1)

            def route(g, nb):
                act.wait_ge(r_sub, g + 1)
                act.activation(pw[:, 0:nb, :], pw[:, 0:nb, :], ACT.Exp).then_inc(r_exp, 1)
                act.wait_ge(r_gsub, g + 1)
                act.activation(gl[0:nb, 1, :], gl[0:nb, 0, :], ACT.Exp).then_inc(r_gexp, 1)
                act.wait_ge(r_gb_ps, g + 1)
                copy(gb[:, 0:nb, :].rearrange("p b e -> p (b e)"), G[2][:, 320:320 + nb * E]).then_inc(r_gb, 1)

            def hidden(g, nb, e):
                n = nb * N
                for m in range(HB):
                    i = e * HB + m
                    act.wait_ge(m_h_ps, g * (E * HB) + (i + 1))
                    act.activation(ht[:, e % 2, m, 0:n], G[i % 3][:, 0:n], ACT.Gelu,
                                   bias=b1_s[:, e, m:m + 1]).then_inc(m_h, 1)

            def expert_out(g, nb, e):
                n = nb * N
                act.wait_ge(m_e_ps, g * E + (e + 1))
                if e >= 2:
                    act.wait_ge(m_acc, g * E + (e - 1))
                act.activation(eo[:, e % 2, 0:nb, :].rearrange("p b n -> p (b n)"), G[3][:, 0:n], ACT.Gelu,
                               bias=b2_s[:, e:e + 1]).then_inc(m_e, 1)

            def experts(g, nb, lo, hi):
                for e in range(lo, hi):
                    hidden(g, nb, e)
                    if e > 0:
                        expert_out(g, nb, e - 1)
                if hi == E:
                    expert_out(g, nb, E - 1)

            for c in range(4):
                act.wait_ge(setup_ps, c + 1)
                copy(ck[:, c * 512:c * 512 + 512], S[c % 2][:, :]).then_inc(setup_ck, 1)
            act.wait_ge(consts, NCONST)
            a_stage(0, NB)
            act.wait_ge(packed, 64)
            t_stage(0, 0, 128, True)
            t_soft(0, 128)

            def step(s, nxt, cur, prev, first=False):
                t0 = s * 2
                rows = 128 if cur == NB else N
                if cur:
                    unit(t0, 0, rows)
                if cur == NB:
                    t_stage(t0 + 1, 1, 128, False)
                    t_soft(t0 + 1, 128)
                if cur:
                    unit(t0, 1, rows)
                if nxt:
                    a_stage(s + 1, nxt)
                if prev:
                    l_proj(s - 1, prev)
                if cur:
                    unit(t0, 2, rows)
                if prev:
                    l_attn(s - 1, prev)
                    start_acc(s - 1, prev)
                if cur:
                    unit(t0, 3, rows)
                if nxt:
                    t_stage(t0 + 2, 0, 128 if nxt == NB else N, False)
                    t_soft(t0 + 2, 128 if nxt == NB else N)
                if cur == NB:
                    unit(t0 + 1, 0, rows)
                if prev:
                    route(s - 1, prev)
                if cur == NB:
                    unit(t0 + 1, 1, rows)
                if prev:
                    experts(s - 1, prev, 0, 4)
                if cur == NB:
                    unit(t0 + 1, 2, rows)
                if prev:
                    experts(s - 1, prev, 4, E)
                if cur == NB:
                    unit(t0 + 1, 3, rows)

            step(0, NB, NB, 0, first=True)
            step(1, NB, NB, NB)
            with act.Fori(2, GROUPS - 1) as s:
                step(s, NB, NB, NB)
            step(GROUPS - 1, LAST, NB, NB)
            step(GROUPS, 0, LAST, NB)
            step(GROUPS + 1, 0, 0, LAST)

        A_STEPS, T_STEPS, U_STEPS, L_STEPS = 18, 72, 7, 74

        @block.vector
        def _(dve):
            tt, ts, stt = dve.tensor_tensor, dve.tensor_scalar, dve.scalar_tensor_tensor

            def rsqrt(ch, mv, w, nb):
                v, y, a = w[:, 0, 0:nb], w[:, 1, 0:nb], w[:, 2, 0:nb]
                bits = w[:, 3, 0:nb].bitcast(U32)
                ch.did(ts(v, mv, LN_EPS, None, ALU.add))
                ch.wait()
                ch.did(ts(bits, v.bitcast(U32), 1, None, ALU.logical_shift_right))
                ch.wait()
                ch.did(ts(y.bitcast(I32), bits.bitcast(I32), -1.0, float(MAGIC), ALU.mult, ALU.add))
                for _ in range(NEWTON):
                    ch.wait()
                    ch.did(tt(a, y, y, ALU.mult))
                    ch.wait()
                    ch.did(stt(a, a, -0.5, v, ALU.mult, ALU.mult))
                    ch.wait()
                    ch.did(stt(y, a, 1.5, y, ALU.add, ALU.mult))
                ch.wait()

            def a_stage(g, nb):
                ch = Chain(dve, a_dve, g, A_STEPS)
                dve.wait_ge(a_h0, g + 1)
                for b in range(nb):
                    ch.did(dve.bn_stats(st0[:, b, :], h0[:, b, :]))
                ch.wait()
                dve.sem_inc(carried)
                for b in range(nb):
                    ch.did(dve.bn_aggr(mv0[:, b, :], st0[:, b, :]))
                ch.wait()
                rsqrt(ch, mv0[:, 0:nb, 1], nw0, nb)
                for b in range(nb):
                    ins = ts(z0[:, b, :], h0[:, b, :], mv0[:, b, 0:1], nw0[:, 1, b:b + 1], ALU.subtract, ALU.mult)
                ins.then_inc(a_z0, 1)
                ch.end(nb == NB)
                dve.wait_ge(a_out_ps, g + 1)
                if not isinstance(g, int) or g > 0:
                    dve.wait_ge(packed, g * 64)
                tt(h1[:, 0:nb, :].rearrange("p b d -> p (b d)"), G[0][0:N, 0:nb * D],
                   h0[:, 0:nb, :].rearrange("p b d -> p (b d)"), ALU.add).then_inc(a_h1, 1)

            def t_stage(t, g, j, rows, first, nb=NB):
                r = slice(0, rows)
                ch = Chain(dve, t_dve, t, T_STEPS)
                dve.wait_ge(packed, g * 64 + (64 if nb == NB else 16))
                ch.did(dve.bn_stats(st1[r], h1p[r, j, :]))
                ch.wait()
                dve.sem_inc(carried)
                ch.did(dve.bn_aggr(mv1[r], st1[r]))
                ch.wait()
                rsqrt(ch, mv1[r, 1:2], nw1[r], 1)
                if not first:
                    dve.wait_ge(t_qt_ps, t)
                    dve.wait_ge(t_qrep, t)
                ts(q_s[r], h1p[r, j, :], mv1[r, 0:1], nw1[r, 1, 0:1], ALU.subtract, ALU.mult).then_inc(t_q, 1)
                for c in range(4):
                    dve.wait_ge(t_sc, t * 4 + (c + 1))
                    dve.sem_inc(carried)
                    for i in range(4 * c, 4 * c + 4):
                        ch.did(dve.max(s8[r, i, :], sc[r, i, :]))
                    if c:
                        ch.wait(4)
                        dve.sem_inc(carried)
                        for i in range(4 * c - 4, 4 * c):
                            dve.max_index(i8[r, i, :], s8[r, i, :], sc[r, i, :]).then_inc(t_dve, 1)
                            ch.n += 1
                ch.wait(4)
                dve.sem_inc(carried)
                for i in range(12, 16):
                    ch.did(dve.max_index(i8[r, i, :], s8[r, i, :], sc[r, i, :]))
                shape = [rows, HEADS, TOPK, TOPK]
                ch.did(tt(pair[r], s8[r, 0:HEADS, :].unsqueeze(3).to_broadcast(shape),
                          s8[r, HEADS:2 * HEADS, :].unsqueeze(2).to_broadcast(shape), ALU.add))
                ch.wait(1)
                ch.did(dve.tensor_copy(i8f[r], i8[r]))
                ch.wait(1)
                dve.sem_inc(carried)
                for h in range(HEADS):
                    ch.did(dve.max(best[r, h, :], pair[r, h, :, :].rearrange("p a b -> p (a b)")))
                ch.wait()
                dve.sem_inc(carried)
                for h in range(HEADS):
                    ch.did(dve.max_index(pos[r, h, :], best[r, h, :], pair[r, h, :, :].rearrange("p a b -> p (a b)")))
                tt(es[r], best[r], best[r, :, 0:1].to_broadcast([rows, HEADS, TOPK]), ALU.subtract).then_inc(t_es, 1)
                ch.wait()
                flat = pos[r].rearrange("p h k -> p (h k)")
                ch.did(ts(ab[r, 0, :], flat, 3, None, ALU.logical_shift_right))
                ch.did(ts(ab[r, 1, :], flat, 7, None, ALU.bitwise_and))
                ch.wait()
                hits = hit[r].rearrange("p i k a -> p (i k) a")
                ch.did(tt(hits, ab[r].rearrange("p i k -> p (i k)").unsqueeze(2).to_broadcast([rows, 128, TOPK]),
                          iota8[r].unsqueeze(1).to_broadcast([rows, 128, TOPK]), ALU.is_equal))
                ch.wait()
                ch.did(tt(hit[r], hit[r], i8f[r].unsqueeze(2).to_broadcast([rows, 2 * HEADS, TOPK, TOPK]), ALU.mult))
                ch.wait()
                ch.did(dve.tensor_reduce(iab[r].rearrange("p i k -> p (i k)"), hits, AX.X, ALU.add))
                ch.wait()
                stt(idx[r, j, :], iab[r, 0, :], float(EXP), iab[r, 1, :], ALU.mult, ALU.add).then_inc(t_idx, 1)
                dve.wait_ge(t_ee, t + 1)
                ch.did(dve.tensor_reduce(den[r, 0, :], es[r], AX.X, ALU.add))
                ch.wait()
                ch.did(dve.reciprocal(den[r, 1, :], den[r, 0, :]))
                ch.wait()
                ch.did(stt(smh[r, j, :].rearrange("p (h k) -> p h k", h=HEADS), es[r], 0.5,
                           den[r, 1, :].unsqueeze(2).to_broadcast([rows, HEADS, TOPK]), ALU.mult, ALU.mult))
                ch.wait()
                ch.end()

            def unit(t, j, u, rows):
                r = slice(0, rows)
                ch = Chain(dve, u_dve, t * UNITS + u, U_STEPS)
                dve.wait_ge(gathered[u], t * (UR * 16) + UR * 16)
                half = UR // 2
                for i in range(2):
                    w = ring[r, u, i * half:i * half + half, 0:D]
                    ch.did(tt(w, w, qrep[r, j, :].unsqueeze(1).to_broadcast([rows, half, D]), ALU.mult))
                for i in range(2):
                    ch.wait(1) if i == 0 else ch.wait(1)
                    ch.did(dve.tensor_reduce(xu[r, 0, i * half:i * half + half], ring[r, u, i * half:i * half + half, 0:D],
                                             AX.X, ALU.add))
                ch.wait()
                ch.did(tt(xu[r, 1, :], xu[r, 0, :], xu[r, 0, :], ALU.mult))
                ch.wait()
                ch.did(ts(xu[r, 1, :], xu[r, 1, :], 0.044715, 1.0, ALU.mult, ALU.add))
                ch.wait()
                tt(xu[r, 2, :], xu[r, 1, :], xu[r, 0, :], ALU.mult).then_inc(u_arg, 1)
                ch.did(tt(xu[r, 3, :], xu[r, 0, :], smh[r, j, u * UR:u * UR + UR], ALU.mult))
                dve.wait_ge(u_th, t * UNITS + (u + 1))
                ch.wait()
                stt(vu[r, u, :], th[r], 1.0, xu[r, 3, :], ALU.add, ALU.mult).then_inc(u_v, 1)
                ch.end()

            def end_tile(t, j, rows):
                r = slice(0, rows)
                dve.wait_ge(u_sum, t * UNITS + UNITS)
                dve.tensor_reduce(usum[r], U[r].rearrange("p (k d) -> p d k", k=4), AX.X, ALU.add).then_inc(t_red, 1)
                if not isinstance(t, int) or t >= 2:
                    dve.wait_ge(unpacked, (t - j) * 32 - (32 if j == 0 else 0))
                dve.wait_ge(t_red, t + 1)
                tt(h2p[r, j, :], usum[r], hres[r, j, :], ALU.add).then_inc(t_h2, 1)

            def normalise(ch, src, dst, nb, done):
                for b in range(nb):
                    ch.did(dve.bn_stats(st2[:, b, :], src[:, b, :]))
                ch.wait()
                dve.sem_inc(carried)
                for b in range(nb):
                    ch.did(dve.bn_aggr(mv2[:, b, :], st2[:, b, :]))
                ch.wait()
                rsqrt(ch, mv2[:, 0:nb, 1], nw2, nb)
                for b in range(nb):
                    ins = ts(dst[:, b, :], src[:, b, :], mv2[:, b, 0:1], nw2[:, 1, b:b + 1], ALU.subtract, ALU.mult)
                ins.then_inc(done, 1)

            def l_proj(g, nb):
                ch = Chain(dve, l_dve, g, L_STEPS)
                dve.wait_ge(unpacked, g * 64 + (64 if nb == NB else 16))
                normalise(ch, h2, z2, nb, l_z2)
                for b in range(nb):
                    dve.wait_ge(l_q_ps, g * NB + (b + 1))
                    ch.did(dve.tensor_reduce(mx[:, b, :], G[b][0:N, :].rearrange("p (h d) -> p h d", h=LH), AX.X, ALU.max))
                    ch.wait()
                    tt(qe[:, b, :, :], G[b][0:N, :].rearrange("p (h d) -> p h d", h=LH),
                       mx[:, b, :].unsqueeze(2).to_broadcast([N, LH, LD]), ALU.subtract).then_inc(l_qs, 1)
                return ch

            def l_attn(g, nb, ch):
                for b in range(nb):
                    dve.wait_ge(l_qe, g * NB + (b + 1))
                    ch.did(dve.tensor_reduce(qsum[:, b, :], qe[:, b, :, :], AX.X, ALU.add))

                def mask(b, pair_of):
                    dve.wait_ge(l_s_ps, g * NB + (b + 1))
                    for odd in range(2):
                        ins = tt(sm[:, b % 2, :, :].rearrange("p (m o) n -> p o m n", o=2)[:, odd, :, :],
                                 G[pair_of + odd][0:N, 0:HB * N].rearrange("p (m n) -> p m n", m=HB),
                                 causal[:].unsqueeze(1).to_broadcast([N, HB, N]), ALU.mult)
                        if odd:
                            ins.then_inc(l_s, 1)

                def divide(b, pair_of):
                    dve.wait_ge(l_a_ps, g * NB + (b + 1))
                    ch.did(ts(dn[:, b, 0, :], qsum[:, b, :], CLIP * float(LD) ** 0.5, None, ALU.mult))
                    ch.wait()
                    a = [G[pair_of + i][0:N, 0:4 * (LD + 1)].rearrange("p (h d) -> p h d", h=4) for i in range(2)]
                    for i in range(2):
                        ch.did(tt(dn[:, b, 1, 4 * i:4 * i + 4], a[i][:, :, LD], dn[:, b, 0, 4 * i:4 * i + 4], ALU.max))
                    ch.wait()
                    ch.did(dve.reciprocal(dn[:, b, 0, :], dn[:, b, 1, :]))
                    ch.wait()
                    for i in range(2):
                        ins = tt(at_s[:, b, 4 * i:4 * i + 4, :], a[i][:, :, 0:LD],
                                 dn[:, b, 0, 4 * i:4 * i + 4].unsqueeze(2).to_broadcast([N, 4, LD]), ALU.mult)
                    ins.then_inc(l_a, 1)

                if nb == NB:
                    mask(0, 0)
                    mask(1, 2)
                    divide(0, 0)
                    mask(2, 2)
                    divide(1, 0)
                    divide(2, 2)
                else:
                    mask(0, 0)
                    divide(0, 2)
                dve.wait_ge(l_o_ps, g + 1)
                ch.did(tt(h3[:, 0:nb, :].rearrange("p b d -> p (b d)"), G[3][0:N, 0:nb * D],
                          h2[:, 0:nb, :].rearrange("p b d -> p (b d)"), ALU.add))
                ch.wait()
                dve.tensor_copy(usum[0:1, 0:1], h3[0:1, 0, 0:1]).then_inc(l_h3, 1)
                normalise(ch, h3, z3, nb, l_z3)

            def route(g, nb, ch):
                dve.wait_ge(r_sc_ps, g + 1)
                s = pw[:, 0:nb, :]
                ch.did(ts(s, G[2][0:1, 0:nb * N].rearrange("p (b n) -> p b n", b=nb), pool_bs[:], None, ALU.add))
                ch.wait()
                ch.did(dve.tensor_reduce(pmx[:, 0, 0:nb], s, AX.X, ALU.max))
                ch.wait()
                tt(s, s, pmx[:, 0, 0:nb].unsqueeze(2).to_broadcast([1, nb, N]), ALU.subtract).then_inc(r_sub, 1)
                dve.wait_ge(r_exp, g + 1)
                ch.did(dve.tensor_reduce(pmx[:, 0, 0:nb], s, AX.X, ALU.add))
                ch.wait()
                ch.did(dve.reciprocal(pmx[:, 1, 0:nb], pmx[:, 0, 0:nb]))
                ch.wait()
                tt(s, s, pmx[:, 1, 0:nb].unsqueeze(2).to_broadcast([1, nb, N]), ALU.mult).then_inc(r_aw, 1)
                dve.wait_ge(r_aw_ps, g + 1)
                ch.did(tt(pz[:, 0:nb, :], z3t[:, 0:nb, :], G[3][:, 0:nb * N].rearrange("p (b n) -> p b n", b=nb), ALU.mult))
                ch.wait()
                dve.tensor_reduce(pooled[:, 0:nb], pz[:, 0:nb, :], AX.X, ALU.add).then_inc(r_pool, 1)
                p = slice(0, nb)
                dve.wait_ge(r_gate_ps, g + 1)
                lg = G[2][p, 256:256 + E]
                ch.did(dve.tensor_reduce(g1[p, 0:1], lg, AX.X, ALU.max))
                ch.wait()
                ts(gl[p, 0, :], lg, g1[p, 0:1], None, ALU.subtract).then_inc(r_gsub, 1)
                dve.wait_ge(r_gexp, g + 1)
                ch.did(dve.tensor_reduce(g1[p, 1:2], gl[p, 1, :], AX.X, ALU.add))
                ch.wait()
                ch.did(dve.reciprocal(g1[p, 2:3], g1[p, 1:2]))
                ch.wait()
                ch.did(ts(gl[p, 2, :], gl[p, 1, :], g1[p, 2:3], None, ALU.mult))
                ch.wait()
                dve.sem_inc(carried)
                ch.did(dve.max(gl[p, 3, :], gl[p, 2, :]))
                ch.wait()
                dve.sem_inc(carried)
                ch.did(dve.max_index(gi[p, :], gl[p, 3, :], gl[p, 2, :]))
                ch.wait()
                ch.did(dve.tensor_copy(gl[p, 3, :], gi[p, :]))
                ch.wait()
                ch.did(ts(gl[p, 4, :], iota8[p, :], gl[p, 3, 0:1], None, ALU.is_equal))
                ch.wait()
                ch.did(stt(gl[p, 5, :], iota8[p, :], gl[p, 3, 1:2], gl[p, 4, :], ALU.is_equal, ALU.add))
                ch.wait()
                ch.did(tt(gl[p, 4, :], gl[p, 5, :], gl[p, 2, :], ALU.mult))
                ch.wait()
                ch.did(dve.tensor_reduce(g1[p, 1:2], gl[p, 4, :], AX.X, ALU.add))
                ch.wait()
                ch.did(ts(g1[p, 3:4], g1[p, 1:2], DEN_EPS, None, ALU.add))
                ch.wait()
                ch.did(dve.reciprocal(g1[p, 2:3], g1[p, 3:4]))
                ch.wait()
                ch.did(ts(gl[p, 5, :], gl[p, 4, :], g1[p, 2:3], None, ALU.mult))
                ch.wait()
                tt(gd[p, 0:nb, :], own_batch[p, 0:nb, :], gl[p, 5, :].unsqueeze(1).to_broadcast([nb, nb, E]), ALU.mult)\
                    .then_inc(r_gd, 1)
                ch.end(nb == NB)

            def experts(g, nb, lo, hi):
                if lo == 0:
                    dve.wait_ge(r_gb, g + 1)
                    dve.wait_ge(l_acc0, g + 1)
                for e in range(max(lo, 1), hi + (hi == E)):
                    dve.wait_ge(m_e, g * E + e)
                    if e > 1:
                        dve.wait_ge(m_acc, g * E + (e - 1))
                    for b in range(nb):
                        ins = stt(acc[:, b, :], eo[:, (e - 1) % 2, b, :], gb[:, b, e - 1:e], acc[:, b, :], ALU.mult, ALU.add)
                    ins.then_inc(m_acc, 1)

            dve.memset(cb3[:], 0.0).then_inc(setup_cb, 1)
            for c in range(4):
                dve.wait_ge(setup_ps, 5 + c)
                dve.tensor_copy(cb[:, c * 512:c * 512 + 512], G[c][0:1, :]).then_inc(setup_dve, 1)
            dve.wait_ge(setup_dve, 4)
            dve.wait_ge(setup_cb, 1)
            dve.tensor_copy(cb3[0:1, :], cb).then_inc(setup_dve, 1)
            dve.wait_ge(setup_dve, 5)
            tt(cbr, cb, cb3[0:1, :], ALU.subtract).then_inc(setup_dve, 1)
            dve.wait_ge(setup_dve, 6)
            dve.tensor_copy(cbp[:, 0, :], cbr).then_inc(setup_dve, 1)
            dve.wait_ge(setup_dve, 7)
            tt(cb, cbr, cbp[:, 0, :], ALU.subtract).then_inc(setup_dve, 1)
            dve.wait_ge(setup_dve, 8)
            dve.tensor_copy(cbp[:, 1, :], cb).then_inc(setup_cb, 1)
            dve.memset(usum[0:1, 0:1], 0.0).then_inc(setup_cb, 1)
            dve.wait_ge(consts, NCONST)
            a_stage(0, NB)
            t_stage(0, 0, 0, 128, True)

            def step(s, nxt, cur, prev, first=False):
                t0 = s * 2
                rows = 128 if cur == NB else N
                ch = None
                if cur:
                    unit(t0, 0, 0, rows)
                if cur == NB:
                    t_stage(t0 + 1, s, 1, 128, False)
                if cur:
                    unit(t0, 0, 1, rows)
                if nxt:
                    a_stage(s + 1, nxt)
                if prev:
                    if not cur:
                        dve.wait_ge(late_loaded, LATE - 16)
                    ch = l_proj(s - 1, prev)
                if cur:
                    unit(t0, 0, 2, rows)
                if prev:
                    l_attn(s - 1, prev, ch)
                if cur:
                    unit(t0, 0, 3, rows)
                if cur:
                    end_tile(t0, 0, rows)
                if nxt:
                    t_stage(t0 + 2, s + 1, 0, 128 if nxt == NB else N, False, nxt)
                if cur == NB:
                    unit(t0 + 1, 1, 0, rows)
                if prev:
                    route(s - 1, prev, ch)
                if cur == NB:
                    unit(t0 + 1, 1, 1, rows)
                if prev:
                    experts(s - 1, prev, 0, 4)
                if cur == NB:
                    unit(t0 + 1, 1, 2, rows)
                if prev:
                    experts(s - 1, prev, 4, E)
                if cur == NB:
                    unit(t0 + 1, 1, 3, rows)
                    end_tile(t0 + 1, 1, rows)

            step(0, NB, NB, 0, first=True)
            dve.wait_ge(late_loaded, LATE - 16)
            step(1, NB, NB, NB)
            with dve.Fori(2, GROUPS - 1) as s:
                step(s, NB, NB, NB)
            step(GROUPS - 1, LAST, NB, NB)
            step(GROUPS, 0, LAST, NB)
            step(GROUPS + 1, 0, 0, LAST)


def kernel(**inputs):
    import numpy as _np
    import concourse.bacc as _bacc
    from concourse import mybir as _mybir
    from concourse.bass_utils import run_bass_kernel_spmd as _run

    a = {k: _np.asarray(v) for k, v in inputs.items()}
    x = a["x"][:, :CTX * N, :].reshape(B, N, 2, KIN).transpose(0, 3, 2, 1)
    full = x[:GROUPS * NB].reshape(GROUPS, NB, KIN, 2, N).transpose(0, 2, 3, 1, 4)
    keys = a["L0_ffn_keys"].transpose(1, 3, 0, 2)
    data = {
        "xg": full.reshape(GROUPS * KIN, 2 * GT),
        "xl": x[GROUPS * NB:].transpose(1, 2, 0, 3).reshape(KIN, 2 * LAST * N),
        "tok_w": a["L0_tok_weight"].T.reshape(2, KIN, D).transpose(1, 0, 2),
        "tok_b": a["L0_tok_bias"],
        "wv_t": a["L0_attn_W_v"].T,
        "wth_t": a["L0_attn_W_theta"].T,
        "pq_w": a["L0_ffn_Wq"].reshape(HEADS, 128, D).transpose(1, 0, 2).reshape(128, HEADS * D),
        "pq_b": a["L0_ffn_bq"].reshape(HEADS, 128).T,
        "pkeys": keys.reshape(128, HEADS * EXP),
        "table": _np.concatenate([a["L0_ffn_w_down_embed"], a["L0_ffn_w_up_embed"]], axis=1),
        "aq": a["L1_attn_Wq"],
        "ak": a["L1_attn_Wk"],
        "av": a["L1_attn_Wv"],
        "ao": a["L1_attn_Wo"].reshape(HB, D, D).transpose(1, 0, 2).reshape(D, HB * D),
        "abo": a["L1_attn_bo"].reshape(1, D),
        "pool_w": a["L1_ffn_attn_w"],
        "pool_b": a["L1_ffn_attn_b"].reshape(1, 1),
        "gate_w": a["L1_ffn_gate_w"],
        "gate_b": a["L1_ffn_gate_b"].reshape(1, E),
        "w1": a["L1_ffn_w1"].transpose(1, 0, 2).reshape(D, E * HID),
        "b1": a["L1_ffn_b1"].reshape(E, HB, D).transpose(2, 0, 1).reshape(D, E * HB),
        "w2": a["L1_ffn_w2"].reshape(E, HB, D, D).transpose(2, 0, 1, 3).reshape(D, E * HB * D),
        "b2": a["L1_ffn_b2"].T,
    }
    nc = _bacc.Bacc("TRN2", target_bir_lowering=False, num_devices=1)
    arrays, args = {}, []
    for name, v in data.items():
        v = _np.ascontiguousarray(v)
        arrays[f"in_{name}_dram"] = v
        args.append(nc.dram_tensor(f"in_{name}_dram", v.shape, _mybir.dt.from_np(v.dtype), kind="ExternalInput").ap())
    outs = []
    for i, shape in enumerate([(GROUPS * D, GT), (D, LAST * N)]):
        outs.append(nc.dram_tensor(f"out_{i}_dram", shape, F32, kind="ExternalOutput").ap())
    tower(nc, *args, *outs)
    r = _run(nc, [arrays], core_ids=[0])
    main = _np.asarray(r.results[0]["out_0_dram"]).reshape(GROUPS, D, NB, N).transpose(0, 2, 3, 1).reshape(GROUPS * NB, N, D)
    last = _np.asarray(r.results[0]["out_1_dram"]).reshape(D, LAST, N).transpose(1, 2, 0)
    return _np.ascontiguousarray(_np.concatenate([main, last], axis=0))
```

```python
from contextlib import ExitStack

import concourse.bass as bass
from concourse import mybir

F32 = mybir.dt.float32
BF16 = mybir.dt.bfloat16
I32 = mybir.dt.int32
U32 = mybir.dt.uint32
ALU = mybir.AluOpType
ACT = mybir.ActivationFunctionType
AX = mybir.AxisListType

B, FRAMES, FEAT = 64, 256, 64
CTX = 3
N = 85
D = 128
KIN = CTX * FEAT // 2
HEADS, EXP, TOPK = 8, 128, 8
ROW = 2 * D
LH, LD = 8, 64
E, HID = 8, 512
HB = HID // D
LN_EPS = 1e-5
CLIP = 1e-3
DEN_EPS = 1e-9

NB = 3
GROUPS = B // NB
LAST = B - GROUPS * NB
GT = NB * N
UNITS = 4
UR = HEADS * TOPK // UNITS
QSUM = 384
MAGIC = 0x5F3759DF
NEWTON = 3
EO = 4
USES = 3 * E


def tower(nc, xg, xl, tok_w, tok_b, wv_t, wth_t, pq_w, pq_b, pkeys, table, aq, ak, av, ao, abo,
          pool_w, pool_b, gate_w, gate_b, w1, b1, w2, b2, out, out_last):
    ctx = ExitStack()
    with ctx:
        def sb(name, shape, dt=F32):
            return ctx.enter_context(nc.sbuf_tensor(name, shape, dt))

        def bank(name):
            return ctx.enter_context(nc.psum_tensor(name, [128, 512], F32))

        def sem(name):
            return ctx.enter_context(nc.semaphore(name))

        tok_ws = sb("tok_ws", [KIN, 2, D])
        tok_bs = sb("tok_bs", [1, D])
        wv_s = sb("wv_s", [D, D])
        wth_s = sb("wth_s", [D, D])
        ck = sb("ck", [D, 2 * HEADS * EXP])
        cb3 = sb("cb3", [D, 2 * HEADS * EXP], BF16)
        aq_s = sb("aq_s", [D, LH * LD])
        ak_s = sb("ak_s", [D, LH * LD])
        av_s = sb("av_s", [D, LH * LD])
        ao_s = sb("ao_s", [D, HB, D])
        abo_s = sb("abo_s", [1, D])
        pool_ws = sb("pool_ws", [D, 1])
        pool_bs = sb("pool_bs", [1, 1])
        gate_ws = sb("gate_ws", [D, E])
        gate_bs = sb("gate_bs", [1, E])
        w1_s = sb("w1_s", [D, E, HID])
        w2_s = sb("w2_s", [D, E, HB, D])
        b1_s = sb("b1_s", [D, E, HB])
        b2_s = sb("b2_s", [D, E])
        ident = sb("ident", [128, 128])
        ones = sb("ones", [128, 128])
        ones3 = sb("ones3", [128, 128], BF16)
        mean_col = sb("mean_col", [N, 1])
        causal = sb("causal", [N, N])
        iota8 = sb("iota8", [128, 8])
        halves = sb("halves", [D, 2])
        own_batch = sb("own_batch", [NB, NB, E])
        x_s = sb("x_s", [KIN, 2, GT])
        h0 = sb("h0", [N, NB, D])
        z0 = sb("z0", [N, NB, D])
        z0t = sb("z0t", [D, NB, N])
        gram = sb("gram", [D, NB, D])
        zmean = sb("zmean", [D, NB])
        gv = sb("gv", [D, NB, D])
        rmean = sb("rmean", [1, NB, D])
        kv = sb("kv", [D, NB, D])
        h1 = sb("h1", [N, NB, D])
        st0 = sb("st0", [N, NB, 6])
        mv0 = sb("mv0", [N, NB, 2])
        nw0 = sb("nw0", [N, 4, NB])
        h1p = sb("h1p", [128, 2, D])
        hres = sb("hres", [128, 2, D])
        q_s = sb("q_s", [128, D])
        qt_s = sb("qt_s", [D, 128])
        st1 = sb("st1", [128, 6])
        mv1 = sb("mv1", [128, 2])
        nw1 = sb("nw1", [128, 5, 1])
        sc = sb("sc", [128, 2 * HEADS, EXP])
        s8 = sb("s8", [128, 2 * HEADS, TOPK])
        i8 = sb("i8", [128, 2 * HEADS, TOPK], U32)
        i8f = sb("i8f", [128, 2 * HEADS, TOPK])
        pair = sb("pair", [128, HEADS, TOPK, TOPK])
        best = sb("best", [128, HEADS, TOPK])
        pos = sb("pos", [128, HEADS, TOPK], U32)
        ab = sb("ab", [128, 2, HEADS * TOPK], U32)
        hit = sb("hit", [128, 2 * HEADS, TOPK, TOPK])
        iab = sb("iab", [128, 2, HEADS * TOPK])
        idx = sb("idx", [128, 2, HEADS * TOPK], U32)
        es = sb("es", [128, HEADS, TOPK])
        den = sb("den", [128, 2, HEADS])
        smh = sb("smh", [128, 2, HEADS * TOPK])
        ring = sb("ring", [128, UNITS, UR, ROW])
        spare = ring[0:1, 2:4, :, :].rearrange("p u k d -> p (u k d)")
        cb = spare[:, 0:2048]
        cbr = spare[:, 2048:4096]
        cbp = spare[:, 4096:6144].bitcast(BF16).rearrange("p (a n) -> p a n", a=2)
        xu = sb("xu", [128, 4, UR])
        th = sb("th", [128, UR])
        vu = sb("vu", [128, UNITS, UR])
        usum = sb("usum", [128, D])
        h2p = sb("h2p", [128, 2, D])
        h2 = sb("h2", [N, NB, D])
        st2 = sb("st2", [N, NB, 6])
        mv2 = sb("mv2", [N, NB, 2])
        nw2 = sb("nw2", [N, 4, NB])
        z2 = sb("z2", [N, NB, D])
        z2t = sb("z2t", [D, GT])
        kt = sb("kt", [D, HB, GT])
        mx = sb("mx", [N, NB, LH])
        qe = sb("qe", [N, NB, LH, LD])
        vx = sb("vx", [N, NB, LH, LD + 1])
        qt = sb("qt", [D, NB, HB, N])
        sm = sb("sm", [N, 2, HB, N])
        dn = sb("dn", [N, NB, 3, LH])
        at_s = qe
        att = qt
        h3 = sb("h3", [N, NB, D])
        z3 = sb("z3", [N, NB, D])
        z3t = sb("z3t", [D, NB, N])
        pw = sb("pw", [1, NB, N])
        pmx = sb("pmx", [1, 2, NB])
        pz = sb("pz", [D, NB, N])
        pooled = sb("pooled", [D, NB])
        gl = sb("gl", [NB, 6, E])
        g1 = sb("g1", [NB, 4])
        gi = sb("gi", [NB, E], U32)
        gd = sb("gd", [NB, NB, E])
        gb = sb("gb", [D, NB, E])
        ht = sb("ht", [D, 2, HB, GT])
        eo = sb("eo", [D, EO, NB, N])
        h3t = sb("h3t", [D, NB, N])
        acc = sb("acc", [D, NB, N])

        S = [bank("bank_s0"), bank("bank_s1")]
        U = bank("bank_u")
        Q = bank("bank_q")
        G = [bank("bank_l0"), bank("bank_l1")]
        X = [bank("bank_x0"), bank("bank_x1")]
        qrep = Q[:, 0:2 * D].rearrange("p (j d) -> p j d", j=2)
        qtp = S[0][:, 0:128]

        tokens_loaded = sem("tokens_loaded")
        loaded = sem("loaded")
        late_loaded = sem("late_loaded")
        split_moved = sem("split_moved")
        consts = sem("consts")
        pool_order = sem("pool_order")
        setup_ps = sem("setup_ps")
        setup_ck = sem("setup_ck")
        setup_cb = sem("setup_cb")
        setup_dve = sem("setup_dve")
        x_in = sem("x_in")
        a_tok = sem("a_tok")
        a_h0 = sem("a_h0")
        a_dve = sem("a_dve")
        a_z0 = sem("a_z0")
        a_gram_ps = sem("a_gram_ps")
        a_gram = sem("a_gram")
        a_gv_ps = sem("a_gv_ps")
        a_gv = sem("a_gv")
        a_kv_ps = sem("a_kv_ps")
        a_kv = sem("a_kv")
        a_out_ps = sem("a_out_ps")
        a_h1 = sem("a_h1")
        packed = sem("packed")
        t_dve = sem("t_dve")
        t_q = sem("t_q")
        t_qt_ps = sem("t_qt_ps")
        t_qt = sem("t_qt")
        t_qrep = sem("t_qrep")
        t_kept = sem("t_kept")
        t_sc_ps = sem("t_sc_ps")
        t_sc = sem("t_sc")
        t_idx = sem("t_idx")
        t_es = sem("t_es")
        t_ee = sem("t_ee")
        gathered = [sem(f"gathered{u}") for u in range(UNITS)]
        u_dve = sem("u_dve")
        u_arg = sem("u_arg")
        u_th = sem("u_th")
        u_v = sem("u_v")
        u_up = sem("u_up")
        u_sum = sem("u_sum")
        t_red = sem("t_red")
        t_h2 = sem("t_h2")
        unpacked = sem("unpacked")
        l_dve = sem("l_dve")
        l_z2 = sem("l_z2")
        l_z2t_ps = sem("l_z2t_ps")
        l_z2t = sem("l_z2t")
        l_q_ps = sem("l_q_ps")
        l_qs = sem("l_qs")
        l_qe = sem("l_qe")
        l_k_ps = sem("l_k_ps")
        l_k = sem("l_k")
        l_v_ps = sem("l_v_ps")
        l_v = sem("l_v")
        l_qt_ps = sem("l_qt_ps")
        l_qt = sem("l_qt")
        l_s_ps = sem("l_s_ps")
        l_s = sem("l_s")
        l_a_ps = sem("l_a_ps")
        l_a = sem("l_a")
        l_at_ps = sem("l_at_ps")
        l_at = sem("l_at")
        l_o_ps = sem("l_o_ps")
        l_h3 = sem("l_h3")
        l_z3 = sem("l_z3")
        l_z3t_ps = sem("l_z3t_ps")
        l_z3t = sem("l_z3t")
        l_h3t = sem("l_h3t")
        r_sc_ps = sem("r_sc_ps")
        r_sub = sem("r_sub")
        r_exp = sem("r_exp")
        r_aw = sem("r_aw")
        r_aw_ps = sem("r_aw_ps")
        r_pool = sem("r_pool")
        r_gate_ps = sem("r_gate_ps")
        r_gsub = sem("r_gsub")
        r_gexp = sem("r_gexp")
        r_dve = sem("r_dve")
        r_gd = sem("r_gd")
        r_gb_ps = sem("r_gb_ps")
        r_gb = sem("r_gb")
        x_ps = sem("x_ps")
        x_out = sem("x_out")
        m_acc = sem("m_acc")
        stored = sem("stored")

        carried = sem("carried")
        EARLY = 5 * 16
        LATE = 14 * 16
        NCONST = 11

        def expert_uses():
            uses = []
            for e in range(E):
                uses += [("hidden", e, 0)] + ([("out", e - 1, 0)] if e else []) + [("hidden", e, 1)]
            return uses + [("out", E - 1, 0)]

        uses = expert_uses()
        assert len(uses) == USES
        place = {use: i for i, use in enumerate(uses)}

        def uses_between(lo, hi):
            return list(enumerate(uses))[place["hidden", lo, 0]:place["hidden", hi, 0] if hi < E else USES]

        def first(v):
            return isinstance(v, int) and v <= 0

        class Chain:

            def __init__(self, eng, s, turn, per):
                self.eng, self.s, self.base, self.n, self.per = eng, s, turn * per, 0, per

            def did(self, ins):
                ins.then_inc(self.s, 1)
                self.n += 1

            def wait(self, back=0):
                self.eng.wait_ge(self.s, self.base + (self.n - back))

            def end(self, whole=True):
                assert self.n == self.per or not whole, (self.s, self.n, self.per)

        def run_steps(eng, step):
            def nb(g):
                return NB if 0 <= g < GROUPS else LAST if g == GROUPS else 0

            for s in range(3):
                step(s, nb(s + 1), nb(s), nb(s - 1), nb(s - 2))
            with eng.Fori(3, GROUPS - 1) as s:
                step(s, NB, NB, NB, NB)
            for s in range(GROUPS - 1, GROUPS + 3):
                step(s, nb(s + 1), nb(s), nb(s - 1), nb(s - 2))

        block = ctx.enter_context(nc.Block())

        @block.sync
        def _(sp):
            def load_x(g, nb):
                if nb == NB:
                    sp.dma_start(x_s[:].rearrange("p c n -> p (c n)"), xg[bass.ds(g * KIN, KIN), :]).then_inc(x_in, 16)
                else:
                    sp.dma_start(x_s[:, :, 0:nb * N], xl.rearrange("p (c n) -> p c n", c=2)).then_inc(x_in, 16)

            def pack(g, nb):
                sp.wait_ge(a_h1, g + 1)
                sp.sem_inc(carried)
                sp.wait_ge(t_kept, g * 2)
                sp.sem_inc(carried)
                pieces = [(0, 0, N, 0, 0)]
                if nb == NB:
                    a = 128 - N
                    pieces += [(1, 0, a, 0, N), (1, a, N - a, 1, 0), (2, 0, N, 1, N - a)]
                for b, r, n, j, p in pieces:
                    sp.dma_start(h1p[p:p + n, j, :], h1[r:r + n, b, :]).then_inc(packed, 16)

            def unpack(g, j, nb):
                sp.wait_ge(t_h2, 2 * g + (j + 1))
                a = 128 - N
                if j == 0:
                    pieces = [(0, 0, N, 0)] + ([(1, 0, a, N)] if nb == NB else [])
                else:
                    pieces = [(1, a, N - a, 0), (2, 0, N, N - a)]
                for b, r, n, p in pieces:
                    sp.dma_start(h2[r:r + n, b, :], h2p[p:p + n, j, :]).then_inc(unpacked, 16)

            def store(g, nb):
                sp.wait_ge(m_acc, g * E + E)
                if nb == NB:
                    sp.dma_start(out[bass.ds(g * D, D), :], acc[:].rearrange("p b n -> p (b n)")).then_inc(stored, 16)
                else:
                    sp.dma_start(out_last, acc[:, 0, :]).then_inc(stored, 16)

            load_x(0, NB)
            for dst, src in ((tok_ws[:], tok_w), (tok_bs[:], tok_b)):
                sp.dma_start(dst, src).then_inc(tokens_loaded, 16)
            for dst, src in ((ring[:, 0, 0:4, :], pq_w), (ring[:, 0, 4:8, :], pkeys)):
                sp.dma_start(dst.rearrange("p a b -> p (a b)"), src).then_inc(loaded, 16)
            sp.dma_start(ring[:, 1, 0, 0:HEADS], pq_b).then_inc(loaded, 16)
            for dst, src in ((wv_s[:], wv_t), (wth_s[:], wth_t)):
                sp.dma_start(dst, src).then_inc(loaded, 16)
            pack(0, NB)
            sp.wait_ge(setup_cb, 2)
            sp.dma_start(cb3[1:2, :], cbp[:, 0, :]).then_inc(split_moved, 16)
            sp.dma_start(cb3[2:3, :], cbp[:, 1, :]).then_inc(split_moved, 16)
            for dst, src in ((aq_s[:], aq), (ak_s[:], ak), (av_s[:], av), (ao_s[:].rearrange("p a b -> p (a b)"), ao),
                             (abo_s[:], abo), (pool_ws[:], pool_w), (pool_bs[:], pool_b), (gate_ws[:], gate_w),
                             (gate_bs[:], gate_b), (w1_s[:].rearrange("p e h -> p (e h)"), w1),
                             (w2_s[:].rearrange("p e m d -> p (e m d)"), w2),
                             (b1_s[:].rearrange("p e m -> p (e m)"), b1), (b2_s[:], b2)):
                sp.dma_start(dst, src).then_inc(late_loaded, 16)

            def step(s, nxt, cur, att, moe):
                if nxt:
                    sp.wait_ge(a_tok, s + 1)
                    load_x(s + 1, nxt)
                if att == NB:
                    unpack(s - 1, 1, att)
                if nxt:
                    pack(s + 1, nxt)
                if moe:
                    store(s - 2, moe)
                if cur:
                    if att:
                        sp.wait_ge(l_h3, s)
                    unpack(s, 0, cur)

            run_steps(sp, step)
            sp.wait_ge(stored, (GROUPS + 1) * 16)

        @block.gpsimd
        def _(pool):
            pool.memset(ident[:], 0.0).then_inc(pool_order, 1)
            pool.memset(ones[:], 1.0).then_inc(consts, 1)
            pool.memset(mean_col[:], 1.0 / N).then_inc(consts, 1)
            pool.memset(causal[:], 1.0).then_inc(pool_order, 1)
            pool.memset(own_batch[:], 1.0).then_inc(pool_order, 1)
            pool.memset(ones3[:], 0.0).then_inc(pool_order, 1)
            pool.wait_ge(pool_order, 4)
            pool.affine_select(out=ident[:], in_=ident[:], compare_op=ALU.not_equal, fill=1.0, base=0,
                               pattern=[[-1, 128]], channel_multiplier=1).then_inc(consts, 1)
            pool.affine_select(out=causal[:], in_=causal[:], compare_op=ALU.is_ge, fill=0.0, base=0,
                               pattern=[[1, N]], channel_multiplier=-1).then_inc(consts, 1)
            pool.affine_select(out=own_batch[:], in_=own_batch[:], compare_op=ALU.is_equal, fill=0.0, base=0,
                               pattern=[[1, NB], [0, E]], channel_multiplier=-1).then_inc(consts, 1)
            pool.affine_select(out=ones3[:], in_=ones3[:], compare_op=ALU.is_ge, fill=1.0, base=-3,
                               pattern=[[0, 128]], channel_multiplier=1).then_inc(consts, 1)
            pool.iota(iota8[:], pattern=[[1, 8]], base=0, channel_multiplier=0,
                      allow_small_or_imprecise_dtypes=True).then_inc(consts, 1)
            pool.memset(vx[:, :, :, LD:LD + 1], 1.0).then_inc(consts, 1)
            pool.memset(h1p[:], 0.0).then_inc(consts, 1)
            pool.memset(halves[:], 0.0).then_inc(pool_order, 1)
            pool.wait_ge(pool_order, 5)
            pool.memset(halves[0:LD, 0:1], 1.0).then_inc(consts, 1)
            pool.memset(halves[LD:D, 1:2], 1.0).then_inc(consts, 1)

            def gather(t, j, rows, first):
                pool.wait_ge(t_idx, t + 1)
                for u in range(UNITS):
                    if not first:
                        pool.wait_ge(u_sum, (t - 1) * UNITS + (u + 1))
                    pool.sem_inc(carried)
                    for k in range(UR):
                        c = u * UR + k
                        pool.indirect_dma_start(
                            ring[0:rows, u, k, :], None, table,
                            bass.IndirectOffsetOnAxis(ap=idx[0:rows, j, c:c + 1], axis=0)).then_inc(gathered[u], 16)

            gather(0, 0, 128, True)
            gather(1, 1, 128, False)
            with pool.Fori(1, GROUPS) as g:
                gather(g * 2, 0, 128, False)
                gather(g * 2 + 1, 1, 128, False)
            gather(2 * GROUPS, 0, N, False)

        @block.tensor
        def _(pe):
            mm = pe.matmul

            def a_tokens(g, nb):
                pe.wait_ge(x_in, g * 16 + 16)
                if not first(g):
                    pe.wait_ge(t_sc, g * 8)
                for b in range(nb):
                    o = S[0][0:N, b * D:b * D + D]
                    mm(o, x_s[:, 0, b * N:b * N + N], tok_ws[:, 0, :], start=True, stop=False)
                    mm(o, x_s[:, 1, b * N:b * N + N], tok_ws[:, 1, :], start=False, stop=False)
                    ins = mm(o, ones[0:1, 0:N], tok_bs[:], start=False, stop=True)
                ins.then_inc(a_tok, 1)

            def a_gram_of(g, nb):
                pe.wait_ge(a_z0, g + 1)
                for b in range(nb):
                    mm(S[0][:, b * D:b * D + D], z0[:, b, :], z0[:, b, :], start=True, stop=True)
                for b in range(nb):
                    mm(S[1][:, NB * N + b:NB * N + b + 1], z0[:, b, :], mean_col[:], start=True, stop=True)
                for b in range(nb):
                    ins = pe.transpose(S[1][:, b * N:b * N + N], z0[:, b, :], ident[0:N, 0:N])
                ins.then_inc(a_gram_ps, 1)

            def a_values(g, nb):
                pe.wait_ge(a_gram, g + 1)
                for b in range(nb):
                    mm(S[0][:, b * D:b * D + D], gram[:, b, :], wv_s[:], start=True, stop=True)
                for b in range(nb):
                    ins = mm(S[1][0:1, b * D:b * D + D], zmean[:, b:b + 1], wv_s[:], start=True, stop=True)
                ins.then_inc(a_gv_ps, 1)

            def a_kv_of(g, nb):
                pe.wait_ge(a_gv, g + 1)
                mm(S[0][:, 0:nb * D], wth_s[:], gv[:, 0:nb, :].rearrange("p b d -> p (b d)"), start=True, stop=True).then_inc(a_kv_ps, 1)

            def a_out(g, nb):
                pe.wait_ge(a_kv, g + 1)
                for b in range(nb):
                    o = S[1][0:N, b * D:b * D + D]
                    mm(o, z0t[:, b, :], kv[:, b, :], start=True, stop=False)
                    ins = mm(o, ones[0:1, 0:N], rmean[:, b, :], start=False, stop=True)
                ins.then_inc(a_out_ps, 1)

            def t_turn(t, rows):
                pe.wait_ge(t_q, t + 1)
                pe.transpose(qtp[:, 0:rows], q_s[0:rows, :], ident[0:rows, 0:rows]).then_inc(t_qt_ps, 1)

            def t_scores(t, rows):
                pe.wait_ge(t_qt, t + 1)
                for c in range(4):
                    if c >= 2:
                        pe.wait_ge(t_sc, t * 4 + (c - 1))
                    cols = slice(c * 512, c * 512 + 512)
                    mm(S[c % 2][0:rows, :], qt_s[:, 0:rows], ck[:, cols], start=True, stop=False)
                    mm(S[c % 2][0:rows, :], ones3[:, 0:rows], cb3[:, cols], start=False, stop=True).then_inc(t_sc_ps, 1)

            def unit_sum(t, u, rows):
                pe.wait_ge(u_up, t * UNITS + (u + 1))
                if u == 0 and not first(t):
                    pe.wait_ge(t_red, t)
                for c in range(UR // 4):
                    ins = mm(U[0:rows, :], ident[0:rows, 0:rows], ring[0:rows, u, 4 * c:4 * c + 4, D:ROW],
                             start=(u == 0 and c == 0), stop=(u == UNITS - 1 and c == UR // 4 - 1))
                ins.then_inc(u_sum, 1)

            def l_turn(g, nb):
                pe.wait_ge(l_z2, g + 1)
                if not first(g):
                    pe.wait_ge(r_gb, g)
                for b in range(nb):
                    ins = pe.transpose(G[0][:, b * N:b * N + N], z2[:, b, :], ident[0:N, 0:N])
                ins.then_inc(l_z2t_ps, 1)

            def l_queries(g, nb, bs):
                for b in bs:
                    if b == 0:
                        pe.wait_ge(l_z2t, g + 1)
                    if b == 2:
                        pe.wait_ge(l_qs, g * NB + 1)
                    if b < nb:
                        mm(G[(b + 1) % 2][0:N, :], z2t[:, b * N:b * N + N], aq_s[:], start=True, stop=True).then_inc(l_q_ps, 1)

            def l_keys(g, nb, half):
                n = nb * N
                if nb == NB or half == 1:
                    pe.wait_ge(l_qs, g * NB + (2 + half if nb == NB else 1))
                for m in range(2):
                    w = ak_s[:, (2 * half + m) * D:(2 * half + m + 1) * D]
                    ins = mm(G[half][:, m * n:m * n + n], w, z2t[:, 0:n], start=True, stop=True)
                ins.then_inc(l_k_ps, 1)

            def l_values(g, nb):
                for b in range(nb):
                    if b < 2:
                        pe.wait_ge(l_k, g * 2 + (b + 1))
                    else:
                        pe.wait_ge(l_v, g * NB + 1)
                    mm(G[b % 2][0:N, :], z2t[:, b * N:b * N + N], av_s[:], start=True, stop=True).then_inc(l_v_ps, 1)

            def l_queries_turn(g, nb):
                for b in range(nb):
                    if b == 0:
                        pe.wait_ge(l_v, g * NB + 2) if nb == NB else pe.wait_ge(l_k, g * 2 + 2)
                    elif b == 1:
                        pe.wait_ge(l_v, g * NB + 3)
                    else:
                        pe.wait_ge(l_qt, g * NB + 1)
                    pe.wait_ge(l_qe, g * NB + (b + 1))
                    for m in range(HB):
                        ins = pe.transpose(G[(b + 1) % 2][:, m * N:m * N + N],
                                           qe[:, b, 2 * m:2 * m + 2, :].rearrange("p a d -> p (a d)"), ident[0:N, 0:N])
                    ins.then_inc(l_qt_ps, 1)

            def l_scores(g, nb, b):
                for odd in range(2):
                    if b:
                        pe.wait_ge(l_a, g * (2 * NB) + (2 * b - 1 + odd))
                    elif nb == NB:
                        pe.wait_ge(l_qt, g * NB + (2 + odd))
                    else:
                        pe.wait_ge(l_v, g * NB + 1)
                        pe.wait_ge(l_qt, g * NB + 1)
                    if b:
                        pe.wait_ge(l_qt, g * NB + (b + 1))
                    elif not odd:
                        pe.wait_ge(l_qt, g * NB + nb)
                        for bb in range(nb):
                            for m in range(HB):
                                mm(G[0][0:N, QSUM + bb * LH + 2 * m:QSUM + bb * LH + 2 * m + 2], qt[:, bb, m, :], halves[:],
                                   start=True, stop=True)
                    r = slice(odd * LD, odd * LD + LD)
                    for m in range(HB):
                        ins = mm(G[odd][0:N, m * N:m * N + N], kt[r, m, b * N:b * N + N], qt[r, b, m, :],
                                 start=True, stop=True)
                    ins.then_inc(l_s_ps, 1)

            def l_weighted(g, b):
                for odd in range(2):
                    pe.wait_ge(l_s, g * (2 * NB) + (2 * b + 1 + odd))
                    for m in range(HB):
                        ins = mm(G[odd][0:N, m * (LD + 1):(m + 1) * (LD + 1)], sm[:, odd, m, :], vx[:, b, 2 * m + odd, :],
                                 start=True, stop=True)
                    ins.then_inc(l_a_ps, 1)

            def l_out(g, nb):
                for b in range(nb):
                    if b < 2:
                        pe.wait_ge(l_a, g * (2 * NB) + (2 * nb - 1 + (b if nb == NB else 1)))
                    else:
                        pe.wait_ge(l_at, g * NB + 1)
                    for m in range(HB):
                        ins = pe.transpose(G[b % 2][:, m * N:m * N + N],
                                           at_s[:, b, 2 * m:2 * m + 2, :].rearrange("p a d -> p (a d)"), ident[0:N, 0:N])
                    ins.then_inc(l_at_ps, 1)
                for b in range(nb):
                    pe.wait_ge(l_at, g * NB + (max(b, 1) + 1 if nb == NB else 1))
                    o = G[1][0:N, b * D:b * D + D]
                    for m in range(HB):
                        mm(o, att[:, b, m, :], ao_s[:, m, :], start=(m == 0), stop=False)
                    ins = mm(o, ones[0:1, 0:N], abo_s[:], start=False, stop=True)
                ins.then_inc(l_o_ps, 1)

            def l_turn_out(g, nb):
                pe.wait_ge(l_z3, g + 1)
                for b in range(nb):
                    pe.transpose(G[0][:, b * N:b * N + N], z3[:, b, :], ident[0:N, 0:N])
                for b in range(nb):
                    ins = pe.transpose(G[1][:, b * N:b * N + N], h3[:, b, :], ident[0:N, 0:N])
                ins.then_inc(l_z3t_ps, 1)

            def route(g, nb):
                n = nb * N
                pe.wait_ge(l_z3t, g + 1)
                mm(G[0][0:1, 0:n], pool_ws[:], z3t[:, 0:nb, :].rearrange("p b n -> p (b n)"), start=True, stop=True).then_inc(r_sc_ps, 1)
                pe.wait_ge(l_h3t, g + 1)
                pe.wait_ge(r_aw, g + 1)
                mm(G[1][:, 0:n], ones[0:1, :], pw[:, 0:nb, :].rearrange("p b n -> p (b n)"), start=True, stop=True).then_inc(r_aw_ps, 1)
                pe.wait_ge(r_pool, g + 1)
                mm(G[0][0:nb, 256:256 + E], pooled[:, 0:nb], gate_ws[:], start=True, stop=False)
                mm(G[0][0:nb, 256:256 + E], ones[0:1, 0:nb], gate_bs[:], start=False, stop=True).then_inc(r_gate_ps, 1)

            def spread_gates(g, nb):
                pe.wait_ge(r_gd, g + 1)
                mm(G[0][:, 320:320 + nb * E], ones[0:nb, :], gd[0:nb, 0:nb, :].rearrange("p b e -> p (b e)"), start=True, stop=True).then_inc(r_gb_ps, 1)

            def experts(g, nb, lo, hi):
                n = nb * N
                x = z3t[:, 0:nb, :].rearrange("p b n -> p (b n)")
                for i, (what, e, half) in uses_between(lo, hi):
                    if not (first(g) and i < 2):
                        pe.wait_ge(x_out, g * USES + (i - 1))
                    if what == "hidden":
                        if i == 0:
                            pe.wait_ge(l_z3t, g + 1)
                        for m in range(2):
                            k = 2 * half + m
                            ins = mm(X[i % 2][:, m * n:m * n + n], w1_s[:, e, k * D:(k + 1) * D], x, start=True, stop=True)
                    else:
                        pe.wait_ge(x_out, g * USES + (place["hidden", e, 1] + 1))
                        for m in range(HB):
                            ins = mm(X[i % 2][:, 0:n], w2_s[:, e, m, :], ht[:, e % 2, m, 0:n], start=(m == 0), stop=(m == HB - 1))
                    ins.then_inc(x_ps, 1)

            pe.wait_ge(consts, NCONST)
            pe.wait_ge(tokens_loaded, 32)
            a_tokens(0, NB)
            pe.wait_ge(loaded, EARLY)
            wq_r = ring[:, 0, 0:4, :].rearrange("p a b -> p (a b)").rearrange("p (h d) -> p h d", h=HEADS)
            ky_r = ring[:, 0, 4:8, :].rearrange("p a b -> p (a b)").rearrange("p (h d) -> p h d", h=HEADS)
            bq_r = ring[:, 1, 0, 0:HEADS]
            for c in range(4):
                for i in range(4):
                    half, h = c // 2, (c % 2) * 4 + i
                    r = slice(half * 64, half * 64 + 64)
                    ins = mm((G + X)[c][:, i * EXP:i * EXP + EXP], wq_r[r, h, :], ky_r[r, h, :], start=True, stop=True)
                ins.then_inc(setup_ps, 1)
            a_gram_of(0, NB)
            for c in range(4):
                pe.wait_ge(setup_ck, c + 1)
                for i in range(4):
                    half, h = c // 2, (c % 2) * 4 + i
                    r = slice(half * 64, half * 64 + 64)
                    ins = mm((G + X)[c][0:1, i * EXP:i * EXP + EXP], bq_r[r, h:h + 1], ky_r[r, h, :], start=True, stop=True)
                ins.then_inc(setup_ps, 1)
                if c == 1:
                    a_values(0, NB)
            a_kv_of(0, NB)
            a_out(0, NB)
            t_turn(0, 128)
            pe.wait_ge(split_moved, 32)
            pe.wait_ge(setup_cb, 2)
            t_scores(0, 128)
            pe.wait_ge(setup_dve, 4)

            def step(s, nxt, cur, att, moe):
                t0 = s * 2
                rows = 128 if cur == NB else N
                rows_next = 128 if nxt == NB else N
                if moe:
                    spread_gates(s - 2, moe)
                if cur == NB:
                    t_turn(t0 + 1, 128)
                    t_scores(t0 + 1, 128)
                if moe:
                    experts(s - 2, moe, 1, 2)
                if cur:
                    unit_sum(t0, 0, rows)
                if moe:
                    experts(s - 2, moe, 2, 3)
                if nxt:
                    a_tokens(s + 1, nxt)
                if moe:
                    experts(s - 2, moe, 3, 4)
                if cur:
                    unit_sum(t0, 1, rows)
                if att:
                    if isinstance(s, int) and s == 1:
                        pe.wait_ge(late_loaded, LATE - 16)
                    l_turn(s - 1, att)
                    l_queries(s - 1, att, (0, 1))
                if moe:
                    experts(s - 2, moe, 4, 5)
                if att:
                    l_queries(s - 1, att, (2,))
                    l_keys(s - 1, att, 0)
                if nxt:
                    a_gram_of(s + 1, nxt)
                if cur:
                    unit_sum(t0, 2, rows)
                if nxt:
                    a_values(s + 1, nxt)
                    a_kv_of(s + 1, nxt)
                    a_out(s + 1, nxt)
                if att:
                    l_keys(s - 1, att, 1)
                    l_values(s - 1, att)
                    l_queries_turn(s - 1, att)
                if att:
                    l_scores(s - 1, att, 0)
                if nxt:
                    t_turn(t0 + 2, rows_next)
                if att:
                    l_weighted(s - 1, 0)
                if nxt:
                    t_scores(t0 + 2, rows_next)
                if att == NB:
                    l_scores(s - 1, att, 1)
                if cur:
                    unit_sum(t0, 3, rows)
                if att == NB:
                    l_weighted(s - 1, 1)
                    l_scores(s - 1, att, 2)
                if moe:
                    experts(s - 2, moe, 5, 6)
                if att == NB:
                    l_weighted(s - 1, 2)
                if cur == NB:
                    unit_sum(t0 + 1, 0, 128)
                if moe:
                    experts(s - 2, moe, 6, 7)
                if att:
                    l_out(s - 1, att)
                if moe:
                    experts(s - 2, moe, 7, E)
                if cur == NB:
                    unit_sum(t0 + 1, 1, 128)
                if att:
                    l_turn_out(s - 1, att)
                if cur == NB:
                    unit_sum(t0 + 1, 2, 128)
                if att:
                    route(s - 1, att)
                    experts(s - 1, att, 0, 1)
                if cur == NB:
                    unit_sum(t0 + 1, 3, 128)

            run_steps(pe, step)

        @block.scalar
        def _(act):
            def copy(o, i, scale=1.0):
                return act.activation(o, i, ACT.Copy, scale=scale)

            def a_rows(g, nb):
                act.wait_ge(a_tok, g + 1)
                copy(h0[:, 0:nb, :].rearrange("p b d -> p (b d)"), S[0][0:N, 0:nb * D]).then_inc(a_h0, 1)

            def a_gram_of(g, nb):
                act.wait_ge(a_gram_ps, g + 1)
                copy(gram[:, 0:nb, :].rearrange("p b d -> p (b d)"), S[0][:, 0:nb * D])
                copy(zmean[:, 0:nb], S[1][:, NB * N:NB * N + nb])
                copy(z0t[:, 0:nb, :].rearrange("p b n -> p (b n)"), S[1][:, 0:nb * N]).then_inc(a_gram, 1)

            def a_kv_of(g, nb):
                act.wait_ge(a_gv_ps, g + 1)
                copy(rmean[:, 0:nb, :].rearrange("p b d -> p (b d)"), S[1][0:1, 0:nb * D])
                copy(gv[:, 0:nb, :].rearrange("p b d -> p (b d)"), S[0][:, 0:nb * D]).then_inc(a_gv, 1)
                act.wait_ge(a_kv_ps, g + 1)
                copy(kv[:, 0:nb, :].rearrange("p b d -> p (b d)"), S[0][:, 0:nb * D],
                     scale=1.0 / (N * float(D) ** 0.5)).then_inc(a_kv, 1)

            def t_turn(t, j, rows):
                act.wait_ge(t_q, t + 1)
                act.wait_ge(t_qt_ps, t + 1)
                copy(qt_s[:, 0:rows], qtp[:, 0:rows]).then_inc(t_qt, 1)
                copy(qrep[0:rows, j, :], q_s[0:rows, :]).then_inc(t_qrep, 1)

            def t_keep(t, j, rows):
                if not isinstance(t, int) or t >= 2:
                    act.wait_ge(t_h2, t - 1)
                copy(hres[0:rows, j, :], h1p[0:rows, j, :]).then_inc(t_kept, 1)

            def t_scores(t, rows):
                if not first(t):
                    act.wait_ge(t_idx, t)
                for c in range(4):
                    act.wait_ge(t_sc_ps, t * 4 + (c + 1))
                    copy(sc[0:rows, 4 * c:4 * c + 4, :].rearrange("p a b -> p (a b)"), S[c % 2][0:rows, :]).then_inc(t_sc, 1)

            def t_soft(t, rows):
                act.wait_ge(t_es, t + 1)
                act.activation(es[0:rows, :, :], es[0:rows, :, :], ACT.Exp).then_inc(t_ee, 1)

            def unit_tanh(t, u, rows):
                act.wait_ge(u_arg, t * UNITS + (u + 1))
                act.activation(th[0:rows, :], xu[0:rows, 2, :], ACT.Tanh, scale=0.7978845608028654).then_inc(u_th, 1)

            def unit_scale(t, u, rows):
                act.wait_ge(u_v, t * UNITS + (u + 1))
                for k in range(UR):
                    up = ring[0:rows, u, k, D:ROW]
                    ins = act.activation(up, up, ACT.Copy, scale=vu[0:rows, u, k:k + 1])
                ins.then_inc(u_up, 1)

            def l_turn(g, nb):
                n = nb * N
                act.wait_ge(l_z2t_ps, g + 1)
                copy(z2t[:, 0:n], G[0][:, 0:n]).then_inc(l_z2t, 1)

            def l_keys(g, nb, half):
                n = nb * N
                act.wait_ge(l_k_ps, g * 2 + (half + 1))
                act.activation(kt[:, 2 * half:2 * half + 2, 0:n],
                               G[half][:, 0:2 * n].rearrange("p (m n) -> p m n", m=2), ACT.Exp).then_inc(l_k, 1)

            def l_queries(g, nb):
                for b in range(nb):
                    act.wait_ge(l_qs, g * NB + (b + 1))
                    act.activation(qe[:, b, :, :], qe[:, b, :, :], ACT.Exp).then_inc(l_qe, 1)

            def l_values(g, nb):
                for b in range(nb):
                    act.wait_ge(l_v_ps, g * NB + (b + 1))
                    copy(vx[:, b, :, 0:LD], G[b % 2][0:N, :].rearrange("p (h d) -> p h d", h=LH)).then_inc(l_v, 1)
                for b in range(nb):
                    act.wait_ge(l_qt_ps, g * NB + (b + 1))
                    copy(qt[:, b, :, :].rearrange("p m n -> p (m n)"), G[(b + 1) % 2][:, 0:HB * N]).then_inc(l_qt, 1)

            def l_out(g, nb):
                for b in range(nb):
                    act.wait_ge(l_at_ps, g * NB + (b + 1))
                    copy(att[:, b, :, :].rearrange("p m n -> p (m n)"), G[b % 2][:, 0:HB * N]).then_inc(l_at, 1)

            def l_turn_out(g, nb):
                act.wait_ge(l_z3t_ps, g + 1)
                copy(z3t[:, 0:nb, :].rearrange("p b n -> p (b n)"), G[0][:, 0:nb * N]).then_inc(l_z3t, 1)

            def l_residual(g, nb):
                if not first(g):
                    act.wait_ge(m_acc, g * E - (E - 1))
                copy(h3t[:, 0:nb, :].rearrange("p b n -> p (b n)"), G[1][:, 0:nb * N]).then_inc(l_h3t, 1)

            def pool_soft(g, nb):
                act.wait_ge(r_sub, g + 1)
                act.activation(pw[:, 0:nb, :], pw[:, 0:nb, :], ACT.Exp).then_inc(r_exp, 1)

            def gate_soft(g, nb):
                act.wait_ge(r_gsub, g + 1)
                act.activation(gl[0:nb, 1, :], gl[0:nb, 0, :], ACT.Exp).then_inc(r_gexp, 1)

            def spread_gates(g, nb):
                act.wait_ge(r_gb_ps, g + 1)
                copy(gb[:, 0:nb, :].rearrange("p b e -> p (b e)"), G[0][:, 320:320 + nb * E]).then_inc(r_gb, 1)

            def experts(g, nb, lo, hi):
                n = nb * N
                for i, (what, e, half) in uses_between(lo, hi):
                    act.wait_ge(x_ps, g * USES + (i + 1))
                    if what == "hidden":
                        for m in range(2):
                            k = 2 * half + m
                            ins = act.activation(ht[:, e % 2, k, 0:n], X[i % 2][:, m * n:m * n + n], ACT.Gelu,
                                                 bias=b1_s[:, e, k:k + 1])
                    else:
                        if not (first(g) and e < EO):
                            act.wait_ge(m_acc, g * E + (e - EO + 1))
                        ins = act.activation(eo[:, e % EO, 0:nb, :].rearrange("p b n -> p (b n)"), X[i % 2][:, 0:n],
                                             ACT.Gelu, bias=b2_s[:, e:e + 1])
                    ins.then_inc(x_out, 1)

            act.wait_ge(consts, NCONST)
            a_rows(0, NB)
            for c in range(4):
                act.wait_ge(setup_ps, c + 1)
                copy(ck[:, c * 512:c * 512 + 512], (G + X)[c][:, :]).then_inc(setup_ck, 1)
            a_gram_of(0, NB)
            a_kv_of(0, NB)
            act.wait_ge(packed, 64)
            t_turn(0, 0, 128)
            t_scores(0, 128)
            t_keep(0, 0, 128)
            t_soft(0, 128)

            def step(s, nxt, cur, att, moe):
                t0 = s * 2
                rows = 128 if cur == NB else N
                rows_next = 128 if nxt == NB else N
                if cur:
                    unit_tanh(t0, 0, rows)
                    unit_scale(t0, 0, rows)
                if moe:
                    spread_gates(s - 2, moe)
                if cur == NB:
                    t_turn(t0 + 1, 1, 128)
                    t_scores(t0 + 1, 128)
                    t_keep(t0 + 1, 1, 128)
                if cur:
                    unit_tanh(t0, 1, rows)
                if moe:
                    experts(s - 2, moe, 1, 3)
                if cur:
                    unit_scale(t0, 1, rows)
                if cur == NB:
                    t_soft(t0 + 1, 128)
                if nxt:
                    a_rows(s + 1, nxt)
                if cur:
                    unit_tanh(t0, 2, rows)
                if moe:
                    experts(s - 2, moe, 3, 4)
                if cur:
                    unit_scale(t0, 2, rows)
                if att:
                    l_turn(s - 1, att)
                if moe:
                    experts(s - 2, moe, 4, 5)
                if nxt:
                    a_gram_of(s + 1, nxt)
                if cur:
                    unit_tanh(t0, 3, rows)
                if att:
                    l_keys(s - 1, att, 0)
                if nxt:
                    a_kv_of(s + 1, nxt)
                if att:
                    l_queries(s - 1, att)
                    l_keys(s - 1, att, 1)
                if cur == NB:
                    unit_tanh(t0 + 1, 0, 128)
                if att:
                    l_values(s - 1, att)
                if cur:
                    unit_scale(t0, 3, rows)
                if nxt:
                    t_turn(t0 + 2, 0, rows_next)
                    t_scores(t0 + 2, rows_next)
                if cur == NB:
                    unit_tanh(t0 + 1, 1, 128)
                    unit_scale(t0 + 1, 0, 128)
                if moe:
                    experts(s - 2, moe, 5, 6)
                if moe:
                    experts(s - 2, moe, 6, 7)
                if att:
                    l_out(s - 1, att)
                if nxt:
                    t_keep(t0 + 2, 0, rows_next)
                if cur == NB:
                    unit_scale(t0 + 1, 1, 128)
                if cur == NB:
                    unit_tanh(t0 + 1, 2, 128)
                if moe:
                    experts(s - 2, moe, 7, E)
                if nxt:
                    t_soft(t0 + 2, rows_next)
                if cur == NB:
                    unit_scale(t0 + 1, 2, 128)
                if att:
                    l_turn_out(s - 1, att)
                    l_residual(s - 1, att)
                if cur == NB:
                    unit_tanh(t0 + 1, 3, 128)
                if att:
                    pool_soft(s - 1, att)
                if cur == NB:
                    unit_scale(t0 + 1, 3, 128)
                if att:
                    gate_soft(s - 1, att)
                    experts(s - 1, att, 0, 1)

            run_steps(act, step)

        A_STEPS, T_STEPS, U_STEPS, L_STEPS, R_STEPS = 18, 76, 7, 55, 13

        @block.vector
        def _(dve):
            tt, ts, stt = dve.tensor_tensor, dve.tensor_scalar, dve.scalar_tensor_tensor

            def rsqrt(sets):
                sets = [(ch, mv, w[:, 0, 0:nb], w[:, 1, 0:nb], w[:, 2, 0:nb], w[:, 3, 0:nb].bitcast(U32))
                        for ch, mv, w, nb in sets]
                for ch, mv, v, y, a, bits in sets:
                    ch.wait()
                    ch.did(ts(v, mv, LN_EPS, None, ALU.add))
                for ch, mv, v, y, a, bits in sets:
                    ch.wait()
                    ch.did(ts(bits, v.bitcast(U32), 1, None, ALU.logical_shift_right))
                for ch, mv, v, y, a, bits in sets:
                    ch.wait()
                    ch.did(ts(y.bitcast(I32), bits.bitcast(I32), -1.0, float(MAGIC), ALU.mult, ALU.add))
                for _ in range(NEWTON):
                    for ch, mv, v, y, a, bits in sets:
                        ch.wait()
                        ch.did(tt(a, y, y, ALU.mult))
                    for ch, mv, v, y, a, bits in sets:
                        ch.wait()
                        ch.did(stt(a, a, -0.5, v, ALU.mult, ALU.mult))
                    for ch, mv, v, y, a, bits in sets:
                        ch.wait()
                        ch.did(stt(y, a, 1.5, y, ALU.add, ALU.mult))

            def normalise(sets):
                for ch, src, dst, st, mv, w, nb, done in sets:
                    for b in range(nb):
                        ch.did(dve.bn_stats(st[:, b, :], src[:, b, :]))
                for ch, src, dst, st, mv, w, nb, done in sets:
                    ch.wait()
                dve.sem_inc(carried)
                for ch, src, dst, st, mv, w, nb, done in sets:
                    for b in range(nb):
                        ch.did(dve.bn_aggr(mv[:, b, :], st[:, b, :]))
                rsqrt([(ch, mv[:, 0:nb, 1], w, nb) for ch, src, dst, st, mv, w, nb, done in sets])
                for ch, src, dst, st, mv, w, nb, done in sets:
                    ch.wait()
                    for b in range(nb):
                        ins = ts(dst[:, b, :], src[:, b, :], mv[:, b, 0:1], w[:, 1, b:b + 1], ALU.subtract, ALU.mult)
                    ins.then_inc(done, 1)

            def rsqrt_rows(ch, mv, w):
                v, y, a, h = w[:, 0, :], w[:, 1, :], w[:, 2, :], w[:, 4, :]
                bits = w[:, 3, :].bitcast(U32)
                ch.did(ts(v, mv, LN_EPS, None, ALU.add))
                ch.did(ts(h, mv, LN_EPS, -0.5, ALU.add, ALU.mult))
                ch.wait(1)
                ch.did(ts(bits, v.bitcast(U32), 1, None, ALU.logical_shift_right))
                ch.wait()
                ch.did(ts(y.bitcast(I32), bits.bitcast(I32), -1.0, float(MAGIC), ALU.mult, ALU.add))
                for _ in range(NEWTON):
                    ch.wait()
                    ch.did(stt(a, y, h, y, ALU.mult, ALU.mult))
                    ch.wait()
                    ch.did(stt(y, a, 1.5, y, ALU.add, ALU.mult))
                ch.wait()

            def a_rows(g, nb):
                dve.wait_ge(a_h0, g + 1)
                return Chain(dve, a_dve, g, A_STEPS), h0, z0, st0, mv0, nw0, nb, a_z0

            def l_rows(g, nb):
                dve.wait_ge(unpacked, g * 64 + (64 if nb == NB else 16))
                return Chain(dve, l_dve, g, L_STEPS), h2, z2, st2, mv2, nw2, nb, l_z2

            def a_add(g, nb):
                dve.wait_ge(a_out_ps, g + 1)
                if not first(g):
                    dve.wait_ge(packed, g * 64)
                tt(h1[:, 0:nb, :].rearrange("p b d -> p (b d)"), S[1][0:N, 0:nb * D],
                   h0[:, 0:nb, :].rearrange("p b d -> p (b d)"), ALU.add).then_inc(a_h1, 1)

            def t_normalise(t, g, j, rows, nb=NB):
                r = slice(0, rows)
                ch = Chain(dve, t_dve, t, T_STEPS)
                dve.wait_ge(packed, g * 64 + (64 if nb == NB else 16))
                ch.did(dve.bn_stats(st1[r], h1p[r, j, :]))
                ch.wait()
                dve.sem_inc(carried)
                ch.did(dve.bn_aggr(mv1[r], st1[r]))
                ch.wait()
                rsqrt_rows(ch, mv1[r, 1:2], nw1[r])
                if not first(t):
                    dve.wait_ge(t_qt_ps, t)
                    dve.wait_ge(t_qrep, t)
                ts(q_s[r], h1p[r, j, :], mv1[r, 0:1], nw1[r, 1, 0:1], ALU.subtract, ALU.mult).then_inc(t_q, 1)
                return ch

            def t_best(t, rows, ch, lo, hi):
                r = slice(0, rows)
                for c in range(lo, hi):
                    dve.wait_ge(t_sc, t * 4 + (c + 1))
                    dve.sem_inc(carried)
                    for i in range(4 * c, 4 * c + 4):
                        ch.did(dve.max(s8[r, i, :], sc[r, i, :]))
                    if c > lo:
                        ch.wait(4)
                        dve.sem_inc(carried)
                        for i in range(4 * c - 4, 4 * c):
                            dve.max_index(i8[r, i, :], s8[r, i, :], sc[r, i, :]).then_inc(t_dve, 1)
                            ch.n += 1
                ch.wait()
                dve.sem_inc(carried)
                for i in range(4 * hi - 4, 4 * hi):
                    ch.did(dve.max_index(i8[r, i, :], s8[r, i, :], sc[r, i, :]))

            def t_pairs(t, rows, ch):
                r = slice(0, rows)
                ch.wait()
                shape = [rows, HEADS, TOPK, TOPK]
                ch.did(tt(pair[r], s8[r, 0:HEADS, :].unsqueeze(3).to_broadcast(shape),
                          s8[r, HEADS:2 * HEADS, :].unsqueeze(2).to_broadcast(shape), ALU.add))
                ch.wait(1)
                ch.did(dve.tensor_copy(i8f[r], i8[r]))
                ch.wait(1)
                dve.sem_inc(carried)
                for h in range(HEADS):
                    ch.did(dve.max(best[r, h, :], pair[r, h, :, :].rearrange("p a b -> p (a b)")))
                ch.wait()
                dve.sem_inc(carried)
                for h in range(HEADS):
                    ch.did(dve.max_index(pos[r, h, :], best[r, h, :], pair[r, h, :, :].rearrange("p a b -> p (a b)")))
                tt(es[r], best[r], best[r, :, 0:1].to_broadcast([rows, HEADS, TOPK]), ALU.subtract).then_inc(t_es, 1)
                return ch

            def t_decode(t, j, rows, ch):
                r = slice(0, rows)
                ch.wait()
                flat = pos[r].rearrange("p h k -> p (h k)")
                ch.did(ts(ab[r, 0, :], flat, 3, None, ALU.logical_shift_right))
                ch.did(ts(ab[r, 1, :], flat, 7, None, ALU.bitwise_and))
                ch.wait()
                hits = hit[r].rearrange("p i k a -> p (i k) a")
                for a in range(TOPK):
                    ch.did(stt(hit[r, :, :, a], ab[r].rearrange("p i (h k) -> p (i h) k", h=HEADS), float(a),
                               i8f[r, :, a].unsqueeze(2).to_broadcast([rows, 2 * HEADS, TOPK]), ALU.is_equal, ALU.mult))
                ch.wait()
                ch.did(dve.tensor_reduce(iab[r].rearrange("p i k -> p (i k)"), hits, AX.X, ALU.add))
                ch.wait()
                stt(idx[r, j, :], iab[r, 0, :], float(EXP), iab[r, 1, :], ALU.mult, ALU.add).then_inc(t_idx, 1)

            def t_share(t, j, rows, ch):
                r = slice(0, rows)
                dve.wait_ge(t_ee, t + 1)
                ch.did(dve.tensor_reduce(den[r, 0, :], es[r], AX.X, ALU.add))
                ch.wait()
                ch.did(dve.reciprocal(den[r, 1, :], den[r, 0, :]))
                ch.wait()
                ch.did(stt(smh[r, j, :].rearrange("p (h k) -> p h k", h=HEADS), es[r], 0.5,
                           den[r, 1, :].unsqueeze(2).to_broadcast([rows, HEADS, TOPK]), ALU.mult, ALU.mult))
                ch.wait()
                ch.end()

            def unit_dots(t, j, u, rows, latest=None):
                r = slice(0, rows)
                ch = Chain(dve, u_dve, t * UNITS + u, U_STEPS)
                dve.wait_ge(gathered[u], t * (UR * 16) + UR * 16)
                if latest is not None:
                    dve.wait_ge(t_qrep, latest + 1)
                half = UR // 2
                for i in range(2):
                    w = ring[r, u, i * half:i * half + half, 0:D]
                    ch.did(tt(w, w, qrep[r, j, :].unsqueeze(1).to_broadcast([rows, half, D]), ALU.mult))
                for i in range(2):
                    ch.wait(1)
                    ch.did(dve.tensor_reduce(xu[r, 0, i * half:i * half + half], ring[r, u, i * half:i * half + half, 0:D],
                                             AX.X, ALU.add))
                ch.wait()
                ch.did(tt(xu[r, 1, :], xu[r, 0, :], xu[r, 0, :], ALU.mult))
                ch.wait()
                ch.did(ts(xu[r, 1, :], xu[r, 1, :], 0.044715, 1.0, ALU.mult, ALU.add))
                ch.wait()
                tt(xu[r, 2, :], xu[r, 1, :], xu[r, 0, :], ALU.mult).then_inc(u_arg, 1)
                ch.did(tt(xu[r, 3, :], xu[r, 0, :], smh[r, j, u * UR:u * UR + UR], ALU.mult))
                return ch

            def unit_share(t, u, rows, ch):
                r = slice(0, rows)
                dve.wait_ge(u_th, t * UNITS + (u + 1))
                ch.wait()
                stt(vu[r, u, :], th[r], 1.0, xu[r, 3, :], ALU.add, ALU.mult).then_inc(u_v, 1)
                ch.end()

            def end_tile(t, j, rows):
                r = slice(0, rows)
                dve.wait_ge(u_sum, t * UNITS + UNITS)
                dve.tensor_reduce(usum[r], U[r].rearrange("p (k d) -> p d k", k=4), AX.X, ALU.add).then_inc(t_red, 1)
                if not isinstance(t, int) or t >= 2:
                    dve.wait_ge(unpacked, (t - j) * 32 - (32 if j == 0 else 0))
                dve.wait_ge(t_kept, t + 1)
                dve.wait_ge(t_red, t + 1)
                tt(h2p[r, j, :], usum[r], hres[r, j, :], ALU.add).then_inc(t_h2, 1)

            def l_queries(g, nb, ch, bs):
                for b in bs:
                    if b >= nb:
                        continue
                    dve.wait_ge(l_q_ps, g * NB + (b + 1))
                    q = G[(b + 1) % 2][0:N, :].rearrange("p (h d) -> p h d", h=LH)
                    ch.did(dve.tensor_reduce(mx[:, b, :], q, AX.X, ALU.max))
                    ch.wait()
                    tt(qe[:, b, :, :], q, mx[:, b, :].unsqueeze(2).to_broadcast([N, LH, LD]), ALU.subtract).then_inc(l_qs, 1)

            def l_bounds(g, nb, ch):
                dve.wait_ge(l_s_ps, g * (2 * NB) + 1)
                ch.did(ts(dn[:, 0:nb, 0, :], G[0][0:N, QSUM:QSUM + nb * LH].rearrange("p (b h) -> p b h", b=nb),
                          CLIP * float(LD) ** 0.5, None, ALU.mult))

            def l_mask(g, b):
                for odd in range(2):
                    dve.wait_ge(l_s_ps, g * (2 * NB) + (2 * b + 1 + odd))
                    tt(sm[:, odd, :, :], G[odd][0:N, 0:HB * N].rearrange("p (m n) -> p m n", m=HB),
                       causal[:].unsqueeze(1).to_broadcast([N, HB, N]), ALU.mult).then_inc(l_s, 1)

            def l_divide(g, b, ch):
                a = [G[odd][0:N, 0:HB * (LD + 1)].rearrange("p (m d) -> p m d", m=HB) for odd in range(2)]

                def heads(x, odd):
                    return x.rearrange("p (m o) -> p o m", o=2)[:, odd, :]

                ch.wait()
                for odd in range(2):
                    dve.wait_ge(l_a_ps, g * (2 * NB) + (2 * b + 1 + odd))
                    ch.did(tt(heads(dn[:, b, 1, :], odd), a[odd][:, :, LD], heads(dn[:, b, 0, :], odd), ALU.max))
                ch.wait()
                ch.did(dve.reciprocal(dn[:, b, 2, :], dn[:, b, 1, :]))
                ch.wait()
                for odd in range(2):
                    tt(at_s[:, b, :, :].rearrange("p (m o) d -> p o m d", o=2)[:, odd, :, :], a[odd][:, :, 0:LD],
                       heads(dn[:, b, 2, :], odd).unsqueeze(2).to_broadcast([N, HB, LD]), ALU.mult).then_inc(l_a, 1)

            def l_add(g, nb, ch):
                dve.wait_ge(l_o_ps, g + 1)
                tt(h3[:, 0:nb, :].rearrange("p b d -> p (b d)"), G[1][0:N, 0:nb * D],
                   h2[:, 0:nb, :].rearrange("p b d -> p (b d)"), ALU.add).then_inc(l_h3, 1)
                dve.wait_ge(l_h3, g + 1)
                normalise([(ch, h3, z3, st2, mv2, nw2, nb, l_z3)])

            def pool_scores(g, nb, ch):
                dve.wait_ge(r_sc_ps, g + 1)
                s = pw[:, 0:nb, :]
                ch.did(ts(s, G[0][0:1, 0:nb * N].rearrange("p (b n) -> p b n", b=nb), pool_bs[:], None, ALU.add))
                ch.wait()
                ch.did(dve.tensor_reduce(pmx[:, 0, 0:nb], s, AX.X, ALU.max))
                ch.wait()
                tt(s, s, pmx[:, 0, 0:nb].unsqueeze(2).to_broadcast([1, nb, N]), ALU.subtract).then_inc(r_sub, 1)

            def pool_rows(g, nb, ch):
                s = pw[:, 0:nb, :]
                dve.wait_ge(r_exp, g + 1)
                ch.did(dve.tensor_reduce(pmx[:, 0, 0:nb], s, AX.X, ALU.add))
                ch.wait()
                ch.did(dve.reciprocal(pmx[:, 1, 0:nb], pmx[:, 0, 0:nb]))
                ch.wait()
                tt(s, s, pmx[:, 1, 0:nb].unsqueeze(2).to_broadcast([1, nb, N]), ALU.mult).then_inc(r_aw, 1)
                dve.wait_ge(r_aw_ps, g + 1)
                ch.did(tt(pz[:, 0:nb, :], z3t[:, 0:nb, :], G[1][:, 0:nb * N].rearrange("p (b n) -> p b n", b=nb), ALU.mult))
                ch.wait()
                dve.tensor_reduce(pooled[:, 0:nb], pz[:, 0:nb, :], AX.X, ALU.add).then_inc(r_pool, 1)
                p = slice(0, nb)
                dve.wait_ge(r_gate_ps, g + 1)
                lg = G[0][p, 256:256 + E]
                ch.did(dve.tensor_reduce(g1[p, 0:1], lg, AX.X, ALU.max))
                ch.wait()
                ts(gl[p, 0, :], lg, g1[p, 0:1], None, ALU.subtract).then_inc(r_gsub, 1)
                ch.end(nb == NB)

            def gates(g, nb):
                ch = Chain(dve, r_dve, g, R_STEPS)
                p = slice(0, nb)
                dve.wait_ge(r_gexp, g + 1)
                ch.did(dve.tensor_reduce(g1[p, 1:2], gl[p, 1, :], AX.X, ALU.add))
                ch.wait()
                ch.did(dve.reciprocal(g1[p, 2:3], g1[p, 1:2]))
                ch.wait()
                ch.did(ts(gl[p, 2, :], gl[p, 1, :], g1[p, 2:3], None, ALU.mult))
                ch.wait()
                dve.sem_inc(carried)
                ch.did(dve.max(gl[p, 3, :], gl[p, 2, :]))
                ch.wait()
                dve.sem_inc(carried)
                ch.did(dve.max_index(gi[p, :], gl[p, 3, :], gl[p, 2, :]))
                ch.wait()
                ch.did(dve.tensor_copy(gl[p, 3, :], gi[p, :]))
                ch.wait()
                ch.did(ts(gl[p, 4, :], iota8[p, :], gl[p, 3, 0:1], None, ALU.is_equal))
                ch.wait()
                ch.did(stt(gl[p, 5, :], iota8[p, :], gl[p, 3, 1:2], gl[p, 4, :], ALU.is_equal, ALU.add))
                ch.wait()
                ch.did(tt(gl[p, 4, :], gl[p, 5, :], gl[p, 2, :], ALU.mult))
                ch.wait()
                ch.did(dve.tensor_reduce(g1[p, 1:2], gl[p, 4, :], AX.X, ALU.add))
                ch.wait()
                ch.did(ts(g1[p, 3:4], g1[p, 1:2], DEN_EPS, None, ALU.add))
                ch.wait()
                ch.did(dve.reciprocal(g1[p, 2:3], g1[p, 3:4]))
                ch.wait()
                ch.did(ts(gl[p, 5, :], gl[p, 4, :], g1[p, 2:3], None, ALU.mult))
                ch.wait()
                tt(gd[p, 0:nb, :], own_batch[p, 0:nb, :], gl[p, 5, :].unsqueeze(1).to_broadcast([nb, nb, E]), ALU.mult)\
                    .then_inc(r_gd, 1)
                ch.end(nb == NB)

            def experts(g, nb, lo, hi):
                if lo == 0:
                    dve.wait_ge(r_gb, g + 1)
                    dve.wait_ge(l_h3t, g + 1)
                for i, (what, e, _) in uses_between(lo, hi):
                    if what == "hidden":
                        continue
                    dve.wait_ge(x_out, g * USES + (i + 1))
                    if e > 0:
                        dve.wait_ge(m_acc, g * E + e)
                    elif not first(g):
                        dve.wait_ge(stored, g * 16)
                    before = acc if e else h3t
                    for b in range(nb):
                        ins = stt(acc[:, b, :], eo[:, e % EO, b, :], gb[:, b, e:e + 1], before[:, b, :], ALU.mult, ALU.add)
                    ins.then_inc(m_acc, 1)

            dve.memset(cb3[:], 0.0).then_inc(setup_cb, 1)
            dve.wait_ge(consts, NCONST)
            normalise([a_rows(0, NB)])
            for c in range(4):
                dve.wait_ge(setup_ps, 5 + c)
                dve.tensor_copy(cb[:, c * 512:c * 512 + 512], (G + X)[c][0:1, :]).then_inc(setup_dve, 1)
            dve.wait_ge(setup_dve, 4)
            dve.wait_ge(setup_cb, 1)
            dve.tensor_copy(cb3[0:1, :], cb).then_inc(setup_dve, 1)
            dve.wait_ge(setup_dve, 5)
            tt(cbr, cb, cb3[0:1, :], ALU.subtract).then_inc(setup_dve, 1)
            a_add(0, NB)
            dve.wait_ge(setup_dve, 6)
            dve.tensor_copy(cbp[:, 0, :], cbr).then_inc(setup_dve, 1)
            dve.wait_ge(setup_dve, 7)
            tt(cb, cbr, cbp[:, 0, :], ALU.subtract).then_inc(setup_dve, 1)
            dve.wait_ge(setup_dve, 8)
            dve.tensor_copy(cbp[:, 1, :], cb).then_inc(setup_cb, 1)
            ch = t_normalise(0, 0, 0, 128)
            t_best(0, 128, ch, 0, 4)
            t_pairs(0, 128, ch)
            t_decode(0, 0, 128, ch)
            t_share(0, 0, 128, ch)

            def step(s, nxt, cur, att, moe):
                t0 = s * 2
                rows = 128 if cur == NB else N
                rows_next = 128 if nxt == NB else N
                if cur:
                    uc = unit_dots(t0, 0, 0, rows)
                if moe:
                    gates(s - 2, moe)
                if cur:
                    unit_share(t0, 0, rows, uc)
                if att == NB:
                    end_tile(t0 - 1, 1, 128)
                if cur == NB:
                    tc = t_normalise(t0 + 1, s, 1, 128)
                if cur:
                    uc = unit_dots(t0, 0, 1, rows, t0 + 1 if cur == NB else None)
                if cur == NB:
                    t_best(t0 + 1, 128, tc, 0, 2)
                if cur:
                    unit_share(t0, 1, rows, uc)
                if moe:
                    experts(s - 2, moe, 0, 2)
                if cur == NB:
                    t_best(t0 + 1, 128, tc, 2, 4)
                    t_pairs(t0 + 1, 128, tc)
                    t_decode(t0 + 1, 1, 128, tc)
                if cur:
                    uc = unit_dots(t0, 0, 2, rows)
                if cur == NB:
                    t_share(t0 + 1, 1, 128, tc)
                if cur:
                    unit_share(t0, 2, rows, uc)
                if att and isinstance(s, int) and s == 1:
                    dve.wait_ge(late_loaded, LATE - 16)
                sets = ([l_rows(s - 1, att)] if att else []) + ([a_rows(s + 1, nxt)] if nxt else [])
                if sets:
                    normalise(sets)
                    lc = sets[0][0]
                if moe:
                    experts(s - 2, moe, 2, 4)
                if att:
                    l_queries(s - 1, att, lc, (0, 1))
                if cur:
                    uc = unit_dots(t0, 0, 3, rows)
                if att:
                    l_queries(s - 1, att, lc, (2,))
                if cur:
                    unit_share(t0, 3, rows, uc)
                if cur == NB:
                    uc = unit_dots(t0 + 1, 1, 0, 128)
                if nxt:
                    a_add(s + 1, nxt)
                if moe:
                    experts(s - 2, moe, 4, 5)
                if cur == NB:
                    unit_share(t0 + 1, 0, 128, uc)
                if nxt:
                    tc = t_normalise(t0 + 2, s + 1, 0, rows_next, nxt)
                if att:
                    l_bounds(s - 1, att, lc)
                    l_mask(s - 1, 0)
                    l_divide(s - 1, 0, lc)
                if cur == NB:
                    uc = unit_dots(t0 + 1, 1, 1, 128, t0 + 2)
                if att == NB:
                    l_mask(s - 1, 1)
                if nxt:
                    t_best(t0 + 2, rows_next, tc, 0, 2)
                if att == NB:
                    l_divide(s - 1, 1, lc)
                if cur == NB:
                    unit_share(t0 + 1, 1, 128, uc)
                if cur:
                    end_tile(t0, 0, rows)
                if att == NB:
                    l_mask(s - 1, 2)
                if nxt:
                    t_best(t0 + 2, rows_next, tc, 2, 4)
                if att == NB:
                    l_divide(s - 1, 2, lc)
                if nxt:
                    t_pairs(t0 + 2, rows_next, tc)
                    t_decode(t0 + 2, 0, rows_next, tc)
                if cur == NB:
                    uc = unit_dots(t0 + 1, 1, 2, 128)
                if moe:
                    experts(s - 2, moe, 5, 7)
                if cur == NB:
                    unit_share(t0 + 1, 2, 128, uc)
                if att:
                    l_add(s - 1, att, lc)
                if nxt:
                    t_share(t0 + 2, 0, rows_next, tc)
                if cur == NB:
                    uc = unit_dots(t0 + 1, 1, 3, 128)
                if att:
                    pool_scores(s - 1, att, lc)
                if moe:
                    experts(s - 2, moe, 7, E)
                if cur == NB:
                    unit_share(t0 + 1, 3, 128, uc)
                if att:
                    pool_rows(s - 1, att, lc)

            run_steps(dve, step)


def kernel(**inputs):
    import numpy as _np
    import concourse.bacc as _bacc
    from concourse import mybir as _mybir
    from concourse.bass_utils import run_bass_kernel_spmd as _run

    a = {k: _np.asarray(v) for k, v in inputs.items()}
    x = a["x"][:, :CTX * N, :].reshape(B, N, 2, KIN).transpose(0, 3, 2, 1)
    full = x[:GROUPS * NB].reshape(GROUPS, NB, KIN, 2, N).transpose(0, 2, 3, 1, 4)
    keys = a["L0_ffn_keys"].transpose(1, 3, 0, 2)
    data = {
        "xg": full.reshape(GROUPS * KIN, 2 * GT),
        "xl": x[GROUPS * NB:].transpose(1, 2, 0, 3).reshape(KIN, 2 * LAST * N),
        "tok_w": a["L0_tok_weight"].T.reshape(2, KIN, D).transpose(1, 0, 2),
        "tok_b": a["L0_tok_bias"],
        "wv_t": a["L0_attn_W_v"].T,
        "wth_t": a["L0_attn_W_theta"].T,
        "pq_w": a["L0_ffn_Wq"].reshape(HEADS, 128, D).transpose(1, 0, 2).reshape(128, HEADS * D),
        "pq_b": a["L0_ffn_bq"].reshape(HEADS, 128).T,
        "pkeys": keys.reshape(128, HEADS * EXP),
        "table": _np.concatenate([a["L0_ffn_w_down_embed"], a["L0_ffn_w_up_embed"]], axis=1),
        "aq": a["L1_attn_Wq"],
        "ak": a["L1_attn_Wk"],
        "av": a["L1_attn_Wv"],
        "ao": a["L1_attn_Wo"].reshape(HB, D, D).transpose(1, 0, 2).reshape(D, HB * D),
        "abo": a["L1_attn_bo"].reshape(1, D),
        "pool_w": a["L1_ffn_attn_w"],
        "pool_b": a["L1_ffn_attn_b"].reshape(1, 1),
        "gate_w": a["L1_ffn_gate_w"],
        "gate_b": a["L1_ffn_gate_b"].reshape(1, E),
        "w1": a["L1_ffn_w1"].transpose(1, 0, 2).reshape(D, E * HID),
        "b1": a["L1_ffn_b1"].reshape(E, HB, D).transpose(2, 0, 1).reshape(D, E * HB),
        "w2": a["L1_ffn_w2"].reshape(E, HB, D, D).transpose(2, 0, 1, 3).reshape(D, E * HB * D),
        "b2": a["L1_ffn_b2"].T,
    }
    nc = _bacc.Bacc("TRN2", target_bir_lowering=False, num_devices=1)
    arrays, args = {}, []
    for name, v in data.items():
        v = _np.ascontiguousarray(v)
        arrays[f"in_{name}_dram"] = v
        args.append(nc.dram_tensor(f"in_{name}_dram", v.shape, _mybir.dt.from_np(v.dtype), kind="ExternalInput").ap())
    outs = []
    for i, shape in enumerate([(GROUPS * D, GT), (D, LAST * N)]):
        outs.append(nc.dram_tensor(f"out_{i}_dram", shape, F32, kind="ExternalOutput").ap())
    tower(nc, *args, *outs)
    r = _run(nc, [arrays], core_ids=[0])
    main = _np.asarray(r.results[0]["out_0_dram"]).reshape(GROUPS, D, NB, N).transpose(0, 2, 3, 1).reshape(GROUPS * NB, N, D)
    last = _np.asarray(r.results[0]["out_1_dram"]).reshape(D, LAST, N).transpose(1, 2, 0)
    return _np.ascontiguousarray(_np.concatenate([main, last], axis=0))
```

```python
from contextlib import ExitStack

import concourse.bass as bass
from concourse import mybir

F32 = mybir.dt.float32
BF16 = mybir.dt.bfloat16
I32 = mybir.dt.int32
U32 = mybir.dt.uint32
ALU = mybir.AluOpType
ACT = mybir.ActivationFunctionType
AX = mybir.AxisListType

B, FRAMES, FEAT = 64, 256, 64
CTX = 3
N = 85
D = 128
KIN = CTX * FEAT // 2
HEADS, EXP, TOPK = 8, 128, 8
ROW = 2 * D
LH, LD = 8, 64
E, HID = 8, 512
HB = HID // D
LN_EPS = 1e-5
CLIP = 1e-3
DEN_EPS = 1e-9

NB = 3
GROUPS = B // NB
REST = B - GROUPS * NB
GT = NB * N
UNITS = 4
UR = HEADS * TOPK // UNITS
QSUM = 384
MAGIC = 0x5F3759DF
NEWTON = 3
EO = 4
USES = 3 * E


def tower(nc, xg, xl, tok_w, tok_b, wv_t, wth_t, pq_w, pq_b, pkeys, table, aq, ak, av, ao, abo,
          pool_w, pool_b, gate_w, gate_b, w1, b1, w2, b2, out, out_last):
    ctx = ExitStack()
    with ctx:
        def sb(name, shape, dt=F32):
            return ctx.enter_context(nc.sbuf_tensor(name, shape, dt))

        def bank(name):
            return ctx.enter_context(nc.psum_tensor(name, [128, 512], F32))

        def sem(name):
            return ctx.enter_context(nc.semaphore(name))

        tok_ws = sb("tok_ws", [KIN, 2, D])
        tok_bs = sb("tok_bs", [1, D])
        wv_s = sb("wv_s", [D, D])
        wth_s = sb("wth_s", [D, D])
        ck = sb("ck", [D, 2 * HEADS * EXP])
        cb3 = sb("cb3", [D, 2 * HEADS * EXP], BF16)
        aq_s = sb("aq_s", [D, LH * LD])
        ak_s = sb("ak_s", [D, LH * LD])
        av_s = sb("av_s", [D, LH * LD])
        ao_s = sb("ao_s", [D, HB, D])
        abo_s = sb("abo_s", [1, D])
        pool_ws = sb("pool_ws", [D, 1])
        pool_bs = sb("pool_bs", [1, 1])
        gate_ws = sb("gate_ws", [D, E])
        gate_bs = sb("gate_bs", [1, E])
        w1_s = sb("w1_s", [D, E, HID])
        w2_s = sb("w2_s", [D, E, HB, D])
        b1_s = sb("b1_s", [D, E, HB])
        b2_s = sb("b2_s", [D, E])
        ident = sb("ident", [128, 128])
        ones = sb("ones", [128, 128])
        ones3 = sb("ones3", [128, 128], BF16)
        mean_col = sb("mean_col", [N, 1])
        causal = sb("causal", [N, N])
        iota8 = sb("iota8", [128, 8])
        halves = sb("halves", [D, 2])
        own_batch = sb("own_batch", [NB, NB, E])
        x_s = sb("x_s", [KIN, 2, GT])
        h0 = sb("h0", [N, NB, D])
        z0 = sb("z0", [N, NB, D])
        z0t = sb("z0t", [D, NB, N])
        gram = sb("gram", [D, NB, D])
        zmean = sb("zmean", [D, NB])
        gv = sb("gv", [D, NB, D])
        rmean = sb("rmean", [1, NB, D])
        kv = sb("kv", [D, NB, D])
        h1 = sb("h1", [N, NB, D])
        st0 = sb("st0", [N, NB, 6])
        mv0 = sb("mv0", [N, NB, 2])
        nw0 = sb("nw0", [N, 4, NB])
        h1p = sb("h1p", [128, 2, D])
        hres = sb("hres", [128, 2, D])
        q_s = sb("q_s", [128, D])
        qt_s = sb("qt_s", [D, 128])
        st1 = sb("st1", [128, 6])
        mv1 = sb("mv1", [128, 2])
        nw1 = sb("nw1", [128, 5, 1])
        sc = sb("sc", [128, 2 * HEADS, EXP])
        s8 = sb("s8", [128, 2 * HEADS, TOPK])
        i8 = sb("i8", [128, 2 * HEADS, TOPK], U32)
        i8f = sb("i8f", [128, 2 * HEADS, TOPK])
        pair = sb("pair", [128, HEADS, TOPK, TOPK])
        best = sb("best", [128, HEADS, TOPK])
        pos = sb("pos", [128, HEADS, TOPK], U32)
        ab = sb("ab", [128, 2, HEADS * TOPK], U32)
        hit = sb("hit", [128, 2 * HEADS, TOPK, TOPK])
        iab = sb("iab", [128, 2, HEADS * TOPK])
        idx = sb("idx", [128, 2, HEADS * TOPK], U32)
        es = sb("es", [128, HEADS, TOPK])
        den = sb("den", [128, 2, HEADS])
        smh = sb("smh", [128, 2, HEADS * TOPK])
        ring = sb("ring", [128, UNITS, UR, ROW])
        spare = ring[0:1, 2:4, :, :].rearrange("p u k d -> p (u k d)")
        cb = spare[:, 0:2048]
        cbr = spare[:, 2048:4096]
        cbp = spare[:, 4096:6144].bitcast(BF16).rearrange("p (a n) -> p a n", a=2)
        xu = sb("xu", [128, 4, UR])
        th = sb("th", [128, UR])
        vu = sb("vu", [128, UNITS, UR])
        usum = sb("usum", [128, D])
        h2p = sb("h2p", [128, 2, D])
        h2 = sb("h2", [N, NB, D])
        st2 = sb("st2", [N, NB, 6])
        mv2 = sb("mv2", [N, NB, 2])
        nw2 = sb("nw2", [N, 4, NB])
        z2 = sb("z2", [N, NB, D])
        z2t = sb("z2t", [D, GT])
        kt = sb("kt", [D, HB, GT])
        mx = sb("mx", [N, NB, LH])
        qe = sb("qe", [N, NB, LH, LD])
        vx = sb("vx", [N, NB, LH, LD + 1])
        qt = sb("qt", [D, NB, HB, N])
        sm = sb("sm", [N, 2, HB, N])
        dn = sb("dn", [N, NB, 3, LH])
        at_s = qe
        att = qt
        h3 = sb("h3", [N, NB, D])
        z3 = sb("z3", [N, NB, D])
        z3t = sb("z3t", [D, NB, N])
        pw = sb("pw", [1, NB, N])
        pmx = sb("pmx", [1, 2, NB])
        pz = sb("pz", [D, NB, N])
        pooled = sb("pooled", [D, NB])
        gl = sb("gl", [NB, 6, E])
        g1 = sb("g1", [NB, 4])
        gi = sb("gi", [NB, E], U32)
        gd = sb("gd", [NB, NB, E])
        gb = sb("gb", [D, NB, E])
        ht = sb("ht", [D, 2, HB, GT])
        eo = sb("eo", [D, EO, NB, N])
        h3t = sb("h3t", [D, NB, N])
        acc = sb("acc", [D, NB, N])

        S = [bank("bank_s0"), bank("bank_s1")]
        U = bank("bank_u")
        Q = bank("bank_q")
        G = [bank("bank_l0"), bank("bank_l1")]
        X = [bank("bank_x0"), bank("bank_x1")]
        qrep = Q[:, 0:2 * D].rearrange("p (j d) -> p j d", j=2)
        qtp = S[0][:, 0:128]

        tokens_loaded = sem("tokens_loaded")
        loaded = sem("loaded")
        late_loaded = sem("late_loaded")
        split_moved = sem("split_moved")
        consts = sem("consts")
        pool_order = sem("pool_order")
        setup_ps = sem("setup_ps")
        setup_ck = sem("setup_ck")
        setup_cb = sem("setup_cb")
        setup_dve = sem("setup_dve")
        x_in = sem("x_in")
        a_tok = sem("a_tok")
        a_h0 = sem("a_h0")
        a_dve = sem("a_dve")
        a_z0 = sem("a_z0")
        a_gram_ps = sem("a_gram_ps")
        a_gram = sem("a_gram")
        a_gv_ps = sem("a_gv_ps")
        a_gv = sem("a_gv")
        a_kv_ps = sem("a_kv_ps")
        a_kv = sem("a_kv")
        a_out_ps = sem("a_out_ps")
        a_h1 = sem("a_h1")
        packed = sem("packed")
        t_dve = sem("t_dve")
        t_q = sem("t_q")
        t_qt_ps = sem("t_qt_ps")
        t_qt = sem("t_qt")
        t_qrep = sem("t_qrep")
        t_kept = sem("t_kept")
        t_sc_ps = sem("t_sc_ps")
        t_sc = sem("t_sc")
        t_idx = sem("t_idx")
        t_es = sem("t_es")
        t_ee = sem("t_ee")
        gathered = [sem(f"gathered{u}") for u in range(UNITS)]
        u_dve = sem("u_dve")
        u_arg = sem("u_arg")
        u_th = sem("u_th")
        u_v = sem("u_v")
        u_up = sem("u_up")
        u_sum = sem("u_sum")
        t_red = sem("t_red")
        t_h2 = sem("t_h2")
        unpacked = sem("unpacked")
        l_dve = sem("l_dve")
        l_z2 = sem("l_z2")
        l_z2t_ps = sem("l_z2t_ps")
        l_z2t = sem("l_z2t")
        l_q_ps = sem("l_q_ps")
        l_qs = sem("l_qs")
        l_qe = sem("l_qe")
        l_k_ps = sem("l_k_ps")
        l_k = sem("l_k")
        l_v_ps = sem("l_v_ps")
        l_v = sem("l_v")
        l_qt_ps = sem("l_qt_ps")
        l_qt = sem("l_qt")
        l_s_ps = sem("l_s_ps")
        l_s = sem("l_s")
        l_a_ps = sem("l_a_ps")
        l_a = sem("l_a")
        l_at_ps = sem("l_at_ps")
        l_at = sem("l_at")
        l_o_ps = sem("l_o_ps")
        l_h3 = sem("l_h3")
        l_z3 = sem("l_z3")
        l_z3t_ps = sem("l_z3t_ps")
        l_z3t = sem("l_z3t")
        l_h3t = sem("l_h3t")
        r_sc_ps = sem("r_sc_ps")
        r_sub = sem("r_sub")
        r_exp = sem("r_exp")
        r_aw = sem("r_aw")
        r_aw_ps = sem("r_aw_ps")
        r_pool = sem("r_pool")
        r_gate_ps = sem("r_gate_ps")
        r_gsub = sem("r_gsub")
        r_gexp = sem("r_gexp")
        r_dve = sem("r_dve")
        r_gd = sem("r_gd")
        r_gb_ps = sem("r_gb_ps")
        r_gb = sem("r_gb")
        x_ps = sem("x_ps")
        x_out = sem("x_out")
        m_acc = sem("m_acc")
        stored = sem("stored")

        carried = sem("carried")
        EARLY = 5 * 16
        LATE = 13 * 16
        NCONST = 11

        def expert_uses():
            uses = []
            for e in range(E):
                uses += [("hidden", e, 0)] + ([("out", e - 1, 0)] if e else []) + [("hidden", e, 1)]
            return uses + [("out", E - 1, 0)]

        uses = expert_uses()
        assert len(uses) == USES
        place = {use: i for i, use in enumerate(uses)}

        def uses_between(lo, hi):
            return list(enumerate(uses))[place["hidden", lo, 0]:place["hidden", hi, 0] if hi < E else USES]

        def first(v):
            return isinstance(v, int) and v <= 0

        def batches(g):
            return 0 if first(g) else g * NB - (NB - REST)

        def moves(g):
            return 0 if first(g) else g * 64 - 48

        class Chain:

            def __init__(self, eng, s, turn, per, short=None):
                short = per if short is None else short
                self.eng, self.s, self.n = eng, s, 0
                self.per = short if first(turn) else per
                self.base = 0 if first(turn) else turn * per - (per - short)

            def did(self, ins):
                ins.then_inc(self.s, 1)
                self.n += 1

            def wait(self, back=0):
                self.eng.wait_ge(self.s, self.base + (self.n - back))

            def end(self):
                assert self.n == self.per, (self.s, self.n, self.per)

        def run_steps(eng, step):
            def nb(g):
                return REST if g == 0 else NB if 0 < g <= GROUPS else 0

            for s in range(3):
                step(s, nb(s + 1), nb(s), nb(s - 1), nb(s - 2))
            with eng.Fori(3, GROUPS) as s:
                step(s, NB, NB, NB, NB)
            for s in range(GROUPS, GROUPS + 3):
                step(s, nb(s + 1), nb(s), nb(s - 1), nb(s - 2))

        block = ctx.enter_context(nc.Block())

        @block.sync
        def _(sp):
            def load_x(g, nb):
                if nb == NB:
                    sp.dma_start(x_s[:].rearrange("p c n -> p (c n)"), xg[bass.ds((g - 1) * KIN, KIN), :]).then_inc(x_in, 16)
                else:
                    sp.dma_start(x_s[:, :, 0:nb * N], xl.rearrange("p (c n) -> p c n", c=2)).then_inc(x_in, 16)

            def pack(g, nb):
                sp.wait_ge(a_h1, g + 1)
                sp.sem_inc(carried)
                if not first(g):
                    sp.wait_ge(t_kept, g * 2 - 1)
                    sp.sem_inc(carried)
                pieces = [(0, 0, N, 1, 0)]
                if nb == NB:
                    a = 128 - N
                    pieces = [(0, 0, N, 0, 0), (1, 0, a, 0, N), (1, a, N - a, 1, 0), (2, 0, N, 1, N - a)]
                for b, r, n, j, p in pieces:
                    sp.dma_start(h1p[p:p + n, j, :], h1[r:r + n, b, :]).then_inc(packed, 16)

            def unpack(g, j, nb):
                sp.wait_ge(t_h2, 2 * g + j)
                a = 128 - N
                if nb == REST:
                    pieces = [(0, 0, N, 0)]
                elif j == 0:
                    pieces = [(0, 0, N, 0), (1, 0, a, N)]
                else:
                    pieces = [(1, a, N - a, 0), (2, 0, N, N - a)]
                for b, r, n, p in pieces:
                    sp.dma_start(h2[r:r + n, b, :], h2p[p:p + n, j, :]).then_inc(unpacked, 16)

            def store(g, nb):
                sp.wait_ge(m_acc, g * E + E)
                sp.sem_inc(carried)
                if nb == NB:
                    sp.dma_start(out[bass.ds((g - 1) * D, D), :], acc[:].rearrange("p b n -> p (b n)")).then_inc(stored, 16)
                else:
                    sp.dma_start(out_last, acc[:, 0, :]).then_inc(stored, 16)

            load_x(0, REST)
            for dst, src in ((tok_ws[:], tok_w), (tok_bs[:], tok_b)):
                sp.dma_start(dst, src).then_inc(tokens_loaded, 16)
            for dst, src in ((ring[:, 0, 0:4, :], pq_w), (ring[:, 0, 4:8, :], pkeys)):
                sp.dma_start(dst.rearrange("p a b -> p (a b)"), src).then_inc(loaded, 16)
            sp.dma_start(ring[:, 1, 0, 0:HEADS], pq_b).then_inc(loaded, 16)
            for dst, src in ((wv_s[:], wv_t), (wth_s[:], wth_t)):
                sp.dma_start(dst, src).then_inc(loaded, 16)
            pack(0, REST)
            sp.wait_ge(setup_cb, 2)
            sp.dma_start(cb3[1:2, :], cbp[:, 0, :]).then_inc(split_moved, 16)
            sp.dma_start(cb3[2:3, :], cbp[:, 1, :]).then_inc(split_moved, 16)
            for dst, src in ((aq_s[:], aq), (ak_s[:], ak), (av_s[:], av), (ao_s[:].rearrange("p a b -> p (a b)"), ao),
                             (abo_s[:], abo), (pool_ws[:], pool_w), (pool_bs[:], pool_b), (gate_ws[:], gate_w),
                             (gate_bs[:], gate_b), (w1_s[:].rearrange("p e h -> p (e h)"), w1),
                             (w2_s[:].rearrange("p e m d -> p (e m d)"), w2),
                             (b1_s[:].rearrange("p e m -> p (e m)"), b1), (b2_s[:], b2)):
                sp.dma_start(dst, src).then_inc(late_loaded, 16)

            def step(s, nxt, cur, att, moe):
                if nxt:
                    sp.wait_ge(a_tok, s + 1)
                    sp.sem_inc(carried)
                    load_x(s + 1, nxt)
                if att:
                    unpack(s - 1, 1, att)
                if nxt:
                    pack(s + 1, nxt)
                if moe:
                    store(s - 2, moe)
                if cur == NB:
                    sp.wait_ge(l_h3, s)
                    sp.sem_inc(carried)
                    unpack(s, 0, cur)

            run_steps(sp, step)
            sp.wait_ge(stored, (GROUPS + 1) * 16)

        @block.gpsimd
        def _(pool):
            pool.memset(ident[:], 0.0).then_inc(pool_order, 1)
            pool.memset(ones[:], 1.0).then_inc(consts, 1)
            pool.memset(mean_col[:], 1.0 / N).then_inc(consts, 1)
            pool.memset(causal[:], 1.0).then_inc(pool_order, 1)
            pool.memset(own_batch[:], 1.0).then_inc(pool_order, 1)
            pool.memset(ones3[:], 0.0).then_inc(pool_order, 1)
            pool.wait_ge(pool_order, 4)
            pool.affine_select(out=ident[:], in_=ident[:], compare_op=ALU.not_equal, fill=1.0, base=0,
                               pattern=[[-1, 128]], channel_multiplier=1).then_inc(consts, 1)
            pool.affine_select(out=causal[:], in_=causal[:], compare_op=ALU.is_ge, fill=0.0, base=0,
                               pattern=[[1, N]], channel_multiplier=-1).then_inc(consts, 1)
            pool.affine_select(out=own_batch[:], in_=own_batch[:], compare_op=ALU.is_equal, fill=0.0, base=0,
                               pattern=[[1, NB], [0, E]], channel_multiplier=-1).then_inc(consts, 1)
            pool.affine_select(out=ones3[:], in_=ones3[:], compare_op=ALU.is_ge, fill=1.0, base=-3,
                               pattern=[[0, 128]], channel_multiplier=1).then_inc(consts, 1)
            pool.iota(iota8[:], pattern=[[1, 8]], base=0, channel_multiplier=0,
                      allow_small_or_imprecise_dtypes=True).then_inc(consts, 1)
            pool.memset(vx[:, :, :, LD:LD + 1], 1.0).then_inc(consts, 1)
            pool.memset(h1p[:], 0.0).then_inc(consts, 1)
            pool.memset(halves[:], 0.0).then_inc(pool_order, 1)
            pool.wait_ge(pool_order, 5)
            pool.memset(halves[0:LD, 0:1], 1.0).then_inc(consts, 1)
            pool.memset(halves[LD:D, 1:2], 1.0).then_inc(consts, 1)

            def gather(t, j, rows, first):
                pool.wait_ge(t_idx, t + 1)
                for u in range(UNITS):
                    if not first:
                        pool.wait_ge(u_sum, (t - 1) * UNITS + (u + 1))
                    pool.sem_inc(carried)
                    for k in range(UR):
                        c = u * UR + k
                        pool.indirect_dma_start(
                            ring[0:rows, u, k, :], None, table,
                            bass.IndirectOffsetOnAxis(ap=idx[0:rows, j, c:c + 1], axis=0)).then_inc(gathered[u], 16)

            gather(0, 1, N, True)
            with pool.Fori(1, GROUPS + 1) as g:
                gather(g * 2 - 1, 0, 128, False)
                gather(g * 2, 1, 128, False)

        @block.tensor
        def _(pe):
            mm = pe.matmul

            def a_tokens(g, nb):
                pe.wait_ge(x_in, g * 16 + 16)
                if not first(g):
                    pe.wait_ge(t_sc, g * 8 - 4)
                for b in range(nb):
                    o = S[0][0:N, b * D:b * D + D]
                    mm(o, x_s[:, 0, b * N:b * N + N], tok_ws[:, 0, :], start=True, stop=False)
                    mm(o, x_s[:, 1, b * N:b * N + N], tok_ws[:, 1, :], start=False, stop=False)
                    ins = mm(o, ones[0:1, 0:N], tok_bs[:], start=False, stop=True)
                ins.then_inc(a_tok, 1)

            def a_gram_of(g, nb):
                pe.wait_ge(a_z0, g + 1)
                for b in range(nb):
                    mm(S[0][:, b * D:b * D + D], z0[:, b, :], z0[:, b, :], start=True, stop=True)
                for b in range(nb):
                    mm(S[1][:, NB * N + b:NB * N + b + 1], z0[:, b, :], mean_col[:], start=True, stop=True)
                for b in range(nb):
                    ins = pe.transpose(S[1][:, b * N:b * N + N], z0[:, b, :], ident[0:N, 0:N])
                ins.then_inc(a_gram_ps, 1)

            def a_values(g, nb):
                pe.wait_ge(a_gram, g + 1)
                for b in range(nb):
                    mm(S[0][:, b * D:b * D + D], gram[:, b, :], wv_s[:], start=True, stop=True)
                for b in range(nb):
                    ins = mm(S[1][0:1, b * D:b * D + D], zmean[:, b:b + 1], wv_s[:], start=True, stop=True)
                ins.then_inc(a_gv_ps, 1)

            def a_kv_of(g, nb):
                pe.wait_ge(a_gv, g + 1)
                mm(S[0][:, 0:nb * D], wth_s[:], gv[:, 0:nb, :].rearrange("p b d -> p (b d)"), start=True, stop=True).then_inc(a_kv_ps, 1)

            def a_out(g, nb):
                pe.wait_ge(a_kv, g + 1)
                for b in range(nb):
                    o = S[1][0:N, b * D:b * D + D]
                    mm(o, z0t[:, b, :], kv[:, b, :], start=True, stop=False)
                    ins = mm(o, ones[0:1, 0:N], rmean[:, b, :], start=False, stop=True)
                ins.then_inc(a_out_ps, 1)

            def t_turn(t, rows):
                pe.wait_ge(t_q, t + 1)
                pe.transpose(qtp[:, 0:rows], q_s[0:rows, :], ident[0:rows, 0:rows]).then_inc(t_qt_ps, 1)

            def t_scores(t, rows):
                pe.wait_ge(t_qt, t + 1)
                for c in range(4):
                    if c >= 2:
                        pe.wait_ge(t_sc, t * 4 + (c - 1))
                    cols = slice(c * 512, c * 512 + 512)
                    mm(S[c % 2][0:rows, :], qt_s[:, 0:rows], ck[:, cols], start=True, stop=False)
                    mm(S[c % 2][0:rows, :], ones3[:, 0:rows], cb3[:, cols], start=False, stop=True).then_inc(t_sc_ps, 1)

            def unit_sum(t, u, rows):
                pe.wait_ge(u_up, t * UNITS + (u + 1))
                if u == 0 and not first(t):
                    pe.wait_ge(t_red, t)
                for c in range(UR // 4):
                    ins = mm(U[0:rows, :], ident[0:rows, 0:rows], ring[0:rows, u, 4 * c:4 * c + 4, D:ROW],
                             start=(u == 0 and c == 0), stop=(u == UNITS - 1 and c == UR // 4 - 1))
                ins.then_inc(u_sum, 1)

            def l_turn(g, nb):
                pe.wait_ge(l_z2, g + 1)
                if not first(g):
                    pe.wait_ge(r_gb, g)
                for b in range(nb):
                    ins = pe.transpose(G[0][:, b * N:b * N + N], z2[:, b, :], ident[0:N, 0:N])
                ins.then_inc(l_z2t_ps, 1)

            def l_queries(g, nb, bs):
                for b in bs:
                    if b == 0:
                        pe.wait_ge(l_z2t, g + 1)
                    if b == 2:
                        pe.wait_ge(l_qs, batches(g) + 1)
                    if b < nb:
                        mm(G[(b + 1) % 2][0:N, :], z2t[:, b * N:b * N + N], aq_s[:], start=True, stop=True).then_inc(l_q_ps, 1)

            def l_keys(g, nb, half):
                n = nb * N
                if nb == NB or half == 1:
                    pe.wait_ge(l_qs, batches(g) + (2 + half if nb == NB else 1))
                for m in range(2):
                    w = ak_s[:, (2 * half + m) * D:(2 * half + m + 1) * D]
                    ins = mm(G[half][:, m * n:m * n + n], w, z2t[:, 0:n], start=True, stop=True)
                ins.then_inc(l_k_ps, 1)

            def l_values(g, nb):
                for b in range(nb):
                    if b < 2:
                        pe.wait_ge(l_k, g * 2 + (b + 1))
                    else:
                        pe.wait_ge(l_v, batches(g) + 1)
                    mm(G[b % 2][0:N, :], z2t[:, b * N:b * N + N], av_s[:], start=True, stop=True).then_inc(l_v_ps, 1)

            def l_queries_turn(g, nb):
                for b in range(nb):
                    if b == 0:
                        pe.wait_ge(l_v, batches(g) + 2) if nb == NB else pe.wait_ge(l_k, g * 2 + 2)
                    elif b == 1:
                        pe.wait_ge(l_v, batches(g) + 3)
                    else:
                        pe.wait_ge(l_qt, batches(g) + 1)
                    pe.wait_ge(l_qe, batches(g) + (b + 1))
                    for m in range(HB):
                        ins = pe.transpose(G[(b + 1) % 2][:, m * N:m * N + N],
                                           qe[:, b, 2 * m:2 * m + 2, :].rearrange("p a d -> p (a d)"), ident[0:N, 0:N])
                    ins.then_inc(l_qt_ps, 1)

            def l_scores(g, nb, b):
                for odd in range(2):
                    if b:
                        pe.wait_ge(l_a, 2 * batches(g) + (2 * b - 1 + odd))
                    elif nb == NB:
                        pe.wait_ge(l_qt, batches(g) + (2 + odd))
                    else:
                        pe.wait_ge(l_v, batches(g) + 1)
                        pe.wait_ge(l_qt, batches(g) + 1)
                    if b:
                        pe.wait_ge(l_qt, batches(g) + (b + 1))
                    elif not odd:
                        pe.wait_ge(l_qt, batches(g) + nb)
                        for bb in range(nb):
                            for m in range(HB):
                                mm(G[0][0:N, QSUM + bb * LH + 2 * m:QSUM + bb * LH + 2 * m + 2], qt[:, bb, m, :], halves[:],
                                   start=True, stop=True)
                    r = slice(odd * LD, odd * LD + LD)
                    for m in range(HB):
                        ins = mm(G[odd][0:N, m * N:m * N + N], kt[r, m, b * N:b * N + N], qt[r, b, m, :],
                                 start=True, stop=True)
                    ins.then_inc(l_s_ps, 1)

            def l_weighted(g, b):
                for odd in range(2):
                    pe.wait_ge(l_s, 2 * batches(g) + (2 * b + 1 + odd))
                    for m in range(HB):
                        ins = mm(G[odd][0:N, m * (LD + 1):(m + 1) * (LD + 1)], sm[:, odd, m, :], vx[:, b, 2 * m + odd, :],
                                 start=True, stop=True)
                    ins.then_inc(l_a_ps, 1)

            def l_out(g, nb):
                for b in range(nb):
                    if b < 2:
                        pe.wait_ge(l_a, 2 * batches(g) + (2 * nb - 1 + (b if nb == NB else 1)))
                    else:
                        pe.wait_ge(l_at, batches(g) + 1)
                    for m in range(HB):
                        ins = pe.transpose(G[b % 2][:, m * N:m * N + N],
                                           at_s[:, b, 2 * m:2 * m + 2, :].rearrange("p a d -> p (a d)"), ident[0:N, 0:N])
                    ins.then_inc(l_at_ps, 1)
                for b in range(nb):
                    pe.wait_ge(l_at, batches(g) + (max(b, 1) + 1 if nb == NB else 1))
                    o = G[1][0:N, b * D:b * D + D]
                    for m in range(HB):
                        mm(o, att[:, b, m, :], ao_s[:, m, :], start=(m == 0), stop=False)
                    ins = mm(o, ones[0:1, 0:N], abo_s[:], start=False, stop=True)
                ins.then_inc(l_o_ps, 1)

            def l_turn_out(g, nb):
                pe.wait_ge(l_z3, g + 1)
                for b in range(nb):
                    pe.transpose(G[0][:, b * N:b * N + N], z3[:, b, :], ident[0:N, 0:N])
                for b in range(nb):
                    ins = pe.transpose(G[1][:, b * N:b * N + N], h3[:, b, :], ident[0:N, 0:N])
                ins.then_inc(l_z3t_ps, 1)

            def route(g, nb):
                n = nb * N
                pe.wait_ge(l_z3t, g + 1)
                mm(G[0][0:1, 0:n], pool_ws[:], z3t[:, 0:nb, :].rearrange("p b n -> p (b n)"), start=True, stop=True).then_inc(r_sc_ps, 1)
                pe.wait_ge(l_h3t, g + 1)
                pe.wait_ge(r_aw, g + 1)
                mm(G[1][:, 0:n], ones[0:1, :], pw[:, 0:nb, :].rearrange("p b n -> p (b n)"), start=True, stop=True).then_inc(r_aw_ps, 1)
                pe.wait_ge(r_pool, g + 1)
                mm(G[0][0:nb, 256:256 + E], pooled[:, 0:nb], gate_ws[:], start=True, stop=False)
                mm(G[0][0:nb, 256:256 + E], ones[0:1, 0:nb], gate_bs[:], start=False, stop=True).then_inc(r_gate_ps, 1)

            def spread_gates(g, nb):
                pe.wait_ge(r_gd, g + 1)
                mm(G[0][:, 320:320 + nb * E], ones[0:nb, :], gd[0:nb, 0:nb, :].rearrange("p b e -> p (b e)"), start=True, stop=True).then_inc(r_gb_ps, 1)

            def experts(g, nb, lo, hi):
                n = nb * N
                x = z3t[:, 0:nb, :].rearrange("p b n -> p (b n)")
                for i, (what, e, half) in uses_between(lo, hi):
                    if not (first(g) and i < 2):
                        pe.wait_ge(x_out, g * USES + (i - 1))
                    if what == "hidden":
                        if i == 0:
                            pe.wait_ge(l_z3t, g + 1)
                        for m in range(2):
                            k = 2 * half + m
                            ins = mm(X[i % 2][:, m * n:m * n + n], w1_s[:, e, k * D:(k + 1) * D], x, start=True, stop=True)
                    else:
                        pe.wait_ge(x_out, g * USES + (place["hidden", e, 1] + 1))
                        for m in range(HB):
                            ins = mm(X[i % 2][:, 0:n], w2_s[:, e, m, :], ht[:, e % 2, m, 0:n], start=(m == 0), stop=(m == HB - 1))
                    ins.then_inc(x_ps, 1)

            pe.wait_ge(consts, NCONST)
            pe.wait_ge(tokens_loaded, 32)
            a_tokens(0, REST)
            pe.wait_ge(loaded, EARLY)
            wq_r = ring[:, 0, 0:4, :].rearrange("p a b -> p (a b)").rearrange("p (h d) -> p h d", h=HEADS)
            ky_r = ring[:, 0, 4:8, :].rearrange("p a b -> p (a b)").rearrange("p (h d) -> p h d", h=HEADS)
            bq_r = ring[:, 1, 0, 0:HEADS]
            for c in range(4):
                for i in range(4):
                    half, h = c // 2, (c % 2) * 4 + i
                    r = slice(half * 64, half * 64 + 64)
                    ins = mm((G + X)[c][:, i * EXP:i * EXP + EXP], wq_r[r, h, :], ky_r[r, h, :], start=True, stop=True)
                ins.then_inc(setup_ps, 1)
            a_gram_of(0, REST)
            for c in range(4):
                pe.wait_ge(setup_ck, c + 1)
                for i in range(4):
                    half, h = c // 2, (c % 2) * 4 + i
                    r = slice(half * 64, half * 64 + 64)
                    ins = mm((G + X)[c][0:1, i * EXP:i * EXP + EXP], bq_r[r, h:h + 1], ky_r[r, h, :], start=True, stop=True)
                ins.then_inc(setup_ps, 1)
                if c == 1:
                    a_values(0, REST)
            a_kv_of(0, REST)
            a_out(0, REST)
            t_turn(0, N)
            pe.wait_ge(split_moved, 32)
            pe.wait_ge(setup_cb, 2)
            t_scores(0, N)
            pe.wait_ge(setup_dve, 4)

            def step(s, nxt, cur, att, moe):
                t0 = s * 2 - 1
                rows = 128 if cur == NB else N
                if moe:
                    spread_gates(s - 2, moe)
                if cur == NB:
                    t_turn(t0 + 1, 128)
                    t_scores(t0 + 1, 128)
                if moe:
                    experts(s - 2, moe, 1, 2)
                if cur == NB:
                    unit_sum(t0, 0, 128)
                if moe:
                    experts(s - 2, moe, 2, 3)
                if nxt:
                    a_tokens(s + 1, nxt)
                if moe:
                    experts(s - 2, moe, 3, 4)
                if cur == NB:
                    unit_sum(t0, 1, 128)
                if att:
                    if isinstance(s, int) and s == 1:
                        pe.wait_ge(late_loaded, LATE)
                    l_turn(s - 1, att)
                    l_queries(s - 1, att, (0, 1))
                if moe:
                    experts(s - 2, moe, 4, 5)
                if att:
                    l_queries(s - 1, att, (2,))
                    l_keys(s - 1, att, 0)
                if nxt:
                    a_gram_of(s + 1, nxt)
                if cur == NB:
                    unit_sum(t0, 2, 128)
                if nxt:
                    a_values(s + 1, nxt)
                    a_kv_of(s + 1, nxt)
                    a_out(s + 1, nxt)
                if att:
                    l_keys(s - 1, att, 1)
                    l_values(s - 1, att)
                    l_queries_turn(s - 1, att)
                if att:
                    l_scores(s - 1, att, 0)
                if nxt:
                    t_turn(t0 + 2, 128)
                if att:
                    l_weighted(s - 1, 0)
                if nxt:
                    t_scores(t0 + 2, 128)
                if att == NB:
                    l_scores(s - 1, att, 1)
                if cur == NB:
                    unit_sum(t0, 3, 128)
                if att == NB:
                    l_weighted(s - 1, 1)
                    l_scores(s - 1, att, 2)
                if moe:
                    experts(s - 2, moe, 5, 6)
                if att == NB:
                    l_weighted(s - 1, 2)
                if cur:
                    unit_sum(t0 + 1, 0, rows)
                if moe:
                    experts(s - 2, moe, 6, 7)
                if att:
                    l_out(s - 1, att)
                if moe:
                    experts(s - 2, moe, 7, E)
                if cur:
                    unit_sum(t0 + 1, 1, rows)
                if att:
                    l_turn_out(s - 1, att)
                if cur:
                    unit_sum(t0 + 1, 2, rows)
                if att:
                    route(s - 1, att)
                    experts(s - 1, att, 0, 1)
                if cur:
                    unit_sum(t0 + 1, 3, rows)

            run_steps(pe, step)

        @block.scalar
        def _(act):
            def copy(o, i, scale=1.0):
                return act.activation(o, i, ACT.Copy, scale=scale)

            def a_rows(g, nb):
                act.wait_ge(a_tok, g + 1)
                copy(h0[:, 0:nb, :].rearrange("p b d -> p (b d)"), S[0][0:N, 0:nb * D]).then_inc(a_h0, 1)

            def a_gram_of(g, nb):
                act.wait_ge(a_gram_ps, g + 1)
                copy(gram[:, 0:nb, :].rearrange("p b d -> p (b d)"), S[0][:, 0:nb * D])
                copy(zmean[:, 0:nb], S[1][:, NB * N:NB * N + nb])
                copy(z0t[:, 0:nb, :].rearrange("p b n -> p (b n)"), S[1][:, 0:nb * N]).then_inc(a_gram, 1)

            def a_kv_of(g, nb):
                act.wait_ge(a_gv_ps, g + 1)
                copy(rmean[:, 0:nb, :].rearrange("p b d -> p (b d)"), S[1][0:1, 0:nb * D])
                copy(gv[:, 0:nb, :].rearrange("p b d -> p (b d)"), S[0][:, 0:nb * D]).then_inc(a_gv, 1)
                act.wait_ge(a_kv_ps, g + 1)
                copy(kv[:, 0:nb, :].rearrange("p b d -> p (b d)"), S[0][:, 0:nb * D],
                     scale=1.0 / (N * float(D) ** 0.5)).then_inc(a_kv, 1)

            def t_turn(t, j, rows):
                act.wait_ge(t_q, t + 1)
                act.wait_ge(t_qt_ps, t + 1)
                copy(qt_s[:, 0:rows], qtp[:, 0:rows]).then_inc(t_qt, 1)
                copy(qrep[0:rows, j, :], q_s[0:rows, :]).then_inc(t_qrep, 1)

            def t_keep(t, j, rows):
                if not isinstance(t, int) or t >= 2:
                    act.wait_ge(t_h2, t - 1)
                copy(hres[0:rows, j, :], h1p[0:rows, j, :]).then_inc(t_kept, 1)

            def t_scores(t, rows):
                if not first(t):
                    act.wait_ge(t_idx, t)
                for c in range(4):
                    act.wait_ge(t_sc_ps, t * 4 + (c + 1))
                    copy(sc[0:rows, 4 * c:4 * c + 4, :].rearrange("p a b -> p (a b)"), S[c % 2][0:rows, :]).then_inc(t_sc, 1)

            def t_soft(t, rows):
                act.wait_ge(t_es, t + 1)
                act.activation(es[0:rows, :, :], es[0:rows, :, :], ACT.Exp).then_inc(t_ee, 1)

            def unit_tanh(t, u, rows):
                act.wait_ge(u_arg, t * UNITS + (u + 1))
                act.activation(th[0:rows, :], xu[0:rows, 2, :], ACT.Tanh, scale=0.7978845608028654).then_inc(u_th, 1)

            def unit_scale(t, u, rows):
                act.wait_ge(u_v, t * UNITS + (u + 1))
                for k in range(UR):
                    up = ring[0:rows, u, k, D:ROW]
                    ins = act.activation(up, up, ACT.Copy, scale=vu[0:rows, u, k:k + 1])
                ins.then_inc(u_up, 1)

            def l_turn(g, nb):
                n = nb * N
                act.wait_ge(l_z2t_ps, g + 1)
                copy(z2t[:, 0:n], G[0][:, 0:n]).then_inc(l_z2t, 1)

            def l_keys(g, nb, half):
                n = nb * N
                act.wait_ge(l_k_ps, g * 2 + (half + 1))
                act.activation(kt[:, 2 * half:2 * half + 2, 0:n],
                               G[half][:, 0:2 * n].rearrange("p (m n) -> p m n", m=2), ACT.Exp).then_inc(l_k, 1)

            def l_queries(g, nb):
                for b in range(nb):
                    act.wait_ge(l_qs, batches(g) + (b + 1))
                    act.activation(qe[:, b, :, :], qe[:, b, :, :], ACT.Exp).then_inc(l_qe, 1)

            def l_values(g, nb):
                for b in range(nb):
                    act.wait_ge(l_v_ps, batches(g) + (b + 1))
                    copy(vx[:, b, :, 0:LD], G[b % 2][0:N, :].rearrange("p (h d) -> p h d", h=LH)).then_inc(l_v, 1)
                for b in range(nb):
                    act.wait_ge(l_qt_ps, batches(g) + (b + 1))
                    copy(qt[:, b, :, :].rearrange("p m n -> p (m n)"), G[(b + 1) % 2][:, 0:HB * N]).then_inc(l_qt, 1)

            def l_out(g, nb):
                for b in range(nb):
                    act.wait_ge(l_at_ps, batches(g) + (b + 1))
                    copy(att[:, b, :, :].rearrange("p m n -> p (m n)"), G[b % 2][:, 0:HB * N]).then_inc(l_at, 1)

            def l_turn_out(g, nb):
                act.wait_ge(l_z3t_ps, g + 1)
                copy(z3t[:, 0:nb, :].rearrange("p b n -> p (b n)"), G[0][:, 0:nb * N]).then_inc(l_z3t, 1)

            def l_residual(g, nb):
                if not first(g):
                    act.wait_ge(m_acc, g * E - (E - 1))
                copy(h3t[:, 0:nb, :].rearrange("p b n -> p (b n)"), G[1][:, 0:nb * N]).then_inc(l_h3t, 1)

            def pool_soft(g, nb):
                act.wait_ge(r_sub, g + 1)
                act.activation(pw[:, 0:nb, :], pw[:, 0:nb, :], ACT.Exp).then_inc(r_exp, 1)

            def gate_soft(g, nb):
                act.wait_ge(r_gsub, g + 1)
                act.activation(gl[0:nb, 1, :], gl[0:nb, 0, :], ACT.Exp).then_inc(r_gexp, 1)

            def spread_gates(g, nb):
                act.wait_ge(r_gb_ps, g + 1)
                copy(gb[:, 0:nb, :].rearrange("p b e -> p (b e)"), G[0][:, 320:320 + nb * E]).then_inc(r_gb, 1)

            def experts(g, nb, lo, hi):
                n = nb * N
                for i, (what, e, half) in uses_between(lo, hi):
                    act.wait_ge(x_ps, g * USES + (i + 1))
                    if what == "hidden":
                        for m in range(2):
                            k = 2 * half + m
                            ins = act.activation(ht[:, e % 2, k, 0:n], X[i % 2][:, m * n:m * n + n], ACT.Gelu,
                                                 bias=b1_s[:, e, k:k + 1])
                    else:
                        if not (first(g) and e < EO):
                            act.wait_ge(m_acc, g * E + (e - EO + 1))
                        ins = act.activation(eo[:, e % EO, 0:nb, :].rearrange("p b n -> p (b n)"), X[i % 2][:, 0:n],
                                             ACT.Gelu, bias=b2_s[:, e:e + 1])
                    ins.then_inc(x_out, 1)

            act.wait_ge(consts, NCONST)
            a_rows(0, REST)
            for c in range(4):
                act.wait_ge(setup_ps, c + 1)
                copy(ck[:, c * 512:c * 512 + 512], (G + X)[c][:, :]).then_inc(setup_ck, 1)
            a_gram_of(0, REST)
            a_kv_of(0, REST)
            act.wait_ge(packed, 16)
            t_turn(0, 1, N)
            t_scores(0, N)
            t_keep(0, 1, N)
            t_soft(0, N)

            def step(s, nxt, cur, att, moe):
                t0 = s * 2 - 1
                rows = 128 if cur == NB else N
                if cur == NB:
                    unit_tanh(t0, 0, 128)
                    unit_scale(t0, 0, 128)
                if moe:
                    spread_gates(s - 2, moe)
                if cur == NB:
                    t_turn(t0 + 1, 1, 128)
                    t_scores(t0 + 1, 128)
                    t_keep(t0 + 1, 1, 128)
                if cur == NB:
                    unit_tanh(t0, 1, 128)
                if moe:
                    experts(s - 2, moe, 1, 3)
                if cur == NB:
                    unit_scale(t0, 1, 128)
                    t_soft(t0 + 1, 128)
                if nxt:
                    a_rows(s + 1, nxt)
                if cur == NB:
                    unit_tanh(t0, 2, 128)
                if moe:
                    experts(s - 2, moe, 3, 4)
                if cur == NB:
                    unit_scale(t0, 2, 128)
                if att:
                    l_turn(s - 1, att)
                if moe:
                    experts(s - 2, moe, 4, 5)
                if nxt:
                    a_gram_of(s + 1, nxt)
                if cur == NB:
                    unit_tanh(t0, 3, 128)
                if att:
                    l_keys(s - 1, att, 0)
                if nxt:
                    a_kv_of(s + 1, nxt)
                if att:
                    l_queries(s - 1, att)
                    l_keys(s - 1, att, 1)
                if cur:
                    unit_tanh(t0 + 1, 0, rows)
                if att:
                    l_values(s - 1, att)
                if cur == NB:
                    unit_scale(t0, 3, 128)
                if nxt:
                    t_turn(t0 + 2, 0, 128)
                    t_scores(t0 + 2, 128)
                if cur:
                    unit_tanh(t0 + 1, 1, rows)
                    unit_scale(t0 + 1, 0, rows)
                if moe:
                    experts(s - 2, moe, 5, 6)
                    experts(s - 2, moe, 6, 7)
                if att:
                    l_out(s - 1, att)
                if nxt:
                    t_keep(t0 + 2, 0, 128)
                if cur:
                    unit_scale(t0 + 1, 1, rows)
                if cur:
                    unit_tanh(t0 + 1, 2, rows)
                if moe:
                    experts(s - 2, moe, 7, E)
                if nxt:
                    t_soft(t0 + 2, 128)
                if cur:
                    unit_scale(t0 + 1, 2, rows)
                if att:
                    l_turn_out(s - 1, att)
                    l_residual(s - 1, att)
                if cur:
                    unit_tanh(t0 + 1, 3, rows)
                if att:
                    pool_soft(s - 1, att)
                if cur:
                    unit_scale(t0 + 1, 3, rows)
                if att:
                    gate_soft(s - 1, att)
                    experts(s - 1, att, 0, 1)

            run_steps(act, step)

        A_SHORT, L_SHORT = 14, 39
        A_STEPS, T_STEPS, U_STEPS, L_STEPS, R_STEPS = 18, 76, 7, 55, 13

        @block.vector
        def _(dve):
            tt, ts, stt = dve.tensor_tensor, dve.tensor_scalar, dve.scalar_tensor_tensor

            def rsqrt(sets):
                sets = [(ch, mv, w[:, 0, 0:nb], w[:, 1, 0:nb], w[:, 2, 0:nb], w[:, 3, 0:nb].bitcast(U32))
                        for ch, mv, w, nb in sets]
                for ch, mv, v, y, a, bits in sets:
                    ch.wait()
                    ch.did(ts(v, mv, LN_EPS, None, ALU.add))
                for ch, mv, v, y, a, bits in sets:
                    ch.wait()
                    ch.did(ts(bits, v.bitcast(U32), 1, None, ALU.logical_shift_right))
                for ch, mv, v, y, a, bits in sets:
                    ch.wait()
                    ch.did(ts(y.bitcast(I32), bits.bitcast(I32), -1.0, float(MAGIC), ALU.mult, ALU.add))
                for _ in range(NEWTON):
                    for ch, mv, v, y, a, bits in sets:
                        ch.wait()
                        ch.did(tt(a, y, y, ALU.mult))
                    for ch, mv, v, y, a, bits in sets:
                        ch.wait()
                        ch.did(stt(a, a, -0.5, v, ALU.mult, ALU.mult))
                    for ch, mv, v, y, a, bits in sets:
                        ch.wait()
                        ch.did(stt(y, a, 1.5, y, ALU.add, ALU.mult))

            def normalise(sets):
                for ch, src, dst, st, mv, w, nb, done in sets:
                    for b in range(nb):
                        ch.did(dve.bn_stats(st[:, b, :], src[:, b, :]))
                for ch, src, dst, st, mv, w, nb, done in sets:
                    ch.wait()
                dve.sem_inc(carried)
                for ch, src, dst, st, mv, w, nb, done in sets:
                    for b in range(nb):
                        ch.did(dve.bn_aggr(mv[:, b, :], st[:, b, :]))
                rsqrt([(ch, mv[:, 0:nb, 1], w, nb) for ch, src, dst, st, mv, w, nb, done in sets])
                for ch, src, dst, st, mv, w, nb, done in sets:
                    ch.wait()
                    for b in range(nb):
                        ins = ts(dst[:, b, :], src[:, b, :], mv[:, b, 0:1], w[:, 1, b:b + 1], ALU.subtract, ALU.mult)
                    ins.then_inc(done, 1)

            def rsqrt_rows(ch, mv, w):
                v, y, a, h = w[:, 0, :], w[:, 1, :], w[:, 2, :], w[:, 4, :]
                bits = w[:, 3, :].bitcast(U32)
                ch.did(ts(v, mv, LN_EPS, None, ALU.add))
                ch.did(ts(h, mv, LN_EPS, -0.5, ALU.add, ALU.mult))
                ch.wait(1)
                ch.did(ts(bits, v.bitcast(U32), 1, None, ALU.logical_shift_right))
                ch.wait()
                ch.did(ts(y.bitcast(I32), bits.bitcast(I32), -1.0, float(MAGIC), ALU.mult, ALU.add))
                for _ in range(NEWTON):
                    ch.wait()
                    ch.did(stt(a, y, h, y, ALU.mult, ALU.mult))
                    ch.wait()
                    ch.did(stt(y, a, 1.5, y, ALU.add, ALU.mult))
                ch.wait()

            def a_rows(g, nb):
                dve.wait_ge(a_h0, g + 1)
                return Chain(dve, a_dve, g, A_STEPS, A_SHORT), h0, z0, st0, mv0, nw0, nb, a_z0

            def l_rows(g, nb):
                dve.wait_ge(unpacked, moves(g) + (64 if nb == NB else 16))
                return Chain(dve, l_dve, g, L_STEPS, L_SHORT), h2, z2, st2, mv2, nw2, nb, l_z2

            def a_add(g, nb):
                dve.wait_ge(a_out_ps, g + 1)
                if not first(g):
                    dve.wait_ge(packed, moves(g))
                tt(h1[:, 0:nb, :].rearrange("p b d -> p (b d)"), S[1][0:N, 0:nb * D],
                   h0[:, 0:nb, :].rearrange("p b d -> p (b d)"), ALU.add).then_inc(a_h1, 1)

            def t_normalise(t, g, j, rows, nb=NB):
                r = slice(0, rows)
                ch = Chain(dve, t_dve, t, T_STEPS)
                dve.wait_ge(packed, moves(g) + (64 if nb == NB else 16))
                ch.did(dve.bn_stats(st1[r], h1p[r, j, :]))
                ch.wait()
                dve.sem_inc(carried)
                ch.did(dve.bn_aggr(mv1[r], st1[r]))
                ch.wait()
                rsqrt_rows(ch, mv1[r, 1:2], nw1[r])
                if not first(t):
                    dve.wait_ge(t_qt_ps, t)
                    dve.wait_ge(t_qrep, t)
                ts(q_s[r], h1p[r, j, :], mv1[r, 0:1], nw1[r, 1, 0:1], ALU.subtract, ALU.mult).then_inc(t_q, 1)
                return ch

            def t_best(t, rows, ch, lo, hi):
                r = slice(0, rows)
                for c in range(lo, hi):
                    dve.wait_ge(t_sc, t * 4 + (c + 1))
                    dve.sem_inc(carried)
                    for i in range(4 * c, 4 * c + 4):
                        ch.did(dve.max(s8[r, i, :], sc[r, i, :]))
                    if c > lo:
                        ch.wait(4)
                        dve.sem_inc(carried)
                        for i in range(4 * c - 4, 4 * c):
                            dve.max_index(i8[r, i, :], s8[r, i, :], sc[r, i, :]).then_inc(t_dve, 1)
                            ch.n += 1
                ch.wait()
                dve.sem_inc(carried)
                for i in range(4 * hi - 4, 4 * hi):
                    ch.did(dve.max_index(i8[r, i, :], s8[r, i, :], sc[r, i, :]))

            def t_pairs(t, rows, ch):
                r = slice(0, rows)
                ch.wait()
                shape = [rows, HEADS, TOPK, TOPK]
                ch.did(tt(pair[r], s8[r, 0:HEADS, :].unsqueeze(3).to_broadcast(shape),
                          s8[r, HEADS:2 * HEADS, :].unsqueeze(2).to_broadcast(shape), ALU.add))
                ch.wait(1)
                ch.did(dve.tensor_copy(i8f[r], i8[r]))
                ch.wait(1)
                dve.sem_inc(carried)
                for h in range(HEADS):
                    ch.did(dve.max(best[r, h, :], pair[r, h, :, :].rearrange("p a b -> p (a b)")))
                ch.wait()
                dve.sem_inc(carried)
                for h in range(HEADS):
                    ch.did(dve.max_index(pos[r, h, :], best[r, h, :], pair[r, h, :, :].rearrange("p a b -> p (a b)")))
                tt(es[r], best[r], best[r, :, 0:1].to_broadcast([rows, HEADS, TOPK]), ALU.subtract).then_inc(t_es, 1)
                return ch

            def t_decode(t, j, rows, ch):
                r = slice(0, rows)
                ch.wait()
                flat = pos[r].rearrange("p h k -> p (h k)")
                ch.did(ts(ab[r, 0, :], flat, 3, None, ALU.logical_shift_right))
                ch.did(ts(ab[r, 1, :], flat, 7, None, ALU.bitwise_and))
                ch.wait()
                hits = hit[r].rearrange("p i k a -> p (i k) a")
                for a in range(TOPK):
                    ch.did(stt(hit[r, :, :, a], ab[r].rearrange("p i (h k) -> p (i h) k", h=HEADS), float(a),
                               i8f[r, :, a].unsqueeze(2).to_broadcast([rows, 2 * HEADS, TOPK]), ALU.is_equal, ALU.mult))
                ch.wait()
                ch.did(dve.tensor_reduce(iab[r].rearrange("p i k -> p (i k)"), hits, AX.X, ALU.add))
                ch.wait()
                stt(idx[r, j, :], iab[r, 0, :], float(EXP), iab[r, 1, :], ALU.mult, ALU.add).then_inc(t_idx, 1)

            def t_share(t, j, rows, ch):
                r = slice(0, rows)
                dve.wait_ge(t_ee, t + 1)
                ch.did(dve.tensor_reduce(den[r, 0, :], es[r], AX.X, ALU.add))
                ch.wait()
                ch.did(dve.reciprocal(den[r, 1, :], den[r, 0, :]))
                ch.wait()
                ch.did(stt(smh[r, j, :].rearrange("p (h k) -> p h k", h=HEADS), es[r], 0.5,
                           den[r, 1, :].unsqueeze(2).to_broadcast([rows, HEADS, TOPK]), ALU.mult, ALU.mult))
                ch.wait()
                ch.end()

            def unit_dots(t, j, u, rows, latest=None):
                r = slice(0, rows)
                ch = Chain(dve, u_dve, t * UNITS + u, U_STEPS)
                dve.wait_ge(gathered[u], t * (UR * 16) + UR * 16)
                if latest is not None:
                    dve.wait_ge(t_qrep, latest + 1)
                half = UR // 2
                for i in range(2):
                    w = ring[r, u, i * half:i * half + half, 0:D]
                    ch.did(tt(w, w, qrep[r, j, :].unsqueeze(1).to_broadcast([rows, half, D]), ALU.mult))
                for i in range(2):
                    ch.wait(1)
                    ch.did(dve.tensor_reduce(xu[r, 0, i * half:i * half + half], ring[r, u, i * half:i * half + half, 0:D],
                                             AX.X, ALU.add))
                ch.wait()
                ch.did(tt(xu[r, 1, :], xu[r, 0, :], xu[r, 0, :], ALU.mult))
                ch.wait()
                ch.did(ts(xu[r, 1, :], xu[r, 1, :], 0.044715, 1.0, ALU.mult, ALU.add))
                ch.wait()
                tt(xu[r, 2, :], xu[r, 1, :], xu[r, 0, :], ALU.mult).then_inc(u_arg, 1)
                ch.did(tt(xu[r, 3, :], xu[r, 0, :], smh[r, j, u * UR:u * UR + UR], ALU.mult))
                return ch

            def unit_share(t, u, rows, ch):
                r = slice(0, rows)
                dve.wait_ge(u_th, t * UNITS + (u + 1))
                ch.wait()
                stt(vu[r, u, :], th[r], 1.0, xu[r, 3, :], ALU.add, ALU.mult).then_inc(u_v, 1)
                ch.end()

            def end_tile(t, g, j, rows):
                r = slice(0, rows)
                dve.wait_ge(u_sum, t * UNITS + UNITS)
                dve.tensor_reduce(usum[r], U[r].rearrange("p (k d) -> p d k", k=4), AX.X, ALU.add).then_inc(t_red, 1)
                if j == 1 and not first(g):
                    dve.wait_ge(unpacked, moves(g))
                if j == 0 and not first(g - 1):
                    dve.wait_ge(unpacked, moves(g - 1) + 32)
                dve.wait_ge(t_kept, t + 1)
                dve.wait_ge(t_red, t + 1)
                tt(h2p[r, j, :], usum[r], hres[r, j, :], ALU.add).then_inc(t_h2, 1)

            def l_queries(g, nb, ch, bs):
                for b in bs:
                    if b >= nb:
                        continue
                    dve.wait_ge(l_q_ps, batches(g) + (b + 1))
                    q = G[(b + 1) % 2][0:N, :].rearrange("p (h d) -> p h d", h=LH)
                    ch.did(dve.tensor_reduce(mx[:, b, :], q, AX.X, ALU.max))
                    ch.wait()
                    tt(qe[:, b, :, :], q, mx[:, b, :].unsqueeze(2).to_broadcast([N, LH, LD]), ALU.subtract).then_inc(l_qs, 1)

            def l_bounds(g, nb, ch):
                dve.wait_ge(l_s_ps, 2 * batches(g) + 1)
                ch.did(ts(dn[:, 0:nb, 0, :], G[0][0:N, QSUM:QSUM + nb * LH].rearrange("p (b h) -> p b h", b=nb),
                          CLIP * float(LD) ** 0.5, None, ALU.mult))

            def l_mask(g, b):
                for odd in range(2):
                    dve.wait_ge(l_s_ps, 2 * batches(g) + (2 * b + 1 + odd))
                    tt(sm[:, odd, :, :], G[odd][0:N, 0:HB * N].rearrange("p (m n) -> p m n", m=HB),
                       causal[:].unsqueeze(1).to_broadcast([N, HB, N]), ALU.mult).then_inc(l_s, 1)

            def l_divide(g, b, ch):
                a = [G[odd][0:N, 0:HB * (LD + 1)].rearrange("p (m d) -> p m d", m=HB) for odd in range(2)]

                def heads(x, odd):
                    return x.rearrange("p (m o) -> p o m", o=2)[:, odd, :]

                ch.wait()
                for odd in range(2):
                    dve.wait_ge(l_a_ps, 2 * batches(g) + (2 * b + 1 + odd))
                    ch.did(tt(heads(dn[:, b, 1, :], odd), a[odd][:, :, LD], heads(dn[:, b, 0, :], odd), ALU.max))
                ch.wait()
                ch.did(dve.reciprocal(dn[:, b, 2, :], dn[:, b, 1, :]))
                ch.wait()
                for odd in range(2):
                    tt(at_s[:, b, :, :].rearrange("p (m o) d -> p o m d", o=2)[:, odd, :, :], a[odd][:, :, 0:LD],
                       heads(dn[:, b, 2, :], odd).unsqueeze(2).to_broadcast([N, HB, LD]), ALU.mult).then_inc(l_a, 1)

            def l_add(g, nb, ch):
                dve.wait_ge(l_o_ps, g + 1)
                tt(h3[:, 0:nb, :].rearrange("p b d -> p (b d)"), G[1][0:N, 0:nb * D],
                   h2[:, 0:nb, :].rearrange("p b d -> p (b d)"), ALU.add).then_inc(l_h3, 1)
                dve.wait_ge(l_h3, g + 1)
                normalise([(ch, h3, z3, st2, mv2, nw2, nb, l_z3)])

            def pool_scores(g, nb, ch):
                dve.wait_ge(r_sc_ps, g + 1)
                s = pw[:, 0:nb, :]
                ch.did(ts(s, G[0][0:1, 0:nb * N].rearrange("p (b n) -> p b n", b=nb), pool_bs[:], None, ALU.add))
                ch.wait()
                ch.did(dve.tensor_reduce(pmx[:, 0, 0:nb], s, AX.X, ALU.max))
                ch.wait()
                tt(s, s, pmx[:, 0, 0:nb].unsqueeze(2).to_broadcast([1, nb, N]), ALU.subtract).then_inc(r_sub, 1)

            def pool_rows(g, nb, ch):
                s = pw[:, 0:nb, :]
                dve.wait_ge(r_exp, g + 1)
                ch.did(dve.tensor_reduce(pmx[:, 0, 0:nb], s, AX.X, ALU.add))
                ch.wait()
                ch.did(dve.reciprocal(pmx[:, 1, 0:nb], pmx[:, 0, 0:nb]))
                ch.wait()
                tt(s, s, pmx[:, 1, 0:nb].unsqueeze(2).to_broadcast([1, nb, N]), ALU.mult).then_inc(r_aw, 1)
                dve.wait_ge(r_aw_ps, g + 1)
                ch.did(tt(pz[:, 0:nb, :], z3t[:, 0:nb, :], G[1][:, 0:nb * N].rearrange("p (b n) -> p b n", b=nb), ALU.mult))
                ch.wait()
                dve.tensor_reduce(pooled[:, 0:nb], pz[:, 0:nb, :], AX.X, ALU.add).then_inc(r_pool, 1)
                p = slice(0, nb)
                dve.wait_ge(r_gate_ps, g + 1)
                lg = G[0][p, 256:256 + E]
                ch.did(dve.tensor_reduce(g1[p, 0:1], lg, AX.X, ALU.max))
                ch.wait()
                ts(gl[p, 0, :], lg, g1[p, 0:1], None, ALU.subtract).then_inc(r_gsub, 1)
                ch.end()

            def gates(g, nb):
                ch = Chain(dve, r_dve, g, R_STEPS)
                p = slice(0, nb)
                dve.wait_ge(r_gexp, g + 1)
                ch.did(dve.tensor_reduce(g1[p, 1:2], gl[p, 1, :], AX.X, ALU.add))
                ch.wait()
                ch.did(dve.reciprocal(g1[p, 2:3], g1[p, 1:2]))
                ch.wait()
                ch.did(ts(gl[p, 2, :], gl[p, 1, :], g1[p, 2:3], None, ALU.mult))
                ch.wait()
                dve.sem_inc(carried)
                ch.did(dve.max(gl[p, 3, :], gl[p, 2, :]))
                ch.wait()
                dve.sem_inc(carried)
                ch.did(dve.max_index(gi[p, :], gl[p, 3, :], gl[p, 2, :]))
                ch.wait()
                ch.did(dve.tensor_copy(gl[p, 3, :], gi[p, :]))
                ch.wait()
                ch.did(ts(gl[p, 4, :], iota8[p, :], gl[p, 3, 0:1], None, ALU.is_equal))
                ch.wait()
                ch.did(stt(gl[p, 5, :], iota8[p, :], gl[p, 3, 1:2], gl[p, 4, :], ALU.is_equal, ALU.add))
                ch.wait()
                ch.did(tt(gl[p, 4, :], gl[p, 5, :], gl[p, 2, :], ALU.mult))
                ch.wait()
                ch.did(dve.tensor_reduce(g1[p, 1:2], gl[p, 4, :], AX.X, ALU.add))
                ch.wait()
                ch.did(ts(g1[p, 3:4], g1[p, 1:2], DEN_EPS, None, ALU.add))
                ch.wait()
                ch.did(dve.reciprocal(g1[p, 2:3], g1[p, 3:4]))
                ch.wait()
                ch.did(ts(gl[p, 5, :], gl[p, 4, :], g1[p, 2:3], None, ALU.mult))
                ch.wait()
                tt(gd[p, 0:nb, :], own_batch[p, 0:nb, :], gl[p, 5, :].unsqueeze(1).to_broadcast([nb, nb, E]), ALU.mult)\
                    .then_inc(r_gd, 1)
                ch.end()

            def experts(g, nb, lo, hi):
                if lo == 0:
                    dve.wait_ge(r_gb, g + 1)
                    dve.wait_ge(l_h3t, g + 1)
                for i, (what, e, _) in uses_between(lo, hi):
                    if what == "hidden":
                        continue
                    dve.wait_ge(x_out, g * USES + (i + 1))
                    if e > 0:
                        dve.wait_ge(m_acc, g * E + e)
                    elif not first(g):
                        dve.wait_ge(stored, g * 16)
                    before = acc if e else h3t
                    for b in range(nb):
                        ins = stt(acc[:, b, :], eo[:, e % EO, b, :], gb[:, b, e:e + 1], before[:, b, :], ALU.mult, ALU.add)
                    ins.then_inc(m_acc, 1)

            dve.memset(cb3[:], 0.0).then_inc(setup_cb, 1)
            dve.wait_ge(consts, NCONST)
            normalise([a_rows(0, REST)])
            for c in range(4):
                dve.wait_ge(setup_ps, 5 + c)
                dve.tensor_copy(cb[:, c * 512:c * 512 + 512], (G + X)[c][0:1, :]).then_inc(setup_dve, 1)
            dve.wait_ge(setup_dve, 4)
            dve.wait_ge(setup_cb, 1)
            dve.tensor_copy(cb3[0:1, :], cb).then_inc(setup_dve, 1)
            dve.wait_ge(setup_dve, 5)
            tt(cbr, cb, cb3[0:1, :], ALU.subtract).then_inc(setup_dve, 1)
            a_add(0, REST)
            dve.wait_ge(setup_dve, 6)
            dve.tensor_copy(cbp[:, 0, :], cbr).then_inc(setup_dve, 1)
            dve.wait_ge(setup_dve, 7)
            tt(cb, cbr, cbp[:, 0, :], ALU.subtract).then_inc(setup_dve, 1)
            dve.wait_ge(setup_dve, 8)
            dve.tensor_copy(cbp[:, 1, :], cb).then_inc(setup_cb, 1)
            ch = t_normalise(0, 0, 1, N, REST)
            t_best(0, N, ch, 0, 4)
            t_pairs(0, N, ch)
            t_decode(0, 1, N, ch)
            t_share(0, 1, N, ch)

            def step(s, nxt, cur, att, moe):
                t0 = s * 2 - 1
                rows = 128 if cur == NB else N
                if cur == NB:
                    uc = unit_dots(t0, 0, 0, 128)
                if moe:
                    gates(s - 2, moe)
                if cur == NB:
                    unit_share(t0, 0, 128, uc)
                if att:
                    end_tile(t0 - 1, s - 1, 1, 128 if att == NB else N)
                if cur == NB:
                    tc = t_normalise(t0 + 1, s, 1, 128)
                if cur == NB:
                    uc = unit_dots(t0, 0, 1, 128, t0 + 1)
                    t_best(t0 + 1, 128, tc, 0, 2)
                    unit_share(t0, 1, 128, uc)
                if moe:
                    experts(s - 2, moe, 0, 2)
                if cur == NB:
                    t_best(t0 + 1, 128, tc, 2, 4)
                    t_pairs(t0 + 1, 128, tc)
                    t_decode(t0 + 1, 1, 128, tc)
                if cur == NB:
                    uc = unit_dots(t0, 0, 2, 128)
                    t_share(t0 + 1, 1, 128, tc)
                    unit_share(t0, 2, 128, uc)
                if att and isinstance(s, int) and s == 1:
                    dve.wait_ge(late_loaded, LATE)
                sets = ([l_rows(s - 1, att)] if att else []) + ([a_rows(s + 1, nxt)] if nxt else [])
                if sets:
                    normalise(sets)
                    lc = sets[0][0]
                if moe:
                    experts(s - 2, moe, 2, 4)
                if att:
                    l_queries(s - 1, att, lc, (0, 1))
                if cur == NB:
                    uc = unit_dots(t0, 0, 3, 128)
                if att:
                    l_queries(s - 1, att, lc, (2,))
                if cur == NB:
                    unit_share(t0, 3, 128, uc)
                if cur:
                    uc = unit_dots(t0 + 1, 1, 0, rows)
                if nxt:
                    a_add(s + 1, nxt)
                if moe:
                    experts(s - 2, moe, 4, 5)
                if cur:
                    unit_share(t0 + 1, 0, rows, uc)
                if nxt:
                    tc = t_normalise(t0 + 2, s + 1, 0, 128, nxt)
                if att:
                    l_bounds(s - 1, att, lc)
                    l_mask(s - 1, 0)
                    l_divide(s - 1, 0, lc)
                if cur:
                    uc = unit_dots(t0 + 1, 1, 1, rows, t0 + 2 if nxt else None)
                if att == NB:
                    l_mask(s - 1, 1)
                if nxt:
                    t_best(t0 + 2, 128, tc, 0, 2)
                if att == NB:
                    l_divide(s - 1, 1, lc)
                if cur:
                    unit_share(t0 + 1, 1, rows, uc)
                if cur == NB:
                    end_tile(t0, s, 0, 128)
                if att == NB:
                    l_mask(s - 1, 2)
                if nxt:
                    t_best(t0 + 2, 128, tc, 2, 4)
                if att == NB:
                    l_divide(s - 1, 2, lc)
                if nxt:
                    t_pairs(t0 + 2, 128, tc)
                    t_decode(t0 + 2, 0, 128, tc)
                if cur:
                    uc = unit_dots(t0 + 1, 1, 2, rows)
                if moe:
                    experts(s - 2, moe, 5, 7)
                if cur:
                    unit_share(t0 + 1, 2, rows, uc)
                if att:
                    l_add(s - 1, att, lc)
                if nxt:
                    t_share(t0 + 2, 0, 128, tc)
                if cur:
                    uc = unit_dots(t0 + 1, 1, 3, rows)
                if att:
                    pool_scores(s - 1, att, lc)
                if moe:
                    experts(s - 2, moe, 7, E)
                if cur:
                    unit_share(t0 + 1, 3, rows, uc)
                if att:
                    pool_rows(s - 1, att, lc)

            run_steps(dve, step)


def kernel(**inputs):
    import numpy as _np
    import concourse.bacc as _bacc
    from concourse import mybir as _mybir
    from concourse.bass_utils import run_bass_kernel_spmd as _run

    a = {k: _np.asarray(v) for k, v in inputs.items()}
    x = a["x"][:, :CTX * N, :].reshape(B, N, 2, KIN).transpose(0, 3, 2, 1)
    full = x[:GROUPS * NB].reshape(GROUPS, NB, KIN, 2, N).transpose(0, 2, 3, 1, 4)
    keys = a["L0_ffn_keys"].transpose(1, 3, 0, 2)
    data = {
        "xg": full.reshape(GROUPS * KIN, 2 * GT),
        "xl": x[GROUPS * NB:].transpose(1, 2, 0, 3).reshape(KIN, 2 * REST * N),
        "tok_w": a["L0_tok_weight"].T.reshape(2, KIN, D).transpose(1, 0, 2),
        "tok_b": a["L0_tok_bias"],
        "wv_t": a["L0_attn_W_v"].T,
        "wth_t": a["L0_attn_W_theta"].T,
        "pq_w": a["L0_ffn_Wq"].reshape(HEADS, 128, D).transpose(1, 0, 2).reshape(128, HEADS * D),
        "pq_b": a["L0_ffn_bq"].reshape(HEADS, 128).T,
        "pkeys": keys.reshape(128, HEADS * EXP),
        "table": _np.concatenate([a["L0_ffn_w_down_embed"], a["L0_ffn_w_up_embed"]], axis=1),
        "aq": a["L1_attn_Wq"],
        "ak": a["L1_attn_Wk"],
        "av": a["L1_attn_Wv"],
        "ao": a["L1_attn_Wo"].reshape(HB, D, D).transpose(1, 0, 2).reshape(D, HB * D),
        "abo": a["L1_attn_bo"].reshape(1, D),
        "pool_w": a["L1_ffn_attn_w"],
        "pool_b": a["L1_ffn_attn_b"].reshape(1, 1),
        "gate_w": a["L1_ffn_gate_w"],
        "gate_b": a["L1_ffn_gate_b"].reshape(1, E),
        "w1": a["L1_ffn_w1"].transpose(1, 0, 2).reshape(D, E * HID),
        "b1": a["L1_ffn_b1"].reshape(E, HB, D).transpose(2, 0, 1).reshape(D, E * HB),
        "w2": a["L1_ffn_w2"].reshape(E, HB, D, D).transpose(2, 0, 1, 3).reshape(D, E * HB * D),
        "b2": a["L1_ffn_b2"].T,
    }
    nc = _bacc.Bacc("TRN2", target_bir_lowering=False, num_devices=1)
    arrays, args = {}, []
    for name, v in data.items():
        v = _np.ascontiguousarray(v)
        arrays[f"in_{name}_dram"] = v
        args.append(nc.dram_tensor(f"in_{name}_dram", v.shape, _mybir.dt.from_np(v.dtype), kind="ExternalInput").ap())
    outs = []
    for i, shape in enumerate([(GROUPS * D, GT), (D, REST * N)]):
        outs.append(nc.dram_tensor(f"out_{i}_dram", shape, F32, kind="ExternalOutput").ap())
    tower(nc, *args, *outs)
    r = _run(nc, [arrays], core_ids=[0])
    main = _np.asarray(r.results[0]["out_0_dram"]).reshape(GROUPS, D, NB, N).transpose(0, 2, 3, 1).reshape(GROUPS * NB, N, D)
    last = _np.asarray(r.results[0]["out_1_dram"]).reshape(D, REST, N).transpose(1, 2, 0)
    return _np.ascontiguousarray(_np.concatenate([main, last], axis=0))
```
